# Optimizing a Trainium2 kernel written in Bass

```python
import numpy as np
import jax
import jax.numpy as jnp

def _softmax(x, axis=-1):
    return jax.nn.softmax(x, axis=axis)

def _gelu(x):
    return jax.nn.gelu(x, approximate=True)

def _silu(x):
    return jax.nn.silu(x)

def _sigmoid(x):
    return jax.nn.sigmoid(x)

def _layernorm(x, axis=-1, eps=1e-05):
    m = jnp.mean(x, axis=axis, keepdims=True)
    v = jnp.var(x, axis=axis, keepdims=True)
    return (x - m) / jnp.sqrt(v + eps)

def _scatter_add(tgt, idx, src, axis=0):
    return tgt.at[idx].add(src)

def _segment_sum(src, seg, n):
    return jax.ops.segment_sum(src, seg, n)
kernel_name = 'mk_adj_preln_d4_adj_r2_0bacc2'

def setup_inputs(seed: int=0):
    np.random.seed(seed)
    _w = jnp.asarray

    def _rec_inputs():
        import jax
        import jax.numpy as jnp
        _gk = jax.random.key(seed)
        x = -0.0002928 + 1 * jax.random.normal(jax.random.fold_in(_gk, 1), (64, 128, 128), jnp.float32)
        _a = jax.random.bernoulli(jax.random.fold_in(_gk, 2), 0.015625, (64, 128, 128))
        _a = jnp.logical_or(_a, jnp.swapaxes(_a, -1, -2))
        _a = jnp.logical_or(_a, jnp.eye(128, dtype=bool))
        adj = _a.astype(jnp.int32)
        return (x, adj)
    x, adj = _rec_inputs()

    def _L0_gnn_setup():
        import jax, jax.numpy as jnp
        import numpy as np
        B, N, DIN, DOUT, H = (8, 1024, 128, 128, 8)
        HD = DOUT // H
        SCALE = HD ** (-0.5)
        key = jax.random.key(seed)
        ks = jax.random.split(key, 10)
        x = jax.random.normal(ks[0], (B, N, DIN), dtype=jnp.float32)
        adj = jax.random.randint(ks[1], (B, N, N), 0, 2, dtype=jnp.int32)
        eye = jnp.eye(N, dtype=jnp.int32)
        adj = jnp.maximum(adj, eye[None])
        s_in = (2.0 / DIN) ** 0.5
        s_out = (2.0 / DOUT) ** 0.5
        Wq = jax.random.normal(ks[2], (DOUT, DIN), dtype=jnp.float32) * s_in
        Wk = jax.random.normal(ks[3], (DOUT, DIN), dtype=jnp.float32) * s_in
        Wv = jax.random.normal(ks[4], (DOUT, DIN), dtype=jnp.float32) * s_in
        Wo = jax.random.normal(ks[5], (DOUT, DOUT), dtype=jnp.float32) * s_out
        bq = jnp.zeros((DOUT,), jnp.float32)
        bk = jnp.zeros((DOUT,), jnp.float32)
        bv = jnp.zeros((DOUT,), jnp.float32)
        bo = jnp.zeros((DOUT,), jnp.float32)
        return {'x': x, 'adj': adj, 'Wq': Wq, 'bq': bq, 'Wk': Wk, 'bk': bk, 'Wv': Wv, 'bv': bv, 'Wo': Wo, 'bo': bo}
    _L0_gnn_all = _L0_gnn_setup()
    _L0_gnn_in = {k: v for k, v in _L0_gnn_all.items() if k in ('Wq', 'bq', 'Wk', 'bk', 'Wv', 'bv', 'Wo', 'bo')}
    del _L0_gnn_all

    def _L1_gnn_setup():
        import jax, jax.numpy as jnp
        import numpy as np
        ALPHA = 0.2
        MASK_VAL = -9000000000000000.0
        key = jax.random.key(seed)
        k = jax.random.split(key, 6)
        B, N, D = (8, 1024, 128)
        x = jax.random.normal(k[0], (B, N, D), dtype=jnp.float32)
        adj = jax.random.randint(k[1], (B, N, N), 0, 2, dtype=jnp.int32)
        W = jax.random.normal(k[2], (D, D), dtype=jnp.float32) * (1.414 / np.sqrt(D))
        a = jax.random.normal(k[3], (2 * D, 1), dtype=jnp.float32) * 0.1
        han_w = jax.random.normal(k[4], (D, D), dtype=jnp.float32) / np.sqrt(D)
        han_b = jax.random.normal(k[5], (D,), dtype=jnp.float32) * 0.01
        return {'x': x, 'adj': adj, 'W': W, 'a': a, 'han_w': han_w, 'han_b': han_b}
    _L1_gnn_all = _L1_gnn_setup()
    _L1_gnn_in = {k: v for k, v in _L1_gnn_all.items() if k in ('W', 'a', 'han_w', 'han_b')}
    del _L1_gnn_all

    def _L2_gnn_setup():
        import jax, jax.numpy as jnp
        import numpy as np
        B, N, IN_F, OUT_F, H, NUM_EDGE_TYPES = (16, 256, 128, 128, 8, 50)
        HEAD_DIM = OUT_F // H
        LN_EPS = 1e-05
        key = jax.random.key(seed)
        ks = jax.random.split(key, 8)
        x = jax.random.normal(ks[0], (B, N, IN_F), dtype=jnp.float32)
        adj = jax.random.randint(ks[1], (B, N, N), 0, 2, dtype=jnp.int32)
        edge_types = jax.random.randint(ks[2], (B, N, N), 0, NUM_EDGE_TYPES, dtype=jnp.int32)
        W = jax.random.normal(ks[3], (IN_F, OUT_F), dtype=jnp.float32) / np.sqrt(IN_F)
        a1 = jax.random.normal(ks[4], (HEAD_DIM,), dtype=jnp.float32) / np.sqrt(HEAD_DIM)
        a2 = jax.random.normal(ks[5], (HEAD_DIM,), dtype=jnp.float32) / np.sqrt(HEAD_DIM)
        edge_emb = jax.random.normal(ks[6], (NUM_EDGE_TYPES, H), dtype=jnp.float32) * 0.02
        edge_emb = edge_emb.at[0].set(0.0)
        ln_gamma = jnp.ones((OUT_F,), dtype=jnp.float32)
        ln_beta = jnp.zeros((OUT_F,), dtype=jnp.float32)
        return {'x': x, 'adj': adj, 'edge_types': edge_types, 'W': W, 'a1': a1, 'a2': a2, 'edge_emb': edge_emb, 'ln_gamma': ln_gamma, 'ln_beta': ln_beta}
    _L2_gnn_all = _L2_gnn_setup()
    _L2_gnn_in = {k: v for k, v in _L2_gnn_all.items() if k in ('W', 'a1', 'a2', 'edge_emb', 'ln_gamma', 'ln_beta')}
    del _L2_gnn_all

    def _L3_gnn_setup():
        import jax, jax.numpy as jnp
        import numpy as np
        OUT = 128
        NUM_LAYERS = 3

        def _gru_cell(inp, h, w_ih, w_hh, b_ih, b_hh):
            gi = inp @ w_ih.T + b_ih
            gh = h @ w_hh.T + b_hh
            i_r, i_z, i_n = jnp.split(gi, 3, axis=-1)
            h_r, h_z, h_n = jnp.split(gh, 3, axis=-1)
            r = jax.nn.sigmoid(i_r + h_r)
            z = jax.nn.sigmoid(i_z + h_z)
            n = jnp.tanh(i_n + r * h_n)
            return (1.0 - z) * n + z * h
        key = jax.random.key(seed)
        ks = jax.random.split(key, 8)
        B, N, D = (32, 256, 128)
        x = jax.random.normal(ks[0], (B, N, D), dtype=jnp.float32)
        adj = jax.random.randint(ks[1], (B, N, N), 0, 2, dtype=jnp.int32)
        s = 1.0 / np.sqrt(OUT)
        weight = jax.random.uniform(ks[2], (NUM_LAYERS, OUT, OUT), jnp.float32, -s, s)
        w_ih = jax.random.uniform(ks[3], (3 * OUT, OUT), jnp.float32, -s, s)
        w_hh = jax.random.uniform(ks[4], (3 * OUT, OUT), jnp.float32, -s, s)
        b_ih = jax.random.uniform(ks[5], (3 * OUT,), jnp.float32, -s, s)
        b_hh = jax.random.uniform(ks[6], (3 * OUT,), jnp.float32, -s, s)
        return {'x': x, 'adj': adj, 'weight': weight, 'w_ih': w_ih, 'w_hh': w_hh, 'b_ih': b_ih, 'b_hh': b_hh}
    _L3_gnn_all = _L3_gnn_setup()
    _L3_gnn_in = {k: v for k, v in _L3_gnn_all.items() if k in ('weight', 'w_ih', 'w_hh', 'b_ih', 'b_hh')}
    del _L3_gnn_all
    return {'x': x, 'adj': adj, 'L0_gnn_Wq': _L0_gnn_in['Wq'], 'L0_gnn_bq': _L0_gnn_in['bq'], 'L0_gnn_Wk': _L0_gnn_in['Wk'], 'L0_gnn_bk': _L0_gnn_in['bk'], 'L0_gnn_Wv': _L0_gnn_in['Wv'], 'L0_gnn_bv': _L0_gnn_in['bv'], 'L0_gnn_Wo': _L0_gnn_in['Wo'], 'L0_gnn_bo': _L0_gnn_in['bo'], 'L1_gnn_W': _L1_gnn_in['W'], 'L1_gnn_a': _L1_gnn_in['a'], 'L1_gnn_han_w': _L1_gnn_in['han_w'], 'L1_gnn_han_b': _L1_gnn_in['han_b'], 'L2_gnn_W': _L2_gnn_in['W'], 'L2_gnn_a1': _L2_gnn_in['a1'], 'L2_gnn_a2': _L2_gnn_in['a2'], 'L2_gnn_edge_emb': _L2_gnn_in['edge_emb'], 'L2_gnn_ln_gamma': _L2_gnn_in['ln_gamma'], 'L2_gnn_ln_beta': _L2_gnn_in['ln_beta'], 'L3_gnn_weight': _L3_gnn_in['weight'], 'L3_gnn_w_ih': _L3_gnn_in['w_ih'], 'L3_gnn_w_hh': _L3_gnn_in['w_hh'], 'L3_gnn_b_ih': _L3_gnn_in['b_ih'], 'L3_gnn_b_hh': _L3_gnn_in['b_hh']}

def reference(x, adj, L0_gnn_Wq, L0_gnn_bq, L0_gnn_Wk, L0_gnn_bk, L0_gnn_Wv, L0_gnn_bv, L0_gnn_Wo, L0_gnn_bo, L1_gnn_W, L1_gnn_a, L1_gnn_han_w, L1_gnn_han_b, L2_gnn_W, L2_gnn_a1, L2_gnn_a2, L2_gnn_edge_emb, L2_gnn_ln_gamma, L2_gnn_ln_beta, L3_gnn_weight, L3_gnn_w_ih, L3_gnn_w_hh, L3_gnn_b_ih, L3_gnn_b_hh):
    import jax
    import jax.numpy as jnp

    def _L0_gnn_ref(x, adj, Wq, bq, Wk, bk, Wv, bv, Wo, bo):
        import jax, jax.numpy as jnp
        import numpy as np
        B, N, DIN, DOUT, H = (8, 1024, 128, 128, 8)
        HD = DOUT // H
        SCALE = HD ** (-0.5)
        b, n, _ = x.shape

        def proj(W, bias):
            y = jnp.einsum('bnf,of->bno', x, W) + bias
            return y.reshape(b, n, H, HD).transpose(0, 2, 1, 3)
        Q, K, V = (proj(Wq, bq), proj(Wk, bk), proj(Wv, bv))
        scores = jnp.einsum('bhnd,bhmd->bhnm', Q, K) * SCALE
        mask = adj[:, None, :, :] == 0
        scores = jnp.where(mask, -jnp.inf, scores)
        attn = jax.nn.softmax(scores, axis=-1)
        attn = jnp.nan_to_num(attn, nan=0.0)
        out = jnp.einsum('bhnm,bhmd->bhnd', attn, V)
        out = out.transpose(0, 2, 1, 3).reshape(b, n, DOUT)
        return jnp.einsum('bno,po->bnp', out, Wo) + bo

    def _L1_gnn_ref(x, adj, W, a, han_w, han_b):
        import jax, jax.numpy as jnp
        import numpy as np
        ALPHA = 0.2
        MASK_VAL = -9000000000000000.0
        B, N, D = x.shape
        h = jnp.matmul(x, W)
        a1 = jnp.matmul(x, a[:D])
        a2 = jnp.matmul(x, a[D:])
        e = jax.nn.leaky_relu(a1 + jnp.swapaxes(a2, 1, 2), negative_slope=ALPHA)
        att = jnp.where(adj > 0, e, MASK_VAL)
        att = jax.nn.softmax(att, axis=1)
        h_prime = jnp.matmul(att, h)
        hid = jax.nn.elu(h_prime)
        return jnp.matmul(hid, han_w) + han_b

    def _L2_gnn_ref(x, adj, edge_types, W, a1, a2, edge_emb, ln_gamma, ln_beta):
        import jax, jax.numpy as jnp
        import numpy as np
        B, N, IN_F, OUT_F, H, NUM_EDGE_TYPES = (16, 256, 128, 128, 8, 50)
        HEAD_DIM = OUT_F // H
        LN_EPS = 1e-05
        Bx, Nx, _ = x.shape
        Wh = (x @ W).reshape(Bx, Nx, H, HEAD_DIM)
        s1 = jnp.einsum('bnhd,d->bnh', Wh, a1)
        s2 = jnp.einsum('bnhd,d->bnh', Wh, a2)
        e = s1[:, :, None, :] + s2[:, None, :, :] + edge_emb[edge_types]
        e = jnp.where(e > 0, e, 0.2 * e)
        e = jnp.where((adj == 0)[..., None], jnp.float32(-1000000000.0), e)
        alpha = jax.nn.softmax(e, axis=2)
        h = jnp.einsum('bijh,bjhd->bihd', alpha, Wh).reshape(Bx, Nx, OUT_F)
        mu = jnp.mean(h, axis=-1, keepdims=True)
        var = jnp.mean(jnp.square(h - mu), axis=-1, keepdims=True)
        hn = (h - mu) * jax.lax.rsqrt(var + LN_EPS) * ln_gamma + ln_beta
        return jax.nn.elu(hn)

    def _L3_gnn_ref(x, adj, weight, w_ih, w_hh, b_ih, b_hh):
        import jax, jax.numpy as jnp
        import numpy as np
        OUT = 128
        NUM_LAYERS = 3

        def _gru_cell(inp, h, w_ih, w_hh, b_ih, b_hh):
            gi = inp @ w_ih.T + b_ih
            gh = h @ w_hh.T + b_hh
            i_r, i_z, i_n = jnp.split(gi, 3, axis=-1)
            h_r, h_z, h_n = jnp.split(gh, 3, axis=-1)
            r = jax.nn.sigmoid(i_r + h_r)
            z = jax.nn.sigmoid(i_z + h_z)
            n = jnp.tanh(i_n + r * h_n)
            return (1.0 - z) * n + z * h
        A = (adj != 0).astype(x.dtype)
        h = x
        L = weight.shape[0]
        for i in range(L):
            m = jnp.einsum('bnd,de->bne', h, weight[i])
            aggr = jnp.einsum('bst,bsd->btd', A, m)
            h = _gru_cell(aggr, h, w_ih, w_hh, b_ih, b_hh)
        return h
    h = jnp.maximum(_layernorm(x, axis=-1), 0.0)
    x = x + _L0_gnn_ref(h, adj, L0_gnn_Wq, L0_gnn_bq, L0_gnn_Wk, L0_gnn_bk, L0_gnn_Wv, L0_gnn_bv, L0_gnn_Wo, L0_gnn_bo)
    h = jnp.maximum(_layernorm(x, axis=-1), 0.0)
    x = x + _L1_gnn_ref(h, adj, L1_gnn_W, L1_gnn_a, L1_gnn_han_w, L1_gnn_han_b)
    h = jnp.maximum(_layernorm(x, axis=-1), 0.0)
    x = x + _L2_gnn_ref(h, adj, adj, L2_gnn_W, L2_gnn_a1, L2_gnn_a2, L2_gnn_edge_emb, L2_gnn_ln_gamma, L2_gnn_ln_beta)
    h = jnp.maximum(_layernorm(x, axis=-1), 0.0)
    x = x + _L3_gnn_ref(h, adj, L3_gnn_weight, L3_gnn_w_ih, L3_gnn_w_hh, L3_gnn_b_ih, L3_gnn_b_hh)
    return x

_drawn_inputs = setup_inputs


def setup_inputs(seed=0):
    import zlib

    import numpy as np

    out = dict(_drawn_inputs(seed))
    spreads = {'L0_gnn_bq': (0.0, 0.35),
     'L0_gnn_bk': (0.0, 2.0),
     'L0_gnn_bv': (0.0, 0.1),
     'L0_gnn_bo': (0.0, 0.1),
     'L2_gnn_ln_gamma': (1.0, 0.2),
     'L2_gnn_ln_beta': (0.0, 0.1)}
    factors = {'L1_gnn_han_b': 7.429, 'L2_gnn_edge_emb': 64.0, 'L3_gnn_b_hh': 4.621, 'L2_gnn_a1': 3.909}
    for name, (base, spread) in spreads.items():
        noise = np.random.default_rng([zlib.crc32(name.encode()), seed]).standard_normal(out[name].shape)
        drawn = base * np.exp(spread * noise) if base else spread * noise
        out[name] = jnp.asarray(drawn.astype(out[name].dtype))
    for name, factor in factors.items():
        out[name] = (out[name] * factor).astype(out[name].dtype)
    return out
```

```python
from contextlib import ExitStack

import concourse.bass as bass
from concourse import mybir

F32 = mybir.dt.float32
BF16 = mybir.dt.bfloat16
I32 = mybir.dt.int32
ALU = mybir.AluOpType
ACT = mybir.ActivationFunctionType
AX = mybir.AxisListType
RMAX = bass.bass_isa.ReduceOp.max

P = 128
GRAPHS = 64
G = 4
U = 2
H = 8
HD = 16
HV = HD + 1
QG = 2
RT = 4
RW = 32
SHIFT = HD
BIG = 1e30
BIG1 = 9e15
STEPS = 3
EPS = 1e-5
SLOPE = 0.2

WEIGHTS = [("wq", QG * P), ("wk", QG * P), ("wv", P), ("wo", P),
           ("w1", P), ("a1rep", P), ("a2col", 1), ("han", P),
           ("w2", P), ("w2T", P), ("adiag", 2 * H), ("emb", H),
           ("gwT", STEPS * P), ("wih", 3 * P), ("whh", 3 * P),
           ("bq", QG), ("bk", QG), ("bih", 3), ("bhh", 3),
           ("bv", P), ("bo", P), ("hanb", P), ("gamma", P), ("beta", P),
           ("ident", P), ("sel", H * P)]
OFFSET = {}
_at = 0
for _name, _n in WEIGHTS:
    OFFSET[_name] = (_at, _n)
    _at += _n
NW = _at


def bcast(ap, axis, n):
    a = ap.unsqueeze(axis)
    shape = list(a.shape)
    shape[axis] = n
    return a.broadcast_to(shape)


def primed(n):
    return n + 1


def prime(eng, *sems):
    for s in sems:
        eng.sem_inc(s, 1)


def settle(eng, passed):
    eng.sem_inc(passed, 1)


def graph_layers(nc, x, adj, adjT, wpack, out, layers=4):
    with ExitStack() as ctx:
        def sb(name, shape, dt=F32):
            return ctx.enter_context(nc.sbuf_tensor(name, shape, dt))

        def sem(name):
            return ctx.enter_context(nc.semaphore(name))

        X = sb("X", [P, GRAPHS, P])
        W = sb("W", [P, NW])
        stats = sb("stats", [P, G, 6])
        meanvar = sb("meanvar", [P, G, 2])
        mean = sb("mean", [P, GRAPHS])
        var = sb("var", [P, GRAPHS])
        rstd = sb("rstd", [P, GRAPHS])
        epsc = sb("epsc", [P, 1])
        scratch = sb("scratch", [P, 1])
        identb = sb("identb", [P, P], BF16)
        psum = ctx.enter_context(nc.psum_tensor("psum", [P, 8, 512], F32))

        def w(name):
            a, n = OFFSET[name]
            return W[:, a:a + n]

        ident = w("ident")

        io = (nc, x, adj, adjT, wpack, out)
        env = dict(nc=nc, x=x, adj=adj, adjT=adjT, wpack=wpack, out=out, X=X, W=W, w=w, ident=ident,
                   identb=identb, stats=stats, meanvar=meanvar, mean=mean, var=var, rstd=rstd, epsc=epsc,
                   psum=psum, scratch=scratch, sb=sb, sem=sem)
        load(env)
        if layers > 0:
            attention_layer(env)
        if layers > 1:
            column_layer(env)
        if layers > 2:
            edge_layer(env)
        if layers > 3:
            gated_layer(env)
        else:
            store(env)


def load(env):
    nc, x, X, W, sem = (env[k] for k in ("nc", "x", "X", "W", "sem"))
    stats, meanvar, mean, var = (env[k] for k in ("stats", "meanvar", "mean", "var"))
    NL = GRAPHS // G
    x_in, w_in = sem("x_in"), sem("w_in")
    x_stats, x_mv, x_saved = sem("x_stats"), sem("x_mv"), sem("x_saved")
    const = sem("const")
    env["w_in"] = w_in
    env["passed"] = sem("passed")
    with nc.Block() as block:
        @block.sync
        def _(sp):
            with sp.Fori(0, NL) as i:
                sp.dma_start(X[:, bass.ds(i * G, G), :], x[:, bass.ds(i * G, G), :]).then_inc(x_in, 16)

        @block.scalar
        def _(act):
            act.dma_start(W[:, :], env["wpack"]).then_inc(w_in, 16)
            act.wait_ge(w_in, 16)

        @block.vector
        def _(dve):
            prime(dve, x_mv, x_saved)
            dve.memset(env["epsc"][:, :], EPS).then_inc(const, 1)
            dve.wait_ge(w_in, 16)
            dve.tensor_copy(env["identb"][:, :], env["ident"]).then_inc(const, 1)
            dve.wait_ge(const, 2)
            dve.wait_ge(x_in, 16 * NL)
            with dve.Fori(0, NL) as i:
                dve.wait_ge(w_in, 16)
                dve.wait_ge(x_mv, primed(i * G))
                settle(dve, env["passed"])
                for b in range(G):
                    dve.bn_stats(stats[:, b, :], X[:, bass.ds(i * G + b, 1), :]).then_inc(x_stats, 1)
                dve.wait_ge(w_in, 16)
                dve.wait_ge(x_stats, (i + 1) * G)
                dve.wait_ge(x_saved, primed(2 * i))
                settle(dve, env["passed"])
                for b in range(G):
                    dve.bn_aggr(meanvar[:, b, :], stats[:, b, :]).then_inc(x_mv, 1)
                dve.wait_ge(w_in, 16)
                dve.wait_ge(x_mv, primed((i + 1) * G))
                dve.tensor_copy(mean[:, bass.ds(i * G, G)], meanvar[:, :, 0]).then_inc(x_saved, 1)
                dve.tensor_copy(var[:, bass.ds(i * G, G)], meanvar[:, :, 1]).then_inc(x_saved, 1)
            dve.wait_ge(x_saved, primed(2 * NL))


def attention_layer(env):
    nc, X, w, ident, identb, psum, sb, sem = (env[k] for k in ("nc", "X", "w", "ident", "identb", "psum", "sb", "sem"))
    stats, meanvar, mean, var, rstd = (env[k] for k in ("stats", "meanvar", "mean", "var", "rstd"))
    NI = GRAPHS // G
    C = U * QG
    with ExitStack() as ctx:
        def sb(name, shape, dt=F32):
            return ctx.enter_context(nc.sbuf_tensor("a_" + name, shape, dt))

        def sem(name):
            return ctx.enter_context(nc.semaphore("a_" + name))

        adj_i = sb("adj_i", [P, G, P], I32)
        adjT_i = sb("adjT_i", [P, G, P], I32)
        maskN = sb("maskN", [P, G, P], BF16)
        maskT = sb("maskT", [P, G, P], BF16)
        hN = sb("hN", [P, G, P])
        hT = sb("hT", [P, G * P])
        QT = sb("QT", [P, QG, G, P])
        KT = sb("KT", [P, QG, G, P])
        V = sb("V", [P, G, H, HV])
        negmax = [sb(f"negmax{u}", [P, C, P]) for u in range(2)]
        QTs = [sb(f"QTs{u}", [P, C, P]) for u in range(2)]
        PT = [sb(f"PT{u}", [P, RT, C, P]) for u in range(2)]
        rden = [sb(f"rden{u}", [P, U, H]) for u in range(2)]
        O = [sb(f"O{u}", [P, U, P]) for u in range(2)]
        OT = [sb(f"OT{u}", [P, U * P]) for u in range(2)]

        adj_in, adjT_in, mask_ready = sem("adj_in"), sem("adjT_in"), sem("mask_ready")
        clean, ln_ready, bias_added, ht_psum, ht_ready = (sem(n) for n in ("clean", "ln_ready", "bias_added", "ht_psum", "ht_ready"))
        q_psum, k_psum, v_psum, qk_ready, kv_ready = (sem(n) for n in ("q_psum", "k_psum", "v_psum", "qk_ready", "kv_ready"))
        scores, max_ready, maxT, qs_ready, scoresT, exp_ready = (sem(n) for n in ("scores", "max_ready", "maxT", "qs_ready", "scoresT", "exp_ready"))
        pv, rden_ready, o_ready, oT_psum, oT_ready, y_psum = (sem(n) for n in ("pv", "rden_ready", "o_ready", "oT_psum", "oT_ready", "y_psum"))
        x_ready, st_ready, mv_ready, stat_ready, sd_ready, rs_ready = (sem(n) for n in ("x_ready", "st_ready", "mv_ready", "stat_ready", "sd_ready", "rs_ready"))

        def bank(n):
            return psum[:, n, :]

        with nc.Block() as block:
            @block.sync
            def _(sp):
                with sp.Fori(0, NI) as i:
                    sp.wait_ge(mask_ready, primed(2 * i))
                    sp.dma_start(adj_i[:, :, :], env["adj"][:, bass.ds(i * G, G), :]).then_inc(adj_in, 16)
                    sp.dma_start(adjT_i[:, :, :], env["adjT"][:, bass.ds(i * G, G), :]).then_inc(adjT_in, 16)

            @block.gpsimd
            def _(pool):
                prime(pool, mask_ready)
                pool.memset(V[:, :, :, :], 1.0).then_inc(clean, 1)
                for u in range(2):
                    pool.memset(negmax[u][:, :, :], 0.0).then_inc(clean, 1)
                with pool.Fori(0, NI) as i:
                    pool.wait_ge(clean, 3)
                    pool.wait_ge(scoresT, primed(2 * i))
                    pool.wait_ge(adj_in, 16 * i + 16)
                    settle(pool, env["passed"])
                    pool.tensor_scalar(maskN[:, :, :], adj_i[:, :, :], BIG, -BIG, ALU.mult, ALU.add).then_inc(mask_ready, 1)
                    pool.wait_ge(clean, 3)
                    pool.wait_ge(adjT_in, 16 * i + 16)
                    settle(pool, env["passed"])
                    pool.tensor_scalar(maskT[:, :, :], adjT_i[:, :, :], BIG, -BIG, ALU.mult, ALU.add).then_inc(mask_ready, 1)
                    pool.wait_ge(ln_ready, i + 1)
                    xg = X[:, bass.ds(i * G, G), :]
                    pool.tensor_tensor(xg, xg, bcast(w("bo"), 1, G), ALU.add).then_inc(bias_added, 1)

            @block.tensor
            def _(pe):
                prime(pe, scoresT, v_psum, y_psum, ht_psum, pv, maxT)
                with pe.Fori(0, NI) as i:
                    pe.wait_ge(x_ready, primed(2 * i))
                    pe.wait_ge(ln_ready, i + 1)
                    for b in range(G):
                        m = pe.transpose(psum[:, 0, b * P:(b + 1) * P], hN[:, b, :], ident)
                    m.then_inc(ht_psum, 1)
                    pe.wait_ge(ht_ready, i + 1)
                    for q in range(QG):
                        pe.matmul(bank(1 + q), w("wq")[:, q * P:(q + 1) * P], hT[:, :], start=True, stop=True).then_inc(q_psum, 1)
                    for q in range(QG):
                        pe.matmul(bank(3 + q), w("wk")[:, q * P:(q + 1) * P], hT[:, :], start=True, stop=True).then_inc(k_psum, 1)
                    for b in range(G):
                        m = pe.matmul(psum[:, 5, b * P:(b + 1) * P], hT[:, b * P:(b + 1) * P], w("wv"), start=True, stop=True)
                    m.then_inc(v_psum, 1)
                    for u in range(2):
                        if u == 0:
                            pe.wait_ge(qk_ready, 3 * i + 3)
                            pe.wait_ge(kv_ready, 2 * i + 1)
                            pe.wait_ge(mask_ready, primed(2 * i + 2))
                        else:
                            pe.wait_ge(kv_ready, 2 * i + 2)
                        for b in range(U):
                            for q in range(QG):
                                for r in range(RT):
                                    rows = slice(r * RW, (r + 1) * RW)
                                    c = b * QG + q
                                    pe.matmul(psum[:, 4 * u + r, c * P:(c + 1) * P], QT[rows, q, U * u + b, :],
                                              KT[rows, q, U * u + b, :], start=(c == 0), stop=False, skip_group_check=True)
                        for r in range(RT):
                            m = pe.matmul(bank(4 * u + r), identb[:, :], bcast(maskN[:, U * u:U * u + U, :], 2, QG),
                                          start=False, stop=True, skip_group_check=True)
                        m.then_inc(scores, 1)
                    for u in range(2):
                        n = 2 * i + u
                        pe.wait_ge(max_ready, n + 1)
                        for c in range(C):
                            m = pe.transpose(psum[:, 4 * u, c * P:(c + 1) * P], negmax[u][:, c, :], ident)
                        m.then_inc(maxT, 1)
                        pe.wait_ge(qs_ready, n + 1)
                        for b in range(U):
                            for q in range(QG):
                                for r in range(RT):
                                    rows = slice(r * RW, (r + 1) * RW)
                                    c = b * QG + q
                                    pe.matmul(psum[:, 4 * u + r, c * P:(c + 1) * P], KT[rows, q, U * u + b, :],
                                              QTs[u][rows, c, :], start=(c == 0), stop=False, skip_group_check=True)
                        for r in range(RT):
                            m = pe.matmul(bank(4 * u + r), identb[:, :], bcast(maskT[:, U * u:U * u + U, :], 2, QG),
                                          start=False, stop=True, skip_group_check=True)
                        m.then_inc(scoresT, 1)
                    for u in range(2):
                        n = 2 * i + u
                        pe.wait_ge(exp_ready, n + 1)
                        for b in range(U):
                            for h in range(H):
                                q, r = divmod(h, RT)
                                at = (b * H + h) * HV
                                m = pe.matmul(psum[:, 4 * u, at:at + HV], PT[u][:, r, b * QG + q, :], V[:, U * u + b, h, :],
                                              start=True, stop=True)
                        m.then_inc(pv, 1)
                    for u in range(2):
                        n = 2 * i + u
                        pe.wait_ge(o_ready, n + 1)
                        for b in range(U):
                            m = pe.transpose(psum[:, 4 * u + 1, b * P:(b + 1) * P], O[u][:, b, :], ident)
                        m.then_inc(oT_psum, 1)
                        pe.wait_ge(oT_ready, n + 1)
                        for b in range(U):
                            m = pe.matmul(psum[:, 4 * u + 2, b * P:(b + 1) * P], OT[u][:, b * P:(b + 1) * P], w("wo"), start=True, stop=True)
                        m.then_inc(y_psum, 1)

            @block.scalar
            def _(act):
                act.activation(rstd[:, :], var[:, :], ACT.Sqrt, bias=env["epsc"][:, :]).then_inc(sd_ready, 1)
                act.activation(env["scratch"][:, :], env["epsc"][:, :], ACT.Exp)
                with act.Fori(0, NI) as i:
                    act.wait_ge(ht_psum, primed(i + 1))
                    act.wait_ge(v_psum, primed(i))
                    act.activation(hT[:, :], bank(0), ACT.Relu).then_inc(ht_ready, 1)
                    for q in range(QG):
                        act.wait_ge(q_psum, 2 * i + q + 1)
                        act.activation(QT[:, q, :, :], bank(1 + q), ACT.Identity, bias=w("bq")[:, q:q + 1], scale=1.0 / 4).then_inc(qk_ready, 1)
                    act.wait_ge(k_psum, 2 * i + 1)
                    act.activation(KT[:, 0, :, :], bank(3), ACT.Identity, bias=w("bk")[:, 0:1]).then_inc(qk_ready, 1)
                    for u in range(2):
                        n = 2 * i + u
                        act.wait_ge(scoresT, primed(n + 1))
                        act.activation(PT[u][:, :, :, :], psum[:, 4 * u:4 * u + RT, :].rearrange("p r (c n) -> p r c n", c=C),
                                       ACT.Exp).then_inc(exp_ready, 1)
                    for u in range(2):
                        n = 2 * i + u
                        act.wait_ge(oT_psum, n + 1)
                        act.wait_ge(y_psum, primed(2 * i))
                        act.activation(OT[u][:, :], psum[:, 4 * u + 1, 0:U * P], ACT.Copy).then_inc(oT_ready, 1)

            @block.vector
            def _(dve):
                prime(dve, x_ready)
                dve.wait_ge(sd_ready, 1)
                dve.reciprocal(rstd[:, :], rstd[:, :]).then_inc(rs_ready, 1)
                dve.tensor_scalar(w("bq"), w("bq"), 1.0 / 4, None, ALU.mult).then_inc(rs_ready, 1)
                dve.wait_ge(rs_ready, 2)
                with dve.Fori(0, NI) as i:
                    dve.wait_ge(ht_psum, primed(i))
                    for b in range(G):
                        g = i * G + b
                        m = dve.tensor_scalar(hN[:, b, :], X[:, bass.ds(g, 1), :], mean[:, bass.ds(g, 1)], rstd[:, bass.ds(g, 1)],
                                              ALU.subtract, ALU.mult)
                    m.then_inc(ln_ready, 1)
                    dve.wait_ge(k_psum, 2 * i + 2)
                    dve.tensor_scalar(KT[:, 1, :, :], bank(4), w("bk")[:, 1:2], None, ALU.add).then_inc(kv_ready, 1)
                    dve.wait_ge(v_psum, primed(i + 1))
                    dve.wait_ge(clean, 3)
                    dve.wait_ge(pv, primed(2 * i))
                    dve.tensor_tensor(V[:, :, :, 0:HD], psum[:, 5, :].rearrange("p (b h d) -> p b h d", b=G, h=H),
                                      bcast(w("bv").rearrange("p (h d) -> p h d", h=H), 1, G), ALU.add).then_inc(kv_ready, 1)
                    for u in range(2):
                        n = 2 * i + u
                        dve.wait_ge(scores, n + 1)
                        dve.wait_ge(maxT, primed(2 * i))
                        dve.tensor_reduce(negmax[u][:, :, :].rearrange("p c (r w) -> p r c w", r=RT)[:, :, :, SHIFT],
                                          psum[:, 4 * u:4 * u + RT, :].rearrange("p r (c n) -> p r c n", c=C),
                                          AX.X, ALU.max, negate=True).then_inc(max_ready, 1)
                    for u in range(2):
                        n = 2 * i + u
                        dve.wait_ge(maxT, primed(n + 1))
                        dve.tensor_tensor(QTs[u][:, :, :].rearrange("p (b q) n -> p b q n", b=U),
                                          psum[:, 4 * u, :].rearrange("p (b q n) -> p b q n", b=U, q=QG),
                                          QT[:, :, U * u:U * u + U, :].rearrange("p q b n -> p b q n"), ALU.add).then_inc(qs_ready, 1)
                    for u in range(2):
                        n = 2 * i + u
                        dve.wait_ge(pv, primed(n + 1))
                        y = psum[:, 4 * u, 0:U * H * HV].rearrange("p (b h d) -> p b h d", b=U, h=H)
                        dve.reciprocal(rden[u][:, :, :], y[:, :, :, HD]).then_inc(rden_ready, 1)
                        dve.wait_ge(rden_ready, n + 1)
                        dve.tensor_tensor(O[u][:, :, :].rearrange("p b (h d) -> p b h d", h=H), y[:, :, :, 0:HD],
                                          bcast(rden[u][:, :, :], 3, HD), ALU.mult).then_inc(o_ready, 1)
                    for u in range(2):
                        n = 2 * i + u
                        g = i * G + u * U
                        dve.wait_ge(y_psum, primed(n + 1))
                        dve.wait_ge(bias_added, i + 1)
                        residual(env, dve, g, U, psum[:, 4 * u + 2, 0:U * P].rearrange("p (b n) -> p b n", b=U), n,
                                 x_ready, st_ready, mv_ready, stat_ready)


def store(env):
    nc, sem, X, out = (env[k] for k in ("nc", "sem", "X", "out"))
    stored = sem("stored")
    with nc.Block() as block:
        @block.sync
        def _(sp):
            sp.dma_start(out, X[:, :, :]).then_inc(stored, 16)
            sp.wait_ge(stored, 16)


def column_layer(env):
    nc, X, w, ident, psum = (env[k] for k in ("nc", "X", "w", "ident", "psum"))
    stats, meanvar, mean, var, rstd = (env[k] for k in ("stats", "meanvar", "mean", "var", "rstd"))
    NI = GRAPHS // (2 * G)
    with ExitStack() as ctx:
        def sb(name, shape, dt=F32):
            return [ctx.enter_context(nc.sbuf_tensor(f"c_{name}{u}", shape, dt)) for u in range(2)]

        def sem(name):
            return ctx.enter_context(nc.semaphore("c_" + name))

        adjT_i, maskT = sb("adjT_i", [P, G, P], I32), sb("maskT", [P, G, P])
        hN, hT = sb("hN", [P, G, P]), sb("hT", [P, G * P])
        a2 = sb("a2", [P, G])
        E, PT = sb("E", [P, G, P]), sb("PT", [P, G, P])
        negmax, den, rden = sb("negmax", [P, G]), sb("den", [P, G]), sb("rden", [P, G])
        hs = sb("hs", [P, G, P])
        pos, neg, hid = sb("pos", [P, G, P]), sb("neg", [P, G, P]), sb("hid", [P, G, P])
        hidT = sb("hidT", [P, G * P])

        adj_in = [sem("adj_in0"), sem("adj_in1")]
        leaky_ready, mask_ready, sd_ready, rs_ready = sem("leaky_ready"), sem("mask_ready"), sem("sd_ready"), sem("rs_ready")
        ln_ready, bias_added, hT_psum, hT_ready = (sem(n) for n in ("ln_ready", "bias_added", "hT_psum", "hT_ready"))
        proj, a2_ready, e_ready, em_ready, max_ready, exp_ready = (sem(n) for n in ("proj", "a2_ready", "e_ready", "em_ready", "max_ready", "exp_ready"))
        rden_ready, hs_ready, att, neg_ready, pos_ready, nexp_ready, hid_ready = (sem(n) for n in ("rden_ready", "hs_ready", "att", "neg_ready", "pos_ready", "nexp_ready", "hid_ready"))
        hidT_psum, hidT_ready, y_psum, x_ready, st_ready, mv_ready, stat_ready = (sem(n) for n in ("hidT_psum", "hidT_ready", "y_psum", "x_ready", "st_ready", "mv_ready", "stat_ready"))

        def bank(u, k):
            return psum[:, 4 * u + k, :]

        def graphs(u, k):
            return psum[:, 4 * u + k, :].rearrange("p (b n) -> p b n", b=G)

        with nc.Block() as block:
            @block.sync
            def _(sp):
                with sp.Fori(0, NI) as i:
                    for u in range(2):
                        sp.wait_ge(mask_ready, primed(2 * i))
                        sp.dma_start(adjT_i[u][:, :, :], env["adjT"][:, bass.ds((2 * i + u) * G, G), :]).then_inc(adj_in[u], 16)

            @block.gpsimd
            def _(pool):
                prime(pool, mask_ready)
                with pool.Fori(0, NI) as i:
                    for u in range(2):
                        pool.wait_ge(sd_ready, 1)
                        pool.wait_ge(em_ready, primed(2 * i))
                        pool.wait_ge(adj_in[u], 16 * i + 16)
                        settle(pool, env["passed"])
                        pool.tensor_scalar(maskT[u][:, :, :], adjT_i[u][:, :, :], BIG1, -BIG1, ALU.mult, ALU.add).then_inc(mask_ready, 1)
                    for u in range(2):
                        pool.wait_ge(ln_ready, 2 * i + u + 1)
                        xg = X[:, bass.ds((2 * i + u) * G, G), :]
                        pool.tensor_tensor(xg, xg, bcast(w("hanb"), 1, G), ALU.add).then_inc(bias_added, 1)

            @block.tensor
            def _(pe):
                with pe.Fori(0, NI) as i:
                    for u in range(2):
                        n = 2 * i + u
                        pe.wait_ge(ln_ready, n + 1)
                        pe.wait_ge(x_ready, primed(2 * i))
                        for b in range(G):
                            m = pe.transpose(graphs(u, 0)[:, b, :], hN[u][:, b, :], ident)
                        m.then_inc(hT_psum, 1)
                    for u in range(2):
                        n = 2 * i + u
                        pe.wait_ge(hT_ready, n + 1)
                        for b in range(G):
                            pe.matmul(psum[:, 4 * u + 2, b:b + 1], hT[u][:, b * P:(b + 1) * P], w("a2col"), start=True, stop=True)
                        pe.matmul(bank(u, 3), w("a1rep"), hT[u][:, :], start=True, stop=True)
                        for b in range(G):
                            m = pe.matmul(graphs(u, 1)[:, b, :], hT[u][:, b * P:(b + 1) * P], w("w1"), start=True, stop=True)
                        m.then_inc(proj, 1)
                    for u in range(2):
                        n = 2 * i + u
                        pe.wait_ge(exp_ready, G * (n + 1))
                        pe.wait_ge(hs_ready, n + 1)
                        for b in range(G):
                            m = pe.matmul(graphs(u, 2)[:, b, :], PT[u][:, b, :], hs[u][:, b, :], start=True, stop=True)
                        m.then_inc(att, 1)
                    for u in range(2):
                        n = 2 * i + u
                        pe.wait_ge(hid_ready, n + 1)
                        for b in range(G):
                            m = pe.transpose(graphs(u, 0)[:, b, :], hid[u][:, b, :], ident)
                        m.then_inc(hidT_psum, 1)
                    for u in range(2):
                        n = 2 * i + u
                        pe.wait_ge(hidT_ready, n + 1)
                        for b in range(G):
                            m = pe.matmul(graphs(u, 1)[:, b, :], hidT[u][:, b * P:(b + 1) * P], w("han"), start=True, stop=True)
                        m.then_inc(y_psum, 1)

            @block.scalar
            def _(act):
                act.activation(rstd[:, :], var[:, :], ACT.Sqrt, bias=env["epsc"][:, :]).then_inc(sd_ready, 1)
                act.activation(env["scratch"][:, :], env["epsc"][:, :], ACT.Exp)
                with act.Fori(0, NI) as i:
                    for u in range(2):
                        n = 2 * i + u
                        act.wait_ge(hT_psum, n + 1)
                        act.activation(hT[u][:, :], bank(u, 0), ACT.Relu).then_inc(hT_ready, 1)
                    for u in range(2):
                        n = 2 * i + u
                        act.wait_ge(proj, n + 1)
                        act.wait_ge(a2_ready, n + 1)
                        for b in range(G):
                            m = act.activation(E[u][:, b, :], graphs(u, 3)[:, b, :], ACT.Identity, bias=a2[u][:, b:b + 1])
                        m.then_inc(e_ready, 1)
                    for u in range(2):
                        n = 2 * i + u
                        act.wait_ge(max_ready, n + 1)
                        for b in range(G):
                            act.activation(PT[u][:, b, :], E[u][:, b, :], ACT.Exp, bias=negmax[u][:, b:b + 1],
                                           accum_out=den[u][:, b:b + 1]).then_inc(exp_ready, 1)
                    for u in range(2):
                        n = 2 * i + u
                        act.wait_ge(neg_ready, n + 1)
                        act.activation(neg[u][:, :, :], neg[u][:, :, :], ACT.Exp).then_inc(nexp_ready, 1)
                    for u in range(2):
                        n = 2 * i + u
                        act.wait_ge(hidT_psum, n + 1)
                        act.activation(hidT[u][:, :], bank(u, 0), ACT.Copy).then_inc(hidT_ready, 1)

            @block.vector
            def _(dve):
                prime(dve, em_ready, x_ready)
                dve.wait_ge(sd_ready, 1)
                dve.reciprocal(rstd[:, :], rstd[:, :]).then_inc(rs_ready, 1)
                dve.wait_ge(rs_ready, 1)
                with dve.Fori(0, NI) as i:
                    for u in range(2):
                        n = 2 * i + u
                        for b in range(G):
                            g = n * G + b
                            m = dve.tensor_scalar(hN[u][:, b, :], X[:, bass.ds(g, 1), :], mean[:, bass.ds(g, 1)], rstd[:, bass.ds(g, 1)],
                                                  ALU.subtract, ALU.mult)
                        m.then_inc(ln_ready, 1)
                    for u in range(2):
                        n = 2 * i + u
                        dve.wait_ge(proj, n + 1)
                        dve.tensor_copy(a2[u][:, :], psum[:, 4 * u + 2, 0:G]).then_inc(a2_ready, 1)
                    for u in range(2):
                        n = 2 * i + u
                        dve.wait_ge(e_ready, n + 1)
                        dve.wait_ge(mask_ready, primed(n + 1))
                        dve.scalar_tensor_tensor(out=E[u][:, :, :], in0=E[u][:, :, :], scalar=SLOPE, in1=E[u][:, :, :],
                                                 op0=ALU.mult, op1=ALU.max).then_inc(leaky_ready, 1)
                        dve.wait_ge(leaky_ready, n + 1)
                        dve.tensor_tensor(E[u][:, :, :], E[u][:, :, :], maskT[u][:, :, :], ALU.add).then_inc(em_ready, 1)
                        dve.wait_ge(em_ready, primed(n + 1))
                        dve.tensor_reduce(negmax[u][:, :], E[u][:, :, :], AX.X, ALU.max, negate=True).then_inc(max_ready, 1)
                    for u in range(2):
                        n = 2 * i + u
                        dve.wait_ge(exp_ready, G * (n + 1))
                        dve.reciprocal(rden[u][:, :], den[u][:, :]).then_inc(rden_ready, 1)
                        dve.wait_ge(rden_ready, n + 1)
                        dve.tensor_tensor(hs[u][:, :, :], graphs(u, 1), bcast(rden[u][:, :], 2, P), ALU.mult).then_inc(hs_ready, 1)
                    for u in range(2):
                        n = 2 * i + u
                        dve.wait_ge(att, n + 1)
                        dve.tensor_scalar(neg[u][:, :, :], graphs(u, 2), 0.0, None, ALU.min).then_inc(neg_ready, 1)
                        dve.tensor_scalar(pos[u][:, :, :], graphs(u, 2), 0.0, None, ALU.max).then_inc(pos_ready, 1)
                    for u in range(2):
                        n = 2 * i + u
                        dve.wait_ge(nexp_ready, n + 1)
                        dve.wait_ge(pos_ready, n + 1)
                        dve.scalar_tensor_tensor(out=hid[u][:, :, :], in0=neg[u][:, :, :], scalar=-1.0, in1=pos[u][:, :, :],
                                                 op0=ALU.add, op1=ALU.add).then_inc(hid_ready, 1)
                    for u in range(2):
                        n = 2 * i + u
                        dve.wait_ge(y_psum, n + 1)
                        dve.wait_ge(bias_added, n + 1)
                        residual(env, dve, n * G, G, graphs(u, 1), n, x_ready, st_ready, mv_ready, stat_ready)


def residual(env, dve, g, count, y, n, x_ready, st_ready, mv_ready, stat_ready):
    X, stats, meanvar, mean, var = (env[k] for k in ("X", "stats", "meanvar", "mean", "var"))
    xu = X[:, bass.ds(g, count), :]
    dve.tensor_tensor(xu, y, xu, ALU.add).then_inc(x_ready, 1)
    dve.wait_ge(env["w_in"], 16)
    dve.wait_ge(x_ready, primed(n + 1))
    settle(dve, env["passed"])
    for b in range(count):
        m = dve.bn_stats(stats[:, b, :], X[:, bass.ds(g + b, 1), :])
    m.then_inc(st_ready, 1)
    dve.wait_ge(env["w_in"], 16)
    dve.wait_ge(st_ready, n + 1)
    settle(dve, env["passed"])
    for b in range(count):
        m = dve.bn_aggr(meanvar[:, b, :], stats[:, b, :])
    m.then_inc(mv_ready, 1)
    dve.wait_ge(env["w_in"], 16)
    dve.wait_ge(mv_ready, n + 1)
    dve.tensor_copy(mean[:, bass.ds(g, count)], meanvar[:, 0:count, 0])
    dve.tensor_copy(var[:, bass.ds(g, count)], meanvar[:, 0:count, 1]).then_inc(stat_ready, 1)
    dve.wait_ge(stat_ready, n + 1)


def edge_layer(env):
    nc, X, w, ident, identb, psum = (env[k] for k in ("nc", "X", "w", "ident", "identb", "psum"))
    stats, meanvar, mean, var, rstd = (env[k] for k in ("stats", "meanvar", "mean", "var", "rstd"))
    NI = GRAPHS // (2 * G)
    PARTS = 3
    with ExitStack() as ctx:
        def one(name, shape, dt=F32):
            return ctx.enter_context(nc.sbuf_tensor("e_" + name, shape, dt))

        def sb(name, shape, dt=F32):
            return [one(f"{name}{u}", shape, dt) for u in range(2)]

        def sem(name):
            return ctx.enter_context(nc.semaphore("e_" + name))

        Y = one("Y", [P, GRAPHS, P])
        ymean, yvar = one("ymean", [P, GRAPHS]), one("yvar", [P, GRAPHS])
        ws = one("ws", [P, 2 * H])
        selb = one("selb", [PARTS * H, H, P], BF16)
        adjT_i, maskT, MT = sb("adjT_i", [P, G, P], I32), sb("maskT", [P, G, P], BF16), sb("MT", [P, G, P])
        hN, hT = sb("hN", [P, G, P]), sb("hT", [P, G * P])
        s1, s2, c, d, t, m02, tm, tm2 = (sb(n, [P, G, H]) for n in ("s1", "s2", "c", "d", "t", "m", "tm", "tm2"))
        rem1, rem2, parts = sb("rem1", [P, G, H]), sb("rem2", [P, G, H]), sb("parts", [P, G, PARTS * H], BF16)
        ns2, up, upp = sb("ns2", [P, G, H]), sb("up", [P, G, H]), sb("upp", [P, G, H])
        rows = sb("rows", [PARTS * H, G, P], BF16)
        R, R2 = sb("R", [P, G, H, 2 * HV]), sb("R2", [P, G, H, HV])
        Gm = sb("Gm", [P, H, P])
        y1, y2, rden = sb("y1", [P, H, HV]), sb("y2", [P, H, HV]), sb("rden", [P, H])

        adj_in = [sem("adj_in0"), sem("adj_in1")]
        names = ("mask_ready", "sd_ready", "rs_ready", "ln_ready", "ws_psum", "ws_ready", "hT_psum", "hT_ready", "proj",
                 "s_ready", "c_ready", "d_ready", "t_ready", "m_ready", "tm_ready", "v_ready", "u_ready", "hi_ready",
                 "rem1_ready", "mid_ready", "rem2_ready", "parts_ready", "rows_psum", "rows_ready", "vv_ready", "r_ready",
                 "z_psum", "g_ready", "pv", "y1_ready", "y2_ready", "rden_ready", "yy_ready", "st_ready", "mv_ready", "stat_ready")
        s = {n: sem(n) for n in names}
        w_in = env["w_in"]

        def bank(u, k):
            return psum[:, 4 * u + k, :]

        def graphs(u, k):
            return psum[:, 4 * u + k, :].rearrange("p (b n) -> p b n", b=G)

        with nc.Block() as block:
            @block.sync
            def _(sp):
                with sp.Fori(0, NI) as i:
                    for u in range(2):
                        sp.wait_ge(s["mask_ready"], primed(4 * i))
                        sp.dma_start(adjT_i[u][:, :, :], env["adjT"][:, bass.ds((2 * i + u) * G, G), :]).then_inc(adj_in[u], 16)

            @block.gpsimd
            def _(pool):
                prime(pool, s["mask_ready"])
                with pool.Fori(0, NI) as i:
                    for u in range(2):
                        n = 2 * i + u
                        pool.wait_ge(w_in, 16)
                        pool.wait_ge(s["pv"], primed(2 * G * i))
                        pool.wait_ge(adj_in[u], 16 * i + 16)
                        settle(pool, env["passed"])
                        pool.tensor_scalar(maskT[u][:, :, :], adjT_i[u][:, :, :], BIG, -BIG, ALU.mult, ALU.add).then_inc(s["mask_ready"], 1)
                        pool.tensor_scalar(MT[u][:, :, :], adjT_i[u][:, :, :], 1.0, 0.0, ALU.min, ALU.max).then_inc(s["mask_ready"], 1)
                    for u in range(2):
                        n = 2 * i + u
                        pool.wait_ge(w_in, 16)
                        pool.wait_ge(s["s_ready"], 3 * n + 3)
                        settle(pool, env["passed"])
                        pool.partition_all_reduce(c[u][:, :, :].rearrange("p b h -> p (b h)"), s2[u][:, :, :].rearrange("p b h -> p (b h)"),
                                                  P, RMAX).then_inc(s["c_ready"], 1)

            @block.tensor
            def _(pe):
                prime(pe, s["pv"])
                pe.wait_ge(w_in, 16)
                pe.matmul(psum[:, 0, 0:2 * H], w("w2T"), w("adiag"), start=True, stop=True).then_inc(s["ws_psum"], 1)
                pe.wait_ge(s["ws_ready"], 2)
                with pe.Fori(0, NI) as i:
                    for u in range(2):
                        n = 2 * i + u
                        pe.wait_ge(s["ln_ready"], n + 1)
                        pe.wait_ge(s["y2_ready"], primed(2 * G * i))
                        for b in range(G):
                            m = pe.transpose(graphs(u, 0)[:, b, :], hN[u][:, b, :], ident)
                        m.then_inc(s["hT_psum"], 1)
                    for u in range(2):
                        n = 2 * i + u
                        pe.wait_ge(s["hT_ready"], n + 1)
                        for b in range(G):
                            pe.matmul(psum[:, 4 * u + 2, 2 * H * b:2 * H * (b + 1)], hT[u][:, b * P:(b + 1) * P], ws[:, :], start=True, stop=True)
                        for b in range(G):
                            m = pe.matmul(graphs(u, 1)[:, b, :], hT[u][:, b * P:(b + 1) * P], w("w2"), start=True, stop=True)
                        m.then_inc(s["proj"], 1)
                    for u in range(2):
                        n = 2 * i + u
                        pe.wait_ge(s["parts_ready"], n + 1)
                        for b in range(G):
                            m = pe.transpose(psum[:, 4 * u + 3, :].bitcast(BF16)[0:PARTS * H, b * P:(b + 1) * P], parts[u][:, b, :], identb[:, :])
                        m.then_inc(s["rows_psum"], 1)

                    def z_scores(u, b):
                        n = 2 * i + u
                        if b == 0:
                            pe.wait_ge(s["rows_ready"], n + 1)
                            pe.wait_ge(s["mask_ready"], primed(2 * n + 2))
                        else:
                            pe.wait_ge(s["g_ready"], 2 * G * i + 2 * (b - 1) + u + 1)
                        for k in range(2):
                            for h in range(4):
                                pe.matmul(graphs(u, 2 + k)[:, h, :], selb[:, 4 * k + h, :], rows[u][:, b, :],
                                          start=(h == 0), stop=False, skip_group_check=True)
                            m = pe.matmul(bank(u, 2 + k), identb[:, :], bcast(maskT[u][:, b, :], 1, 4),
                                          start=False, stop=True, skip_group_check=True)
                        m.then_inc(s["z_psum"], 1)

                    def products(u, b):
                        n = 2 * i + u
                        pe.wait_ge(s["g_ready"], 2 * G * i + 2 * b + u + 1)
                        pe.wait_ge(s["r_ready"], n + 1)
                        if b >= 2:
                            pe.wait_ge(s["y2_ready"], primed(2 * G * i + 2 * (b - 2) + u + 1))
                        o = psum[:, 4 * u + b % 2, 0:2 * H * HV].rearrange("p (h d) -> p h d", h=H)
                        pe.matmul(o[:, :, HV:2 * HV], MT[u][:, b, :], R2[u][:, b, :, :], start=True, stop=False, skip_group_check=True)
                        for h in range(H):
                            m = pe.matmul(o[:, h, :], Gm[u][:, h, :], R[u][:, b, h, :], start=False, stop=(h == H - 1), skip_group_check=True)
                        m.then_inc(s["pv"], 1)

                    z_scores(0, 0)
                    for b in range(G):
                        for u in range(2):
                            if u == 0:
                                z_scores(1, b)
                            elif b + 1 < G:
                                z_scores(0, b + 1)
                            products(u, b)

            @block.scalar
            def _(act):
                act.activation(rstd[:, :], var[:, :], ACT.Sqrt, bias=env["epsc"][:, :]).then_inc(s["sd_ready"], 1)
                act.activation(env["scratch"][:, :], env["epsc"][:, :], ACT.Exp)
                with act.Fori(0, NI) as i:
                    for u in range(2):
                        n = 2 * i + u
                        act.wait_ge(s["hT_psum"], n + 1)
                        act.activation(hT[u][:, :], bank(u, 0), ACT.Relu).then_inc(s["hT_ready"], 1)
                    for u in range(2):
                        n = 2 * i + u
                        act.wait_ge(s["rows_psum"], n + 1)
                        act.activation(rows[u][:, :, :].rearrange("p b n -> p (b n)"), psum[:, 4 * u + 3, :].bitcast(BF16)[0:PARTS * H, 0:G * P],
                                       ACT.Copy).then_inc(s["rows_ready"], 1)
                        act.wait_ge(s["d_ready"], n + 1)
                        act.wait_ge(s["pv"], primed(2 * G * i))
                        act.activation(R[u][:, :, :, HD], d[u][:, :, :], ACT.Exp).then_inc(s["v_ready"], 1)
                        act.activation(R2[u][:, :, :, HD], d[u][:, :, :], ACT.Exp, scale=SLOPE).then_inc(s["v_ready"], 1)
                        act.wait_ge(s["tm_ready"], 2 * n + 2)
                        act.activation(up[u][:, :, :], tm[u][:, :, :], ACT.Exp).then_inc(s["u_ready"], 1)
                        act.activation(upp[u][:, :, :], tm2[u][:, :, :], ACT.Exp).then_inc(s["u_ready"], 1)
                    for u in range(2):
                        n = 2 * i + u
                        act.wait_ge(s["vv_ready"], 2 * n + 2)
                        act.activation(R[u][:, :, :, HV:2 * HV], R2[u][:, :, :, :], ACT.Copy, scale=-1.0).then_inc(s["r_ready"], 1)

            @block.vector
            def _(dve):
                prime(dve, s["y2_ready"])
                dve.wait_ge(s["sd_ready"], 1)
                dve.reciprocal(rstd[:, :], rstd[:, :]).then_inc(s["rs_ready"], 1)
                dve.wait_ge(s["ws_psum"], 1)
                dve.tensor_copy(ws[:, :], psum[:, 0, 0:2 * H]).then_inc(s["ws_ready"], 1)
                dve.wait_ge(w_in, 16)
                dve.tensor_copy(selb[:, :, :], w("sel")[0:PARTS * H, :].rearrange("p (h n) -> p h n", h=H)).then_inc(s["ws_ready"], 1)
                dve.wait_ge(s["rs_ready"], 1)
                with dve.Fori(0, NI) as i:
                    for u in range(2):
                        n = 2 * i + u
                        for b in range(G):
                            g = n * G + b
                            m = dve.tensor_scalar(hN[u][:, b, :], X[:, bass.ds(g, 1), :], mean[:, bass.ds(g, 1)], rstd[:, bass.ds(g, 1)],
                                                  ALU.subtract, ALU.mult)
                        m.then_inc(s["ln_ready"], 1)
                    for u in range(2):
                        n = 2 * i + u
                        dve.wait_ge(s["proj"], n + 1)
                        sp_ = psum[:, 4 * u + 2, 0:2 * H * G].rearrange("p (b k) -> p b k", b=G)
                        dve.tensor_copy(s2[u][:, :, :], sp_[:, :, H:2 * H]).then_inc(s["s_ready"], 1)
                        dve.tensor_scalar(ns2[u][:, :, :], sp_[:, :, H:2 * H], -1.0, None, ALU.mult).then_inc(s["s_ready"], 1)
                        dve.tensor_tensor(s1[u][:, :, :], sp_[:, :, 0:H], bcast(w("emb"), 1, G), ALU.add).then_inc(s["s_ready"], 1)
                        dve.wait_ge(s["s_ready"], 3 * n + 3)
                        dve.tensor_copy(parts[u][:, :, 0:H], s1[u][:, :, :]).then_inc(s["hi_ready"], 1)
                        dve.wait_ge(s["hi_ready"], n + 1)
                        dve.tensor_tensor(rem1[u][:, :, :], s1[u][:, :, :], parts[u][:, :, 0:H], ALU.subtract).then_inc(s["rem1_ready"], 1)
                        dve.wait_ge(s["rem1_ready"], n + 1)
                        dve.tensor_copy(parts[u][:, :, H:2 * H], rem1[u][:, :, :]).then_inc(s["mid_ready"], 1)
                        dve.wait_ge(s["mid_ready"], n + 1)
                        dve.tensor_tensor(parts[u][:, :, 2 * H:3 * H], rem1[u][:, :, :], parts[u][:, :, H:2 * H], ALU.subtract).then_inc(s["parts_ready"], 1)
                    for u in range(2):
                        n = 2 * i + u
                        dve.wait_ge(s["c_ready"], n + 1)
                        dve.tensor_tensor(d[u][:, :, :], s2[u][:, :, :], c[u][:, :, :], ALU.subtract).then_inc(s["d_ready"], 1)
                        dve.tensor_tensor(t[u][:, :, :], s1[u][:, :, :], c[u][:, :, :], ALU.add).then_inc(s["t_ready"], 1)
                        dve.wait_ge(s["t_ready"], n + 1)
                        dve.scalar_tensor_tensor(out=m02[u][:, :, :], in0=t[u][:, :, :], scalar=SLOPE, in1=t[u][:, :, :],
                                                 op0=ALU.mult, op1=ALU.max).then_inc(s["m_ready"], 1)
                        dve.wait_ge(s["m_ready"], n + 1)
                        dve.tensor_tensor(tm[u][:, :, :], t[u][:, :, :], m02[u][:, :, :], ALU.subtract).then_inc(s["tm_ready"], 1)
                        dve.scalar_tensor_tensor(out=tm2[u][:, :, :], in0=t[u][:, :, :], scalar=SLOPE, in1=m02[u][:, :, :],
                                                 op0=ALU.mult, op1=ALU.subtract).then_inc(s["tm_ready"], 1)

                    def values(u):
                        n = 2 * i + u
                        dve.wait_ge(s["v_ready"], 2 * n + 2)
                        V = graphs(u, 1).rearrange("p b (h d) -> p (b h) d", h=H)
                        for r, k in ((R, 2 * HV), (R2, HV)):
                            rr = r[u][:, :, :, :].rearrange("p b h d -> p (b h) d")
                            dve.tensor_tensor(rr[:, :, 0:HD], V, rr[:, :, HD:HD + 1].broadcast_to([P, G * H, HD]), ALU.mult).then_inc(s["vv_ready"], 1)

                    def edges(u, b):
                        n = 2 * i + u
                        dve.wait_ge(s["z_psum"], 2 * G * i + 2 * b + u + 1)
                        dve.wait_ge(s["pv"], primed(2 * G * i + (2 * b - 1 + u if b else 0)))
                        dve.tensor_tensor(Gm[u][:, :, :], psum[:, 4 * u + 2:4 * u + 4, :].rearrange("p k (h n) -> p (k h) n", h=4),
                                          bcast(ns2[u][:, b, :], 2, P), ALU.is_gt).then_inc(s["g_ready"], 1)

                    def outputs(u, b):
                        k = (2 * i) * G + 2 * b + u
                        g = (2 * i + u) * G + b
                        dve.wait_ge(s["pv"], primed(k + 1))
                        o = psum[:, 4 * u + b % 2, 0:2 * H * HV].rearrange("p (h d) -> p h d", h=H)
                        dve.tensor_tensor(y1[u][:, :, :], o[:, :, 0:HV], bcast(up[u][:, b, :], 2, HV), ALU.mult).then_inc(s["y1_ready"], 1)
                        dve.tensor_tensor(y2[u][:, :, :], o[:, :, HV:2 * HV], bcast(upp[u][:, b, :], 2, HV), ALU.mult).then_inc(s["y2_ready"], 1)
                        dve.wait_ge(s["y2_ready"], primed(k + 1))
                        dve.tensor_tensor(y1[u][:, :, :], y1[u][:, :, :], y2[u][:, :, :], ALU.add).then_inc(s["yy_ready"], 1)
                        dve.wait_ge(s["yy_ready"], k + 1)
                        dve.reciprocal(rden[u][:, :], y1[u][:, :, HD]).then_inc(s["rden_ready"], 1)
                        dve.wait_ge(s["rden_ready"], k + 1)
                        yg = Y[:, bass.ds(g, 1), :].rearrange("p b (h d) -> p (b h) d", h=H)
                        dve.tensor_tensor(yg, y1[u][:, :, 0:HD], bcast(rden[u][:, :], 2, HD), ALU.mult).then_inc(s["st_ready"], 1)

                    dve.wait_ge(s["u_ready"], 2 * (2 * i) + 4)
                    values(0)
                    edges(0, 0)
                    values(1)
                    for b in range(G):
                        for u in range(2):
                            if u == 0:
                                edges(1, b)
                            elif b + 1 < G:
                                edges(0, b + 1)
                            outputs(u, b)
                    dve.wait_ge(w_in, 16)
                    dve.wait_ge(s["st_ready"], 2 * G * (i + 1))
                    for u in range(2):
                        k = 2 * i + u
                        settle(dve, env["passed"])
                        for b in range(G):
                            m = dve.bn_stats(stats[:, b, :], Y[:, bass.ds((2 * i + u) * G + b, 1), :])
                        m.then_inc(s["mv_ready"], 1)
                        dve.wait_ge(w_in, 16)
                        dve.wait_ge(s["mv_ready"], 2 * k + 1)
                        settle(dve, env["passed"])
                        for b in range(G):
                            m = dve.bn_aggr(meanvar[:, b, :], stats[:, b, :])
                        m.then_inc(s["mv_ready"], 1)
                        dve.wait_ge(w_in, 16)
                        dve.wait_ge(s["mv_ready"], 2 * k + 2)
                        dve.tensor_copy(ymean[:, bass.ds((2 * i + u) * G, G)], meanvar[:, :, 0])
                        dve.tensor_copy(yvar[:, bass.ds((2 * i + u) * G, G)], meanvar[:, :, 1]).then_inc(s["stat_ready"], 1)
                        dve.wait_ge(s["stat_ready"], k + 1)

        yn, pos, neg = sb("yn", [P, G, P]), sb("pos", [P, G, P]), sb("neg", [P, G, P])
        names2 = ("ysd", "yrs", "yn_ready", "gamma_done", "beta_done", "neg_ready", "pos_ready", "exp_ready", "elu_ready",
                  "x_ready", "st2_ready", "mv2_ready", "stat2_ready")
        s2_ = {n: sem(n) for n in names2}
        NG2 = GRAPHS // (2 * G)
        with nc.Block() as block:
            @block.scalar
            def _(act):
                act.activation(rstd[:, :], yvar[:, :], ACT.Sqrt, bias=env["epsc"][:, :]).then_inc(s2_["ysd"], 1)
                act.activation(env["scratch"][:, :], env["epsc"][:, :], ACT.Exp)
                with act.Fori(0, NG2) as i:
                    for u in range(2):
                        act.wait_ge(s2_["neg_ready"], 2 * i + u + 1)
                        act.activation(neg[u][:, :, :], neg[u][:, :, :], ACT.Exp).then_inc(s2_["exp_ready"], 1)

            @block.gpsimd
            def _(pool):
                with pool.Fori(0, NG2) as i:
                    for u in range(2):
                        n = 2 * i + u
                        pool.wait_ge(s2_["yn_ready"], n + 1)
                        pool.tensor_tensor(yn[u][:, :, :], yn[u][:, :, :], bcast(w("gamma"), 1, G), ALU.mult).then_inc(s2_["gamma_done"], 1)
                        pool.wait_ge(s2_["gamma_done"], n + 1)
                        pool.tensor_tensor(yn[u][:, :, :], yn[u][:, :, :], bcast(w("beta"), 1, G), ALU.add).then_inc(s2_["beta_done"], 1)

            @block.vector
            def _(dve):
                prime(dve, s2_["x_ready"])
                dve.wait_ge(s2_["ysd"], 1)
                dve.reciprocal(rstd[:, :], rstd[:, :]).then_inc(s2_["yrs"], 1)
                dve.wait_ge(s2_["yrs"], 1)
                with dve.Fori(0, NG2) as i:
                    for u in range(2):
                        n = 2 * i + u
                        for b in range(G):
                            g = n * G + b
                            m = dve.tensor_scalar(yn[u][:, b, :], Y[:, bass.ds(g, 1), :], ymean[:, bass.ds(g, 1)], rstd[:, bass.ds(g, 1)],
                                                  ALU.subtract, ALU.mult)
                        m.then_inc(s2_["yn_ready"], 1)
                    for u in range(2):
                        n = 2 * i + u
                        dve.wait_ge(s2_["beta_done"], n + 1)
                        dve.tensor_scalar(neg[u][:, :, :], yn[u][:, :, :], 0.0, None, ALU.min).then_inc(s2_["neg_ready"], 1)
                        dve.tensor_scalar(pos[u][:, :, :], yn[u][:, :, :], 0.0, None, ALU.max).then_inc(s2_["pos_ready"], 1)
                    for u in range(2):
                        n = 2 * i + u
                        dve.wait_ge(s2_["exp_ready"], n + 1)
                        dve.wait_ge(s2_["pos_ready"], n + 1)
                        dve.scalar_tensor_tensor(out=pos[u][:, :, :], in0=neg[u][:, :, :], scalar=-1.0, in1=pos[u][:, :, :],
                                                 op0=ALU.add, op1=ALU.add).then_inc(s2_["elu_ready"], 1)
                        dve.wait_ge(s2_["elu_ready"], n + 1)
                        residual(env, dve, n * G, G, pos[u][:, :, :], n, s2_["x_ready"], s2_["st2_ready"], s2_["mv2_ready"], s2_["stat2_ready"])


def gated_layer(env):
    nc, X, w, ident, psum = (env[k] for k in ("nc", "X", "w", "ident", "psum"))
    mean, var, rstd = (env[k] for k in ("mean", "var", "rstd"))
    NI = GRAPHS // (2 * G)
    with ExitStack() as ctx:
        def one(name, shape, dt=F32):
            return ctx.enter_context(nc.sbuf_tensor("g_" + name, shape, dt))

        def sb(name, shape, dt=F32):
            return [one(f"{name}{u}", shape, dt) for u in range(2)]

        wg = one("wg", [P, STEPS, 3, P])
        brz = one("brz", [P, 2])
        adj_i, A = sb("adj_i", [P, G, P], I32), sb("A", [P, G, P])
        h, hT, aT = sb("h", [P, G, P]), sb("hT", [P, G * P]), sb("aT", [P, G * P])
        r, z, nn, tt = (sb(n, [P, G * P]) for n in ("r", "z", "n", "t"))
        o = sb("o", [P, G, P])

        def sem(name):
            return ctx.enter_context(nc.semaphore("g_" + name))

        adj_in = [sem("adj_in0"), sem("adj_in1")]
        stored = [sem("stored0"), sem("stored1")]
        names = ("a_ready", "sd", "rs", "wg_psum", "wg_ready", "ln_ready", "h_ready", "hT_psum", "hT_ready", "agg", "agg_ready",
                 "rz_psum", "n_psum", "r_ready", "z_ready", "rh_ready", "t_ready", "n_ready", "d_ready", "dz_ready", "new_ready",
                 "hN_psum", "hN_ready", "out_ready")
        s = {n: sem(n) for n in names}
        w_in = env["w_in"]

        def bank(u, k):
            return psum[:, 4 * u + k, :]

        def graphs(u, k):
            return psum[:, 4 * u + k, :].rearrange("p (b n) -> p b n", b=G)

        with nc.Block() as block:
            @block.sync
            def _(sp):
                prime(sp, *stored)
                with sp.Fori(0, NI) as i:
                    for u in range(2):
                        sp.wait_ge(s["a_ready"], primed(2 * i))
                        sp.dma_start(adj_i[u][:, :, :], env["adj"][:, bass.ds((2 * i + u) * G, G), :]).then_inc(adj_in[u], 16)
                    for u in range(2):
                        n = 2 * i + u
                        sp.wait_ge(s["out_ready"], primed(n + 1))
                        sp.dma_start(env["out"][:, bass.ds(n * G, G), :], o[u][:, :, :]).then_inc(stored[u], 16)
                for u in range(2):
                    sp.wait_ge(stored[u], primed(16 * NI))

            @block.gpsimd
            def _(pool):
                prime(pool, s["a_ready"])
                with pool.Fori(0, NI) as i:
                    for u in range(2):
                        pool.wait_ge(w_in, 16)
                        pool.wait_ge(s["hN_psum"], primed(2 * STEPS * i))
                        pool.wait_ge(adj_in[u], 16 * i + 16)
                        settle(pool, env["passed"])
                        pool.tensor_scalar(A[u][:, :, :], adj_i[u][:, :, :], 1.0, 0.0, ALU.min, ALU.max).then_inc(s["a_ready"], 1)

            @block.tensor
            def _(pe):
                prime(pe, s["hN_psum"])
                pe.wait_ge(w_in, 16)
                for k in range(STEPS):
                    pe.matmul(psum[:, k, 0:3 * P], w("gwT")[:, k * P:(k + 1) * P], w("wih"), start=True, stop=True).then_inc(s["wg_psum"], 1)
                pe.wait_ge(s["wg_ready"], STEPS)
                with pe.Fori(0, NI) as i:
                    for u in range(2):
                        n = 2 * i + u
                        pe.wait_ge(s["h_ready"], n + 1)
                        pe.wait_ge(s["out_ready"], primed(2 * i))
                        for b in range(G):
                            m = pe.transpose(graphs(u, 1)[:, b, :], h[u][:, b, :], ident)
                        m.then_inc(s["hT_psum"], 1)
                    for k in range(STEPS):
                        for u in range(2):
                            n = 2 * i + u
                            q = (2 * STEPS) * i + 2 * k + u
                            if k == 0:
                                pe.wait_ge(s["a_ready"], primed(n + 1))
                            else:
                                pe.wait_ge(s["hN_ready"], (2 * (STEPS - 1)) * i + 2 * (k - 1) + u + 1)
                            for b in range(G):
                                m = pe.matmul(graphs(u, 0)[:, b, :], h[u][:, b, :], A[u][:, b, :], start=True, stop=True)
                            m.then_inc(s["agg"], 1)
                        for u in range(2):
                            q = (2 * STEPS) * i + 2 * k + u
                            if k == 0:
                                pe.wait_ge(s["hT_ready"], 2 * i + u + 1)
                            pe.matmul(bank(u, 1), w("whh")[:, 0:P], hT[u][:, :], start=True, stop=False)
                            pe.matmul(bank(u, 2), w("whh")[:, P:2 * P], hT[u][:, :], start=True, stop=False)
                            pe.wait_ge(s["agg_ready"], q + 1)
                            pe.matmul(bank(u, 1), wg[:, k, 0, :], aT[u][:, :], start=False, stop=True)
                            pe.matmul(bank(u, 2), wg[:, k, 1, :], aT[u][:, :], start=False, stop=True).then_inc(s["rz_psum"], 1)
                            pe.matmul(bank(u, 0), w("whh")[:, 2 * P:3 * P], hT[u][:, :], start=True, stop=True)
                            pe.matmul(bank(u, 3), wg[:, k, 2, :], aT[u][:, :], start=True, stop=True).then_inc(s["n_psum"], 1)
                        for u in range(2):
                            q = (2 * STEPS) * i + 2 * k + u
                            pe.wait_ge(s["new_ready"], q + 1)
                            for b in range(G):
                                m = pe.transpose(graphs(u, 1)[:, b, :], hT[u][:, b * P:(b + 1) * P], ident)
                            m.then_inc(s["hN_psum"], 1)

            @block.scalar
            def _(act):
                act.activation(rstd[:, :], var[:, :], ACT.Sqrt, bias=env["epsc"][:, :]).then_inc(s["sd"], 1)
                act.activation(env["scratch"][:, :], env["epsc"][:, :], ACT.Sigmoid)
                with act.Fori(0, NI) as i:
                    for u in range(2):
                        n = 2 * i + u
                        act.wait_ge(s["ln_ready"], n + 1)
                        act.activation(h[u][:, :, :], h[u][:, :, :], ACT.Relu).then_inc(s["h_ready"], 1)
                    for u in range(2):
                        n = 2 * i + u
                        act.wait_ge(s["hT_psum"], n + 1)
                        act.activation(hT[u][:, :], bank(u, 1), ACT.Copy).then_inc(s["hT_ready"], 1)
                    for k in range(STEPS):
                        for u in range(2):
                            q = (2 * STEPS) * i + 2 * k + u
                            act.wait_ge(s["agg"], q + 1)
                            act.activation(aT[u][:, :], bank(u, 0), ACT.Copy).then_inc(s["agg_ready"], 1)
                        for u in range(2):
                            q = (2 * STEPS) * i + 2 * k + u
                            act.wait_ge(s["rz_psum"], q + 1)
                            act.activation(r[u][:, :], bank(u, 1), ACT.Sigmoid, bias=brz[:, 0:1]).then_inc(s["r_ready"], 1)
                            act.activation(z[u][:, :], bank(u, 2), ACT.Sigmoid, bias=brz[:, 1:2]).then_inc(s["z_ready"], 1)
                            act.wait_ge(s["t_ready"], q + 1)
                            act.activation(nn[u][:, :], tt[u][:, :], ACT.Tanh, bias=w("bih")[:, 2:3]).then_inc(s["n_ready"], 1)
                        if k < STEPS - 1:
                            for u in range(2):
                                q = (2 * STEPS) * i + 2 * k + u
                                act.wait_ge(s["hN_psum"], primed(q + 1))
                                act.activation(h[u][:, :, :], graphs(u, 1), ACT.Copy).then_inc(s["hN_ready"], 1)

            @block.vector
            def _(dve):
                prime(dve, s["out_ready"])
                dve.wait_ge(s["sd"], 1)
                dve.reciprocal(rstd[:, :], rstd[:, :]).then_inc(s["rs"], 1)
                for k in range(STEPS):
                    dve.wait_ge(s["wg_psum"], k + 1)
                    dve.tensor_copy(wg[:, k, :, :].rearrange("p g n -> p (g n)"), psum[:, k, 0:3 * P]).then_inc(s["wg_ready"], 1)
                dve.tensor_tensor(brz[:, :], w("bih")[:, 0:2], w("bhh")[:, 0:2], ALU.add).then_inc(s["rs"], 1)
                dve.wait_ge(s["rs"], 2)
                with dve.Fori(0, NI) as i:
                    for u in range(2):
                        n = 2 * i + u
                        dve.wait_ge(s["hN_psum"], primed(2 * STEPS * i))
                        for b in range(G):
                            g = n * G + b
                            m = dve.tensor_scalar(h[u][:, b, :], X[:, bass.ds(g, 1), :], mean[:, bass.ds(g, 1)], rstd[:, bass.ds(g, 1)],
                                                  ALU.subtract, ALU.mult)
                        m.then_inc(s["ln_ready"], 1)
                    for k in range(STEPS):
                        for u in range(2):
                            q = (2 * STEPS) * i + 2 * k + u
                            dve.wait_ge(s["n_psum"], q + 1)
                            dve.wait_ge(s["r_ready"], q + 1)
                            dve.scalar_tensor_tensor(out=tt[u][:, :], in0=bank(u, 0), scalar=w("bhh")[:, 2:3], in1=r[u][:, :],
                                                     op0=ALU.add, op1=ALU.mult).then_inc(s["rh_ready"], 1)
                            dve.wait_ge(s["rh_ready"], q + 1)
                            dve.tensor_tensor(tt[u][:, :], tt[u][:, :], bank(u, 3), ALU.add).then_inc(s["t_ready"], 1)
                        for u in range(2):
                            q = (2 * STEPS) * i + 2 * k + u
                            dve.wait_ge(s["n_ready"], q + 1)
                            dve.tensor_tensor(r[u][:, :], hT[u][:, :], nn[u][:, :], ALU.subtract).then_inc(s["d_ready"], 1)
                            dve.wait_ge(s["d_ready"], q + 1)
                            dve.tensor_tensor(r[u][:, :], r[u][:, :], z[u][:, :], ALU.mult).then_inc(s["dz_ready"], 1)
                            dve.wait_ge(s["dz_ready"], q + 1)
                            dve.tensor_tensor(hT[u][:, :], r[u][:, :], nn[u][:, :], ALU.add).then_inc(s["new_ready"], 1)
                    for u in range(2):
                        n = 2 * i + u
                        dve.wait_ge(s["hN_psum"], primed(2 * STEPS * i + 2 * (STEPS - 1) + u + 1))
                        dve.wait_ge(stored[u], primed(16 * i))
                        dve.tensor_tensor(o[u][:, :, :], graphs(u, 1), X[:, bass.ds(n * G, G), :], ALU.add).then_inc(s["out_ready"], 1)


def _pack(a):
    import numpy as np
    f = np.float32

    def head_rows(m):
        t = np.zeros((QG, RT, RW) + m.shape[1:], f)
        t[:, :, :HD] = m.reshape((QG, RT, HD) + m.shape[1:])
        return t.reshape((QG, P) + m.shape[1:])

    def rows(v):
        return np.broadcast_to(v, (P, v.shape[-1]))

    a1, a2 = a["L1_gnn_a"][:P], a["L1_gnn_a"][P:]
    adiag = np.zeros((P, 2 * H), f)
    sel = np.zeros((P, H, P), f)
    for h in range(H):
        adiag[h * HD:(h + 1) * HD, h] = a["L2_gnn_a1"]
        adiag[h * HD:(h + 1) * HD, H + h] = a["L2_gnn_a2"]
        sel[h::H, h, :] = 1.0
    bk = head_rows(a["L0_gnn_bk"])
    bk.reshape(QG, RT, RW)[:, :, SHIFT] = 1.0
    parts = {
        "wq": head_rows(a["L0_gnn_Wq"]).reshape(QG * P, P).T, "wk": head_rows(a["L0_gnn_Wk"]).reshape(QG * P, P).T,
        "wv": a["L0_gnn_Wv"].T, "wo": a["L0_gnn_Wo"].T,
        "w1": a["L1_gnn_W"], "a1rep": np.broadcast_to(a1, (P, P)), "a2col": a2, "han": a["L1_gnn_han_w"],
        "w2": a["L2_gnn_W"], "w2T": a["L2_gnn_W"].T, "adiag": adiag, "emb": rows(a["L2_gnn_edge_emb"][1]),
        "gwT": a["L3_gnn_weight"].transpose(2, 0, 1).reshape(P, STEPS * P),
        "wih": a["L3_gnn_w_ih"].T, "whh": a["L3_gnn_w_hh"].T,
        "bq": head_rows(a["L0_gnn_bq"]).T, "bk": bk.T,
        "bih": a["L3_gnn_b_ih"].reshape(3, P).T, "bhh": a["L3_gnn_b_hh"].reshape(3, P).T,
        "bv": rows(a["L0_gnn_bv"]), "bo": rows(a["L0_gnn_bo"]), "hanb": rows(a["L1_gnn_han_b"]),
        "gamma": rows(a["L2_gnn_ln_gamma"]), "beta": rows(a["L2_gnn_ln_beta"]),
        "ident": np.eye(P, dtype=f), "sel": sel.reshape(P, H * P),
    }
    return np.ascontiguousarray(np.concatenate([parts[n] for n, _ in WEIGHTS], axis=1))


def _arrays(inputs):
    import numpy as np
    a = {k: np.asarray(v) for k, v in inputs.items()}
    return {
        "x": np.ascontiguousarray(a["x"].transpose(1, 0, 2)),
        "adj": np.ascontiguousarray(a["adj"].transpose(1, 0, 2)),
        "adjT": np.ascontiguousarray(a["adj"].transpose(2, 0, 1)),
        "wpack": _pack(a),
    }


def kernel(**inputs):
    import concourse.bacc as bacc
    import numpy as np
    from concourse.bass_utils import run_bass_kernel_spmd

    nc = bacc.Bacc("TRN2", target_bir_lowering=False, num_devices=1)
    arrays = _arrays(inputs)
    args = [nc.dram_tensor(n, v.shape, mybir.dt.from_np(v.dtype), kind="ExternalInput").ap() for n, v in arrays.items()]
    out = nc.dram_tensor("out", (P, GRAPHS, P), F32, kind="ExternalOutput").ap()
    graph_layers(nc, *args, out)
    got = run_bass_kernel_spmd(nc, [arrays], core_ids=[0]).results[0]["out"]
    return np.ascontiguousarray(np.asarray(got).transpose(1, 0, 2))
```

```python
from contextlib import ExitStack

import concourse.bass as bass
from concourse import mybir

F32 = mybir.dt.float32
BF16 = mybir.dt.bfloat16
I32 = mybir.dt.int32
ALU = mybir.AluOpType
ACT = mybir.ActivationFunctionType
AX = mybir.AxisListType
RMAX = bass.bass_isa.ReduceOp.max

P = 128
GRAPHS = 64
G = 4
H = 8
HD = 16
HV = HD + 1
BIG = 1e30
BIG1 = 9e15
STEPS = 3
EPS = 1e-5
SLOPE = 0.2

WEIGHTS = [("wq", P), ("wk", P), ("wv", P), ("wo", P),
           ("w1", P), ("a1rep", P), ("a2col", 1), ("han", P),
           ("w2", P), ("w2T", P), ("adiag", 2 * H), ("emb", H),
           ("gwT", STEPS * P), ("wih", 3 * P), ("whh", 3 * P),
           ("bq", 1), ("bk", 1), ("bih", 3), ("bhh", 3),
           ("bv", P), ("bo", P), ("hanb", P), ("gamma", P), ("beta", P),
           ("ident", P), ("sel", H * P)]
OFFSET = {}
_at = 0
for _name, _n in WEIGHTS:
    OFFSET[_name] = (_at, _n)
    _at += _n
NW = _at


def bcast(ap, axis, n):
    a = ap.unsqueeze(axis)
    shape = list(a.shape)
    shape[axis] = n
    return a.broadcast_to(shape)


def primed(n):
    return n + 1


def prime(eng, *sems):
    for s in sems:
        eng.sem_inc(s, 1)


def settle(eng, passed):
    eng.sem_inc(passed, 1)


def graph_layers(nc, x, adj, adjT, wpack, out, layers=4):
    with ExitStack() as ctx:
        def sb(name, shape, dt=F32):
            return ctx.enter_context(nc.sbuf_tensor(name, shape, dt))

        def sem(name):
            return ctx.enter_context(nc.semaphore(name))

        X = sb("X", [P, GRAPHS, P])
        W = sb("W", [P, NW])
        stats = sb("stats", [P, G, 6])
        meanvar = sb("meanvar", [P, G, 2])
        mean = sb("mean", [P, GRAPHS])
        var = sb("var", [P, GRAPHS])
        rstd = sb("rstd", [P, GRAPHS])
        shift = sb("shift", [P, GRAPHS])
        epsc = sb("epsc", [P, 1])
        scratch = sb("scratch", [P, 1])
        identb = sb("identb", [P, P], BF16)
        psum = ctx.enter_context(nc.psum_tensor("psum", [P, 8, 512], F32))

        def w(name):
            a, n = OFFSET[name]
            return W[:, a:a + n]

        ident = w("ident")

        io = (nc, x, adj, adjT, wpack, out)
        env = dict(nc=nc, x=x, adj=adj, adjT=adjT, wpack=wpack, out=out, X=X, W=W, w=w, ident=ident,
                   identb=identb, stats=stats, meanvar=meanvar, mean=mean, var=var, rstd=rstd, shift=shift, epsc=epsc,
                   psum=psum, scratch=scratch, sb=sb, sem=sem)
        load(env)
        if layers > 0:
            attention_layer(env)
        if layers > 1:
            column_layer(env)
        if layers > 2:
            edge_layer(env)
        if layers > 3:
            gated_layer(env)
        else:
            store(env)


def load(env):
    nc, x, X, W, sem = (env[k] for k in ("nc", "x", "X", "W", "sem"))
    stats, meanvar, mean, var = (env[k] for k in ("stats", "meanvar", "mean", "var"))
    NL = GRAPHS // G
    x_in, w_in = sem("x_in"), sem("w_in")
    x_stats, x_mv, x_saved = sem("x_stats"), sem("x_mv"), sem("x_saved")
    const = sem("const")
    env["w_in"] = w_in
    env["passed"] = sem("passed")
    with nc.Block() as block:
        @block.sync
        def _(sp):
            with sp.Fori(0, NL) as i:
                sp.dma_start(X[:, bass.ds(i * G, G), :], x[:, bass.ds(i * G, G), :]).then_inc(x_in, 16)

        @block.scalar
        def _(act):
            act.dma_start(W[:, :], env["wpack"]).then_inc(w_in, 16)
            act.wait_ge(w_in, 16)

        @block.vector
        def _(dve):
            prime(dve, x_mv, x_saved)
            dve.memset(env["epsc"][:, :], EPS).then_inc(const, 1)
            dve.wait_ge(w_in, 16)
            dve.tensor_copy(env["identb"][:, :], env["ident"]).then_inc(const, 1)
            dve.wait_ge(const, 2)
            dve.wait_ge(x_in, 16 * NL)
            with dve.Fori(0, NL) as i:
                dve.wait_ge(w_in, 16)
                dve.wait_ge(x_mv, primed(i * G))
                settle(dve, env["passed"])
                for b in range(G):
                    dve.bn_stats(stats[:, b, :], X[:, bass.ds(i * G + b, 1), :]).then_inc(x_stats, 1)
                dve.wait_ge(w_in, 16)
                dve.wait_ge(x_stats, (i + 1) * G)
                dve.wait_ge(x_saved, primed(2 * i))
                settle(dve, env["passed"])
                for b in range(G):
                    dve.bn_aggr(meanvar[:, b, :], stats[:, b, :]).then_inc(x_mv, 1)
                dve.wait_ge(w_in, 16)
                dve.wait_ge(x_mv, primed((i + 1) * G))
                dve.tensor_copy(mean[:, bass.ds(i * G, G)], meanvar[:, :, 0]).then_inc(x_saved, 1)
                dve.tensor_copy(var[:, bass.ds(i * G, G)], meanvar[:, :, 1]).then_inc(x_saved, 1)
            dve.wait_ge(x_saved, primed(2 * NL))


def attention_layer(env):
    nc, X, w, ident, identb, psum = (env[k] for k in ("nc", "X", "w", "ident", "identb", "psum"))
    mean, var, rstd = (env[k] for k in ("mean", "var", "rstd"))
    NG = GRAPHS // G
    Q_PARTS = (0, 0, 1, 0, 2, 1)
    K_PARTS = (0, 1, 0, 2, 0, 1)
    TERMS = len(Q_PARTS)
    VS = 64
    VCOLS = (H - 1) * HV + VS
    with ExitStack() as ctx:
        def one(name, shape, dt=F32):
            return ctx.enter_context(nc.sbuf_tensor("a_" + name, shape, dt))

        def sb(name, shape, dt=F32):
            return [one(f"{name}{u}", shape, dt) for u in range(2)]

        adj_i, adjT_i = sb("adj_i", [P, G, P], I32), sb("adjT_i", [P, G, P], I32)
        maskN, maskT = sb("maskN", [P, G, P], BF16), sb("maskT", [P, G, P], BF16)
        selb = one("selb", [P, H, P], BF16)
        hN, hT = one("hN", [P, G, P]), one("hT", [P, G * P])
        qk = sb("qk", [P, G * P])
        rem = sb("rem", [P, G * P])
        parts = sb("parts", [P, 3, G * P], BF16)
        stack = [sb("stackq", [P, H, G * P], BF16), sb("stackk", [P, H, G * P], BF16)]
        V = sb("V", [P, G, VCOLS])
        negmax, mparts = sb("negmax", [P, H]), sb("mparts", [P, 2 * H], BF16)
        mT = sb("mT", [P, P], BF16)
        PT = sb("PT", [P, H, P])
        rden = sb("rden", [P, H])
        O, OT = sb("O", [P, P]), sb("OT", [P, P])

        names = ("clean", "sd", "rs", "sel_ready", "mask_ready", "ln_ready", "bias_added", "hT_psum", "hT_ready",
                 "q_psum", "k_psum", "v_psum", "qk_ready", "hi_ready", "rem_ready", "mid_ready", "lo_ready", "v_ready",
                 "scores", "max_ready", "mhi_ready", "mparts_ready", "mT_psum", "mT_ready", "scoresT", "exp_ready",
                 "pv", "rden_ready", "o_ready", "oT_psum", "oT_ready", "y_psum", "x_ready", "stat_step")
        s = {n: ctx.enter_context(nc.semaphore("a_" + n)) for n in names}
        adj_in = [ctx.enter_context(nc.semaphore(f"a_adj_in{u}")) for u in range(2)]
        stacked = [ctx.enter_context(nc.semaphore(f"a_stacked{u}")) for u in range(2)]
        w_in = env["w_in"]

        def each_group(eng, before, turn):
            before()
            turn(0, 0, True, False)
            with eng.Fori(0, NG // 2 - 1) as i:
                turn(2 * i + 1, 1, False, False)
                turn(2 * i + 2, 0, False, False)
            turn(NG - 1, 1, False, True)

        def slot(k):
            return psum[:, 2 * (k % 2):2 * (k % 2) + 2, :].rearrange("p a (h n) -> p (a h) n", h=H // 2)

        with nc.Block() as block:
            @block.sync
            def _(sp):
                def load_adj(g, par):
                    if not isinstance(g, int) or g >= 2:
                        sp.wait_ge(s["mask_ready"], primed(2 * (g - 1)))
                        settle(sp, env["passed"])
                    sp.dma_start(adj_i[par][:, :, :], env["adj"][:, bass.ds(g * G, G), :]).then_inc(adj_in[par], 16)
                    sp.dma_start(adjT_i[par][:, :, :], env["adjT"][:, bass.ds(g * G, G), :]).then_inc(adj_in[par], 16)

                def stack_parts(g, par):
                    if not isinstance(g, int) or g >= 2:
                        sp.wait_ge(s["scoresT"], primed(G * (g - 1)))
                        settle(sp, env["passed"])
                    for c, order in ((0, Q_PARTS), (1, K_PARTS)):
                        for t, part in sorted(enumerate(order), key=lambda tp: tp[1]):
                            ready = s[("hi_ready", "mid_ready", "lo_ready")[part]]
                            sp.wait_ge(ready, primed(2 * g + c + 1))
                            settle(sp, env["passed"])
                            sp.dma_start(stack[c][par][t * HD:(t + 1) * HD, :, :], parts[c][:, part, :]).then_inc(stacked[par], 16)

                def before():
                    prime(sp, *stacked)
                    load_adj(0, 0)
                    sp.wait_ge(s["clean"], 8)
                    stack_parts(0, 0)

                def turn(g, par, first, last):
                    if not last:
                        load_adj(g + 1, 1 - par)
                        stack_parts(g + 1, 1 - par)

                each_group(sp, before, turn)

            @block.gpsimd
            def _(pool):
                def masks(g, par):
                    if not isinstance(g, int) or g >= 2:
                        pool.wait_ge(s["scoresT"], primed(G * (g - 1)))
                    for k, (m, a) in enumerate(((maskN, adj_i), (maskT, adjT_i))):
                        if k == 0:
                            pool.wait_ge(adj_in[par], 16 * (g - par + 2))
                            settle(pool, env["passed"])
                        pool.tensor_scalar(m[par][:, :, :], a[par][:, :, :], BIG, -BIG, ALU.mult, ALU.add).then_inc(s["mask_ready"], 1)

                def last_parts(g):
                    for c in range(2):
                        pool.wait_ge(s["mid_ready"], primed(2 * g + c + 1))
                        pool.tensor_tensor(parts[c][:, 2, :], rem[c][:, :], parts[c][:, 1, :], ALU.subtract).then_inc(s["lo_ready"], 1)

                def add_bias(g):
                    pool.wait_ge(s["ln_ready"], g + 1)
                    xg = X[:, bass.ds(g * G, G), :]
                    pool.tensor_tensor(xg, xg, bcast(w("bo"), 1, G), ALU.add).then_inc(s["bias_added"], 1)

                def before():
                    prime(pool, s["mask_ready"], s["lo_ready"])
                    for c in range(2):
                        for par in range(2):
                            pool.memset(stack[c][par][:, :, :], 0.0).then_inc(s["clean"], 1)
                    for par in range(2):
                        pool.memset(V[par][:, :, :], 1.0).then_inc(s["clean"], 1)
                        pool.memset(mT[par][:, :], 0.0).then_inc(s["clean"], 1)
                    masks(0, 0)
                    last_parts(0)
                    add_bias(0)

                def turn(g, par, first, last):
                    if not last:
                        masks(g + 1, 1 - par)
                        add_bias(g + 1)
                        last_parts(g + 1)

                each_group(pool, before, turn)

            @block.tensor
            def _(pe):
                def project(g, par, item):
                    if item == 0:
                        pe.wait_ge(s["ln_ready"], g + 1)
                        if not isinstance(g, int) or g >= 1:
                            pe.wait_ge(s["qk_ready"], 2 * g)
                            pe.wait_ge(s["hi_ready"], primed(2 * g))
                        for b in range(G):
                            m = pe.transpose(psum[:, 4, b * P:(b + 1) * P], hN[:, b, :], ident)
                        m.then_inc(s["hT_psum"], 1)
                    elif item == 1:
                        pe.wait_ge(s["hT_ready"], g + 1)
                        if not isinstance(g, int) or g >= 1:
                            pe.wait_ge(s["v_ready"], g)
                        pe.matmul(psum[:, 5, :], w("wq"), hT[:, :], start=True, stop=True).then_inc(s["q_psum"], 1)
                    elif item == 2:
                        pe.matmul(psum[:, 4, :], w("wk"), hT[:, :], start=True, stop=True).then_inc(s["k_psum"], 1)
                    else:
                        pe.wait_ge(s["qk_ready"], 2 * g + 1)
                        pe.wait_ge(s["hi_ready"], primed(2 * g + 1))
                        for b in range(G):
                            m = pe.matmul(psum[:, 5, b * P:(b + 1) * P], hT[:, b * P:(b + 1) * P], w("wv"), start=True, stop=True)
                        m.then_inc(s["v_psum"], 1)

                def scores(g, par, k):
                    n = G * g + k
                    if k == 0:
                        pe.wait_ge(s["mask_ready"], primed(2 * g + 2))
                        pe.wait_ge(stacked[par], primed(16 * TERMS * (g - par + 2)))
                    if not (isinstance(g, int) and g == 0 and k < 2):
                        pe.wait_ge(s["o_ready"], n - 1)
                    for a in range(2):
                        for h in range(H // 2):
                            hh = a * (H // 2) + h
                            pe.matmul(slot(k)[:, hh, :], stack[0][par][:, hh, k * P:(k + 1) * P], stack[1][par][:, hh, k * P:(k + 1) * P],
                                      start=(h == 0), stop=False, skip_group_check=True)
                        m = pe.matmul(psum[:, 2 * (k % 2) + a, :], identb[:, :], bcast(maskN[par][:, k, :], 1, H // 2),
                                      start=False, stop=True, skip_group_check=True)
                    m.then_inc(s["scores"], 1)

                def shift_rows(g, par, k):
                    n = G * g + k
                    pe.wait_ge(s["mparts_ready"], n + 1)
                    pe.transpose(psum[:, 2 * (k % 2), :].bitcast(BF16)[0:2 * H, 0:P], mparts[k % 2][:, :], identb[:, :]).then_inc(s["mT_psum"], 1)

                def scores_transposed(g, par, k):
                    n = G * g + k
                    pe.wait_ge(s["mT_ready"], n + 1)
                    for a in range(2):
                        for h in range(H // 2):
                            hh = a * (H // 2) + h
                            pe.matmul(slot(k)[:, hh, :], stack[1][par][:, hh, k * P:(k + 1) * P], stack[0][par][:, hh, k * P:(k + 1) * P],
                                      start=(h == 0), stop=False, skip_group_check=True)
                            pe.matmul(slot(k)[:, hh, :], selb[:, hh, :], mT[k % 2][:, :], start=False, stop=False, skip_group_check=True)
                        m = pe.matmul(psum[:, 2 * (k % 2) + a, :], identb[:, :], bcast(maskT[par][:, k, :], 1, H // 2),
                                      start=False, stop=True, skip_group_check=True)
                    m.then_inc(s["scoresT"], 1)

                def weighted_values(g, par, k):
                    n = G * g + k
                    pe.wait_ge(s["exp_ready"], n + 1)
                    if k == 0:
                        pe.wait_ge(s["v_ready"], g + 1)
                    for h in range(H):
                        m = pe.matmul(psum[:, 2 * (k % 2), h * VS:(h + 1) * VS], PT[k % 2][:, h, :], V[par][:, k, h * HV:h * HV + VS], start=True, stop=True)
                    m.then_inc(s["pv"], 1)

                def transpose_output(g, par, k):
                    n = G * g + k
                    pe.wait_ge(s["o_ready"], n + 1)
                    pe.transpose(psum[:, 6, 0:P], O[k % 2][:, :], ident).then_inc(s["oT_psum"], 1)

                def output(g, par, k):
                    n = G * g + k
                    pe.wait_ge(s["oT_ready"], n + 1)
                    if not (isinstance(g, int) and g == 0 and k == 0):
                        pe.wait_ge(s["x_ready"], primed(n))
                    pe.matmul(psum[:, 7, 0:P], OT[k % 2][:, :], w("wo"), start=True, stop=True).then_inc(s["y_psum"], 1)

                def before():
                    prime(pe, s["scoresT"], s["pv"])
                    pe.wait_ge(s["sel_ready"], 1)
                    for item in range(4):
                        project(0, 0, item)

                def unit_before(g, par, k, back):
                    return (g, par, k - back) if k >= back else (g - 1, 1 - par, k - back + G)

                def turn(g, par, first, last):
                    for k in range(G):
                        scores(g, par, k)
                        if not first or k >= 2:
                            output(*unit_before(g, par, k, 2))
                        if not first or k >= 1:
                            weighted_values(*unit_before(g, par, k, 1))
                        shift_rows(g, par, k)
                        if not last:
                            for item in ((0,), (1, 2), (3,), ())[k]:
                                project(g + 1, 1 - par, item)
                        if not first or k >= 1:
                            transpose_output(*unit_before(g, par, k, 1))
                        scores_transposed(g, par, k)
                    if last:
                        output(g, par, G - 2)
                        weighted_values(g, par, G - 1)
                        transpose_output(g, par, G - 1)
                        output(g, par, G - 1)

                each_group(pe, before, turn)

            @block.scalar
            def _(act):
                def relu(g):
                    if not isinstance(g, int) or g >= 1:
                        act.wait_ge(s["v_psum"], g)
                    act.wait_ge(s["hT_psum"], g + 1)
                    act.activation(hT[:, :], psum[:, 4, :], ACT.Relu).then_inc(s["hT_ready"], 1)

                def evacuate(g, par, c):
                    if not isinstance(g, int) or g >= 1:
                        act.wait_ge(s["rem_ready"], 2 * (g - 1) + c + 1)
                        act.wait_ge(stacked[1 - par], primed(16 * TERMS * (g + par)))
                    bank, bias, scale = ((5, w("bq"), 1.0 / 4), (4, w("bk"), 1.0))[c]
                    act.wait_ge(s[("q_psum", "k_psum")[c]], g + 1)
                    act.activation(parts[c][:, 0, :], psum[:, bank, :], ACT.Identity, bias=bias, scale=scale).then_inc(s["hi_ready"], 1)
                    act.activation(qk[c][:, :], psum[:, bank, :], ACT.Identity, bias=bias, scale=scale).then_inc(s["qk_ready"], 1)

                def shift_ready(g, k):
                    n = G * g + k
                    act.wait_ge(s["mT_psum"], n + 1)
                    act.activation(mT[k % 2][0:2 * H, :], psum[:, 2 * (k % 2), :].bitcast(BF16)[0:2 * H, 0:P], ACT.Copy).then_inc(s["mT_ready"], 1)

                def weights(g, k):
                    n = G * g + k
                    act.wait_ge(s["scoresT"], primed(n + 1))
                    act.activation(PT[k % 2][:, :, :], slot(k), ACT.Exp).then_inc(s["exp_ready"], 1)

                def output_ready(g, k):
                    n = G * g + k
                    act.wait_ge(s["oT_psum"], n + 1)
                    act.activation(OT[k % 2][:, :], psum[:, 6, 0:P], ACT.Copy).then_inc(s["oT_ready"], 1)

                def before():
                    prime(act, s["hi_ready"])
                    act.wait_ge(s["rs"], 2)
                    relu(0)
                    evacuate(0, 0, 0)
                    evacuate(0, 0, 1)

                def turn(g, par, first, last):
                    for k in range(G):
                        shift_ready(g, k)
                        if not last and k == 0:
                            relu(g + 1)
                        if not last and k == 1:
                            evacuate(g + 1, 1 - par, 0)
                        if not first or k >= 1:
                            output_ready(*((g, k - 1) if k else (g - 1, G - 1)))
                        weights(g, k)
                        if not last and k == 1:
                            evacuate(g + 1, 1 - par, 1)
                    if last:
                        output_ready(g, G - 1)

                act.activation(rstd[:, :], var[:, :], ACT.Sqrt, bias=env["epsc"][:, :]).then_inc(s["sd"], 1)
                act.activation(env["scratch"][:, :], env["epsc"][:, :], ACT.Exp)
                each_group(act, before, turn)

            @block.vector
            def _(dve):
                def normalise(g):
                    if not isinstance(g, int) or g >= 1:
                        dve.wait_ge(s["hT_psum"], g)
                    for b in range(G):
                        gb = g * G + b
                        m = dve.tensor_scalar(hN[:, b, :], X[:, bass.ds(gb, 1), :], mean[:, bass.ds(gb, 1)], rstd[:, bass.ds(gb, 1)],
                                              ALU.subtract, ALU.mult)
                    m.then_inc(s["ln_ready"], 1)

                def remainder(g, c):
                    if not isinstance(g, int) or g >= 1:
                        dve.wait_ge(s["lo_ready"], primed(2 * (g - 1) + c + 1))
                    dve.wait_ge(s["qk_ready"], 2 * g + c + 1)
                    dve.wait_ge(s["hi_ready"], primed(2 * g + c + 1))
                    dve.tensor_tensor(rem[c][:, :], qk[c][:, :], parts[c][:, 0, :], ALU.subtract).then_inc(s["rem_ready"], 1)
                    dve.wait_ge(s["rem_ready"], 2 * g + c + 1)
                    dve.tensor_copy(parts[c][:, 1, :], rem[c][:, :]).then_inc(s["mid_ready"], 1)

                def values(g, par):
                    dve.wait_ge(s["v_psum"], g + 1)
                    if not isinstance(g, int) or g >= 2:
                        dve.wait_ge(s["pv"], primed(G * (g - 1)))
                    dve.wait_ge(s["clean"], 8)
                    dve.tensor_tensor(V[par][:, :, 0:H * HV].rearrange("p b (h d) -> p b h d", h=H)[:, :, :, 0:HD], psum[:, 5, :].rearrange("p (b h d) -> p b h d", b=G, h=H),
                                      bcast(w("bv").rearrange("p (h d) -> p h d", h=H), 1, G), ALU.add).then_inc(s["v_ready"], 1)

                def maxima(g, k):
                    n = G * g + k
                    dve.wait_ge(s["scores"], n + 1)
                    dve.tensor_reduce(negmax[k % 2][:, :], slot(k), AX.X, ALU.max, negate=True).then_inc(s["max_ready"], 1)
                    dve.wait_ge(s["max_ready"], n + 1)
                    dve.tensor_copy(mparts[k % 2][:, 0:H], negmax[k % 2][:, :]).then_inc(s["mhi_ready"], 1)
                    dve.wait_ge(s["mhi_ready"], n + 1)
                    dve.tensor_tensor(mparts[k % 2][:, H:2 * H], negmax[k % 2][:, :], mparts[k % 2][:, 0:H], ALU.subtract).then_inc(s["mparts_ready"], 1)

                def normalise_output(g, k):
                    n = G * g + k
                    dve.wait_ge(s["pv"], primed(n + 1))
                    y = psum[:, 2 * (k % 2), :].rearrange("p (h d) -> p h d", h=H)
                    dve.reciprocal(rden[k % 2][:, :], y[:, :, HD]).then_inc(s["rden_ready"], 1)
                    dve.wait_ge(s["rden_ready"], n + 1)
                    dve.tensor_tensor(O[k % 2][:, :].rearrange("p (h d) -> p h d", h=H), y[:, :, 0:HD],
                                      bcast(rden[k % 2][:, :], 2, HD), ALU.mult).then_inc(s["o_ready"], 1)

                def add_to_x(g, k):
                    n = G * g + k
                    dve.wait_ge(s["y_psum"], n + 1)
                    if k == 0:
                        dve.wait_ge(s["bias_added"], g + 1)
                    xu = X[:, bass.ds(n, 1), :]
                    dve.tensor_tensor(xu, psum[:, 7, 0:P].unsqueeze(1), xu, ALU.add).then_inc(s["x_ready"], 1)

                def before():
                    prime(dve, s["x_ready"], s["mid_ready"])
                    dve.wait_ge(s["sd"], 1)
                    dve.reciprocal(rstd[:, :], rstd[:, :]).then_inc(s["rs"], 1)
                    dve.tensor_scalar(w("bq"), w("bq"), 1.0 / 4, None, ALU.mult).then_inc(s["rs"], 1)
                    dve.tensor_copy(selb[:, :, :], w("sel").rearrange("p (h n) -> p h n", h=H)).then_inc(s["sel_ready"], 1)
                    dve.wait_ge(s["rs"], 2)
                    normalise(0)
                    remainder(0, 0)
                    remainder(0, 1)
                    values(0, 0)

                def turn(g, par, first, last):
                    if not last:
                        normalise(g + 1)
                    for k in range(G):
                        maxima(g, k)
                        if not last and k == 2:
                            remainder(g + 1, 0)
                        if not first or k >= 2:
                            add_to_x(*((g, k - 2) if k >= 2 else (g - 1, k + G - 2)))
                        if not last and k == 2:
                            remainder(g + 1, 1)
                        if not first or k >= 1:
                            normalise_output(*((g, k - 1) if k else (g - 1, G - 1)))
                        if not first and k == 1:
                            group_statistics(env, dve, g - 1, s["x_ready"], s["stat_step"])
                        if not last and k == 3:
                            values(g + 1, 1 - par)
                    if last:
                        add_to_x(g, G - 2)
                        normalise_output(g, G - 1)
                        add_to_x(g, G - 1)
                        group_statistics(env, dve, g, s["x_ready"], s["stat_step"])

                each_group(dve, before, turn)


def group_statistics(env, dve, g, x_ready, stat_step):
    dve.wait_ge(x_ready, primed(G * (g + 1)))
    row_statistics(env, dve, env["X"], g, env["mean"], env["var"], stat_step)


def row_statistics(env, dve, source, g, mean, var, step):
    stats, meanvar = env["stats"], env["meanvar"]
    settle(dve, env["passed"])
    for b in range(G):
        m = dve.bn_stats(stats[:, b, :], source[:, bass.ds(g * G + b, 1), :])
    m.then_inc(step, 1)
    dve.wait_ge(step, 3 * g + 1)
    settle(dve, env["passed"])
    for b in range(G):
        m = dve.bn_aggr(meanvar[:, b, :], stats[:, b, :])
    m.then_inc(step, 1)
    dve.wait_ge(step, 3 * g + 2)
    settle(dve, env["passed"])
    dve.tensor_copy(mean[:, bass.ds(g * G, G)], meanvar[:, :, 0])
    dve.tensor_copy(var[:, bass.ds(g * G, G)], meanvar[:, :, 1]).then_inc(step, 1)
    dve.wait_ge(step, 3 * g + 3)


def store(env):
    nc, sem, X, out = (env[k] for k in ("nc", "sem", "X", "out"))
    stored = sem("stored")
    with nc.Block() as block:
        @block.sync
        def _(sp):
            sp.dma_start(out, X[:, :, :]).then_inc(stored, 16)
            sp.wait_ge(stored, 16)


def column_layer(env):
    nc, X, w, ident, psum = (env[k] for k in ("nc", "X", "w", "ident", "psum"))
    stats, meanvar, mean, var, rstd = (env[k] for k in ("stats", "meanvar", "mean", "var", "rstd"))
    NI = GRAPHS // (2 * G)
    with ExitStack() as ctx:
        def sb(name, shape, dt=F32):
            return [ctx.enter_context(nc.sbuf_tensor(f"c_{name}{u}", shape, dt)) for u in range(2)]

        def sem(name):
            return ctx.enter_context(nc.semaphore("c_" + name))

        adjT_i, maskT = sb("adjT_i", [P, G, P], I32), sb("maskT", [P, G, P])
        hN, hT = sb("hN", [P, G, P]), sb("hT", [P, G * P])
        a2 = sb("a2", [P, G])
        E, PT = sb("E", [P, G, P]), sb("PT", [P, G, P])
        negmax, den, rden = sb("negmax", [P, G]), sb("den", [P, G]), sb("rden", [P, G])
        hs = sb("hs", [P, G, P])
        pos, neg, hid = sb("pos", [P, G, P]), sb("neg", [P, G, P]), sb("hid", [P, G, P])
        hidT = sb("hidT", [P, G * P])

        adj_in = [sem("adj_in0"), sem("adj_in1")]
        leaky_ready, mask_ready, sd_ready, rs_ready = sem("leaky_ready"), sem("mask_ready"), sem("sd_ready"), sem("rs_ready")
        ln_ready, bias_added, hT_psum, hT_ready = (sem(n) for n in ("ln_ready", "bias_added", "hT_psum", "hT_ready"))
        proj, a2_ready, e_ready, em_ready, max_ready, exp_ready = (sem(n) for n in ("proj", "a2_ready", "e_ready", "em_ready", "max_ready", "exp_ready"))
        rden_ready, hs_ready, att, neg_ready, pos_ready, nexp_ready, hid_ready = (sem(n) for n in ("rden_ready", "hs_ready", "att", "neg_ready", "pos_ready", "nexp_ready", "hid_ready"))
        hidT_psum, hidT_ready, y_psum, x_ready, stat_step = (sem(n) for n in ("hidT_psum", "hidT_ready", "y_psum", "x_ready", "stat_step"))

        def bank(u, k):
            return psum[:, 4 * u + k, :]

        def graphs(u, k):
            return psum[:, 4 * u + k, :].rearrange("p (b n) -> p b n", b=G)

        with nc.Block() as block:
            @block.sync
            def _(sp):
                with sp.Fori(0, NI) as i:
                    for u in range(2):
                        sp.wait_ge(mask_ready, primed(2 * i))
                        sp.dma_start(adjT_i[u][:, :, :], env["adjT"][:, bass.ds((2 * i + u) * G, G), :]).then_inc(adj_in[u], 16)

            @block.gpsimd
            def _(pool):
                prime(pool, mask_ready)
                with pool.Fori(0, NI) as i:
                    for u in range(2):
                        pool.wait_ge(sd_ready, 1)
                        pool.wait_ge(em_ready, primed(2 * i))
                        pool.wait_ge(adj_in[u], 16 * i + 16)
                        settle(pool, env["passed"])
                        pool.tensor_scalar(maskT[u][:, :, :], adjT_i[u][:, :, :], BIG1, -BIG1, ALU.mult, ALU.add).then_inc(mask_ready, 1)
                    for u in range(2):
                        pool.wait_ge(ln_ready, 2 * i + u + 1)
                        xg = X[:, bass.ds((2 * i + u) * G, G), :]
                        pool.tensor_tensor(xg, xg, bcast(w("hanb"), 1, G), ALU.add).then_inc(bias_added, 1)

            @block.tensor
            def _(pe):
                with pe.Fori(0, NI) as i:
                    for u in range(2):
                        n = 2 * i + u
                        pe.wait_ge(ln_ready, n + 1)
                        pe.wait_ge(x_ready, primed(2 * i))
                        for b in range(G):
                            m = pe.transpose(graphs(u, 0)[:, b, :], hN[u][:, b, :], ident)
                        m.then_inc(hT_psum, 1)
                    for u in range(2):
                        n = 2 * i + u
                        pe.wait_ge(hT_ready, n + 1)
                        for b in range(G):
                            pe.matmul(psum[:, 4 * u + 2, b:b + 1], hT[u][:, b * P:(b + 1) * P], w("a2col"), start=True, stop=True)
                        pe.matmul(bank(u, 3), w("a1rep"), hT[u][:, :], start=True, stop=True)
                        for b in range(G):
                            m = pe.matmul(graphs(u, 1)[:, b, :], hT[u][:, b * P:(b + 1) * P], w("w1"), start=True, stop=True)
                        m.then_inc(proj, 1)
                    for u in range(2):
                        n = 2 * i + u
                        pe.wait_ge(exp_ready, G * (n + 1))
                        pe.wait_ge(hs_ready, n + 1)
                        for b in range(G):
                            m = pe.matmul(graphs(u, 2)[:, b, :], PT[u][:, b, :], hs[u][:, b, :], start=True, stop=True)
                        m.then_inc(att, 1)
                    for u in range(2):
                        n = 2 * i + u
                        pe.wait_ge(hid_ready, n + 1)
                        for b in range(G):
                            m = pe.transpose(graphs(u, 0)[:, b, :], hid[u][:, b, :], ident)
                        m.then_inc(hidT_psum, 1)
                    for u in range(2):
                        n = 2 * i + u
                        pe.wait_ge(hidT_ready, n + 1)
                        for b in range(G):
                            m = pe.matmul(graphs(u, 1)[:, b, :], hidT[u][:, b * P:(b + 1) * P], w("han"), start=True, stop=True)
                        m.then_inc(y_psum, 1)

            @block.scalar
            def _(act):
                act.activation(rstd[:, :], var[:, :], ACT.Sqrt, bias=env["epsc"][:, :]).then_inc(sd_ready, 1)
                act.activation(env["scratch"][:, :], env["epsc"][:, :], ACT.Exp)
                with act.Fori(0, NI) as i:
                    for u in range(2):
                        n = 2 * i + u
                        act.wait_ge(hT_psum, n + 1)
                        act.activation(hT[u][:, :], bank(u, 0), ACT.Relu).then_inc(hT_ready, 1)
                    for u in range(2):
                        n = 2 * i + u
                        act.wait_ge(proj, n + 1)
                        act.wait_ge(a2_ready, n + 1)
                        for b in range(G):
                            m = act.activation(E[u][:, b, :], graphs(u, 3)[:, b, :], ACT.Identity, bias=a2[u][:, b:b + 1])
                        m.then_inc(e_ready, 1)
                    for u in range(2):
                        n = 2 * i + u
                        act.wait_ge(max_ready, n + 1)
                        for b in range(G):
                            act.activation(PT[u][:, b, :], E[u][:, b, :], ACT.Exp, bias=negmax[u][:, b:b + 1],
                                           accum_out=den[u][:, b:b + 1]).then_inc(exp_ready, 1)
                    for u in range(2):
                        n = 2 * i + u
                        act.wait_ge(neg_ready, n + 1)
                        act.activation(neg[u][:, :, :], neg[u][:, :, :], ACT.Exp).then_inc(nexp_ready, 1)
                    for u in range(2):
                        n = 2 * i + u
                        act.wait_ge(hidT_psum, n + 1)
                        act.activation(hidT[u][:, :], bank(u, 0), ACT.Copy).then_inc(hidT_ready, 1)

            @block.vector
            def _(dve):
                prime(dve, em_ready, x_ready)
                dve.wait_ge(sd_ready, 1)
                dve.reciprocal(rstd[:, :], rstd[:, :]).then_inc(rs_ready, 1)
                dve.wait_ge(rs_ready, 1)
                with dve.Fori(0, NI) as i:
                    for u in range(2):
                        n = 2 * i + u
                        for b in range(G):
                            g = n * G + b
                            m = dve.tensor_scalar(hN[u][:, b, :], X[:, bass.ds(g, 1), :], mean[:, bass.ds(g, 1)], rstd[:, bass.ds(g, 1)],
                                                  ALU.subtract, ALU.mult)
                        m.then_inc(ln_ready, 1)
                    for u in range(2):
                        n = 2 * i + u
                        dve.wait_ge(proj, n + 1)
                        dve.tensor_copy(a2[u][:, :], psum[:, 4 * u + 2, 0:G]).then_inc(a2_ready, 1)
                    for u in range(2):
                        n = 2 * i + u
                        dve.wait_ge(e_ready, n + 1)
                        dve.wait_ge(mask_ready, primed(n + 1))
                        dve.scalar_tensor_tensor(out=E[u][:, :, :], in0=E[u][:, :, :], scalar=SLOPE, in1=E[u][:, :, :],
                                                 op0=ALU.mult, op1=ALU.max).then_inc(leaky_ready, 1)
                        dve.wait_ge(leaky_ready, n + 1)
                        dve.tensor_tensor(E[u][:, :, :], E[u][:, :, :], maskT[u][:, :, :], ALU.add).then_inc(em_ready, 1)
                        dve.wait_ge(em_ready, primed(n + 1))
                        dve.tensor_reduce(negmax[u][:, :], E[u][:, :, :], AX.X, ALU.max, negate=True).then_inc(max_ready, 1)
                    for u in range(2):
                        n = 2 * i + u
                        dve.wait_ge(exp_ready, G * (n + 1))
                        dve.reciprocal(rden[u][:, :], den[u][:, :]).then_inc(rden_ready, 1)
                        dve.wait_ge(rden_ready, n + 1)
                        dve.tensor_tensor(hs[u][:, :, :], graphs(u, 1), bcast(rden[u][:, :], 2, P), ALU.mult).then_inc(hs_ready, 1)
                    for u in range(2):
                        n = 2 * i + u
                        dve.wait_ge(att, n + 1)
                        dve.tensor_scalar(neg[u][:, :, :], graphs(u, 2), 0.0, None, ALU.min).then_inc(neg_ready, 1)
                        dve.tensor_scalar(pos[u][:, :, :], graphs(u, 2), 0.0, None, ALU.max).then_inc(pos_ready, 1)
                    for u in range(2):
                        n = 2 * i + u
                        dve.wait_ge(nexp_ready, n + 1)
                        dve.wait_ge(pos_ready, n + 1)
                        dve.scalar_tensor_tensor(out=hid[u][:, :, :], in0=neg[u][:, :, :], scalar=-1.0, in1=pos[u][:, :, :],
                                                 op0=ALU.add, op1=ALU.add).then_inc(hid_ready, 1)
                    for u in range(2):
                        n = 2 * i + u
                        dve.wait_ge(y_psum, n + 1)
                        dve.wait_ge(bias_added, n + 1)
                        residual(env, dve, n * G, G, graphs(u, 1), n, x_ready, stat_step)


def residual(env, dve, g, count, y, n, x_ready, stat_step):
    X, stats, meanvar, mean, var = (env[k] for k in ("X", "stats", "meanvar", "mean", "var"))
    xu = X[:, bass.ds(g, count), :]
    dve.tensor_tensor(xu, y, xu, ALU.add).then_inc(x_ready, 1)
    dve.wait_ge(env["w_in"], 16)
    dve.wait_ge(x_ready, primed(n + 1))
    settle(dve, env["passed"])
    for b in range(count):
        m = dve.bn_stats(stats[:, b, :], X[:, bass.ds(g + b, 1), :])
    m.then_inc(stat_step, 1)
    dve.wait_ge(env["w_in"], 16)
    dve.wait_ge(stat_step, 3 * n + 1)
    settle(dve, env["passed"])
    for b in range(count):
        m = dve.bn_aggr(meanvar[:, b, :], stats[:, b, :])
    m.then_inc(stat_step, 1)
    dve.wait_ge(env["w_in"], 16)
    dve.wait_ge(stat_step, 3 * n + 2)
    settle(dve, env["passed"])
    dve.tensor_copy(mean[:, bass.ds(g, count)], meanvar[:, 0:count, 0])
    dve.tensor_copy(var[:, bass.ds(g, count)], meanvar[:, 0:count, 1]).then_inc(stat_step, 1)
    dve.wait_ge(stat_step, 3 * n + 3)


def edge_layer(env):
    nc, X, w, ident, identb, psum = (env[k] for k in ("nc", "X", "w", "ident", "identb", "psum"))
    stats, meanvar, mean, var, rstd, shift = (env[k] for k in ("stats", "meanvar", "mean", "var", "rstd", "shift"))
    NG = GRAPHS // G
    PARTS = 3
    ROWS = P // G
    PROJ = P + 2 * H
    T_BANK, ROW_BANK = 6, 7
    RS = 64
    RCOLS = (H - 1) * 2 * HV + RS
    with ExitStack() as ctx:
        def one(name, shape, dt=F32):
            return ctx.enter_context(nc.sbuf_tensor("e_" + name, shape, dt))

        def sb(name, shape, dt=F32):
            return [one(f"{name}{u}", shape, dt) for u in range(2)]

        def sem(name):
            return ctx.enter_context(nc.semaphore("e_" + name))

        Y = one("Y", [P, GRAPHS, P])
        ymean, yvar = one("ymean", [P, GRAPHS]), one("yvar", [P, GRAPHS])
        wproj = one("wproj", [P, PROJ])
        selb = one("selb", [P, G, H, P], BF16)
        adjT_i, maskT, MT = sb("adjT_i", [P, G, P], I32), sb("maskT", [P, G, P], BF16), sb("MT", [P, G, P])
        hN, hT = one("hN", [P, G, P]), one("hT", [P, G * P])
        s1, s2, c, d, t, m8, m02, tm, t02, tm2 = (one(n, [P, G, H]) for n in ("s1", "s2", "c", "d", "t", "m8", "m", "tm", "t02", "tm2"))
        rem1, parts, rows = one("rem1", [P, G, H]), one("parts", [P, G, ROWS], BF16), sb("rows", [P, P], BF16)
        ns2, U = sb("ns2", [P, G, H]), sb("U", [P, G, H, 2])
        Rpad, R2 = sb("R", [P, G, RCOLS]), sb("R2", [P, G, H, HV])
        R = [a[:, :, 0:H * 2 * HV].rearrange("p b (h d) -> p b h d", h=H) for a in Rpad]
        E = sb("E", [P, H, P])
        y12, yy, rden = sb("y12", [P, H, 2, HV]), sb("yy", [P, H, HV]), sb("rden", [P, H])

        adj_in = [sem("adj_in0"), sem("adj_in1")]
        names = ("mask_ready", "sd_ready", "rs_ready", "ln_ready", "ws_psum", "ws_ready", "parts_clean", "sel_clean", "hT_psum", "hT_ready", "proj",
                 "s1_ready", "s2_ready", "c_ready", "d_ready", "t_step", "tm_ready", "v_ready", "u_ready", "split_step",
                 "parts_ready", "rows_psum", "rows_ready", "vv_ready", "r_ready",
                 "z_psum", "e_ready", "pv", "y12_ready", "yy_ready", "rden_ready", "y_ready", "stat_step")
        s = {n: sem(n) for n in names}
        w_in = env["w_in"]

        def each_group(eng, before, turn):
            before()
            turn(0, 0, True, 2)
            with eng.Fori(0, NG // 2 - 2) as i:
                turn(2 * i + 1, 1, False, 2)
                turn(2 * i + 2, 0, False, 2)
            turn(NG - 3, 1, False, 2)
            turn(NG - 2, 0, False, 1)
            turn(NG - 1, 1, False, 0)

        def unit_before(g, par, k, back):
            return (g, par, k - back) if k >= back else (g - 1, 1 - par, k - back + G)

        def begun(g, n):
            return not isinstance(g, int) or g >= n

        def slot(k):
            return psum[:, 2 * (k % 2):2 * (k % 2) + 2, :].rearrange("p a (h n) -> p (a h) n", h=H // 2)

        def sums(k):
            return psum[:, 4 + k % 2, :].rearrange("p (h d) -> p h d", h=H)

        def projections(b):
            at = PROJ * (b % 2)
            return psum[:, T_BANK + b // 2, at:at + PROJ]

        def score_columns(first):
            return psum[:, T_BANK:T_BANK + 2, 0:2 * PROJ].rearrange("p a (b k) -> p a b k", b=2)[:, :, :, P + first:P + first + H]

        row_parts = psum[:, ROW_BANK, 2 * PROJ:2 * PROJ + P // 2].bitcast(BF16)

        with nc.Block() as block:
            @block.sync
            def _(sp):
                def load_adj(g, par):
                    if begun(g, 2):
                        sp.wait_ge(s["mask_ready"], 2 * (g - 1))
                        settle(sp, env["passed"])
                    sp.dma_start(adjT_i[par][:, :, :], env["adjT"][:, bass.ds(g * G, G), :]).then_inc(adj_in[par], 16)

                def turn(g, par, first, left):
                    if left:
                        load_adj(g + 1, 1 - par)

                each_group(sp, lambda: load_adj(0, 0), turn)

            @block.gpsimd
            def _(pool):
                def masks(g, par):
                    if begun(g, 2):
                        pool.wait_ge(s["pv"], G * (g - 1))
                    pool.wait_ge(adj_in[par], 8 * (g - par) + 16)
                    settle(pool, env["passed"])
                    pool.tensor_scalar(maskT[par][:, :, :], adjT_i[par][:, :, :], BIG, -BIG, ALU.mult, ALU.add).then_inc(s["mask_ready"], 1)
                    pool.tensor_scalar(MT[par][:, :, :], adjT_i[par][:, :, :], 1.0, 0.0, ALU.min, ALU.max).then_inc(s["mask_ready"], 1)

                def split(g):
                    if begun(g, 1):
                        pool.wait_ge(s["rows_psum"], g)
                    pool.wait_ge(s["s1_ready"], g + 1)
                    settle(pool, env["passed"])
                    pool.tensor_copy(parts[:, :, 0:H], s1[:, :, :]).then_inc(s["split_step"], 1)
                    pool.wait_ge(s["split_step"], 3 * g + 1)
                    pool.tensor_tensor(rem1[:, :, :], s1[:, :, :], parts[:, :, 0:H], ALU.subtract).then_inc(s["split_step"], 1)
                    pool.wait_ge(s["split_step"], 3 * g + 2)
                    settle(pool, env["passed"])
                    pool.tensor_copy(parts[:, :, H:2 * H], rem1[:, :, :]).then_inc(s["split_step"], 1)
                    pool.wait_ge(s["split_step"], 3 * g + 3)
                    pool.tensor_tensor(parts[:, :, 2 * H:3 * H], rem1[:, :, :], parts[:, :, H:2 * H], ALU.subtract).then_inc(s["parts_ready"], 1)

                def exponents(g):
                    if begun(g, 1):
                        pool.wait_ge(s["v_ready"], 2 * g)
                        pool.wait_ge(s["u_ready"], 2 * g)
                    pool.wait_ge(s["s2_ready"], 2 * g + 2)
                    settle(pool, env["passed"])
                    pool.partition_all_reduce(c[:, :, :].rearrange("p b h -> p (b h)"), s2[:, :, :].rearrange("p b h -> p (b h)"),
                                              P, RMAX).then_inc(s["c_ready"], 1)
                    pool.wait_ge(s["c_ready"], g + 1)
                    pool.tensor_tensor(d[:, :, :], s2[:, :, :], c[:, :, :], ALU.subtract).then_inc(s["d_ready"], 1)
                    pool.tensor_tensor(t[:, :, :], s1[:, :, :], c[:, :, :], ALU.add).then_inc(s["t_step"], 1)
                    pool.wait_ge(s["t_step"], 4 * g + 1)
                    settle(pool, env["passed"])
                    pool.tensor_scalar(m8[:, :, :], t[:, :, :], 0.0, 1.0 - SLOPE, ALU.max, ALU.mult).then_inc(s["t_step"], 1)
                    pool.tensor_scalar(t02[:, :, :], t[:, :, :], SLOPE, None, ALU.mult).then_inc(s["t_step"], 1)
                    pool.wait_ge(s["t_step"], 4 * g + 3)
                    pool.tensor_tensor(m02[:, :, :], m8[:, :, :], t02[:, :, :], ALU.add).then_inc(s["t_step"], 1)
                    pool.wait_ge(s["t_step"], 4 * g + 4)
                    pool.tensor_tensor(tm[:, :, :], t[:, :, :], m02[:, :, :], ALU.subtract).then_inc(s["tm_ready"], 1)
                    pool.tensor_tensor(tm2[:, :, :], t02[:, :, :], m02[:, :, :], ALU.subtract).then_inc(s["tm_ready"], 1)

                def prepare(g, par):
                    masks(g, par)
                    split(g)
                    exponents(g)

                def turn(g, par, first, left):
                    if left:
                        prepare(g + 1, 1 - par)

                pool.memset(parts[:, :, :], 0.0).then_inc(s["parts_clean"], 1)
                pool.wait_ge(s["parts_clean"], 1)
                each_group(pool, lambda: prepare(0, 0), turn)

            @block.tensor
            def _(pe):
                def project(g, par, item):
                    if item == 0:
                        pe.wait_ge(s["ln_ready"], g + 1)
                        if begun(g, 1):
                            pe.wait_ge(s["vv_ready"], 2 * g)
                        for b in range(G):
                            m = pe.transpose(psum[:, T_BANK, b * P:(b + 1) * P], hN[:, b, :], ident)
                        m.then_inc(s["hT_psum"], 1)
                    if item == 1:
                        pe.wait_ge(s["hT_ready"], g + 1)
                        for b in range(G):
                            m = pe.matmul(projections(b), hT[:, b * P:(b + 1) * P], wproj[:, :], start=True, stop=True)
                        m.then_inc(s["proj"], 1)
                    if item == 2:
                        pe.wait_ge(s["s2_ready"], 2 * g + 2)
                        pe.wait_ge(s["parts_ready"], g + 1)
                        pe.transpose(row_parts, parts[:, :, :].rearrange("p b r -> p (b r)"), identb[:, :]).then_inc(s["rows_psum"], 1)

                def scores(g, par, k):
                    n = G * g + k
                    if k == 0:
                        pe.wait_ge(s["rows_ready"], g + 1)
                        pe.wait_ge(s["mask_ready"], 2 * g + 2)
                    if not (isinstance(g, int) and g == 0 and k < 2):
                        pe.wait_ge(s["e_ready"], n - 1)
                    for a in range(2):
                        for h in range(H // 2):
                            hh = a * (H // 2) + h
                            pe.matmul(slot(k)[:, hh, :], selb[:, k, hh, :], rows[par][:, :], start=(h == 0), stop=False, skip_group_check=True)
                        m = pe.matmul(psum[:, 2 * (k % 2) + a, :], identb[:, :], bcast(maskT[par][:, k, :], 1, H // 2),
                                      start=False, stop=True, skip_group_check=True)
                    m.then_inc(s["z_psum"], 1)

                def products(g, par, k):
                    n = G * g + k
                    if k == 0:
                        pe.wait_ge(s["r_ready"], g + 1)
                    if not (isinstance(g, int) and g == 0 and k < 2):
                        pe.wait_ge(s["y12_ready"], n - 1)
                    pe.matmul(sums(k)[:, :, HV:2 * HV], MT[par][:, k, :], R2[par][:, k, :, :], start=True, stop=False, skip_group_check=True)
                    pe.wait_ge(s["e_ready"], n + 1)
                    for h in range(H):
                        m = pe.matmul(sums(k)[:, h, :], E[k % 2][:, h, :], Rpad[par][:, k, 2 * HV * h:2 * HV * h + RS], start=False, stop=(h == H - 1), skip_group_check=True)
                    m.then_inc(s["pv"], 1)

                def before():
                    pe.wait_ge(w_in, 16)
                    pe.matmul(psum[:, 0, 0:2 * H], w("w2T"), w("adiag"), start=True, stop=True).then_inc(s["ws_psum"], 1)
                    pe.wait_ge(s["ws_ready"], 2)
                    for item in range(3):
                        project(0, 0, item)

                def turn(g, par, first, left):
                    for k in range(G):
                        scores(g, par, k)
                        if left and k in (1, 2):
                            project(g + 1, 1 - par, k)
                        if not first or k >= 1:
                            products(*unit_before(g, par, k, 1))
                        if left and k == 0:
                            project(g + 1, 1 - par, k)
                    if not left:
                        products(g, par, G - 1)

                each_group(pe, before, turn)

            @block.scalar
            def _(act):
                def normalise(g):
                    if begun(g, 1):
                        act.wait_ge(s["hT_psum"], g)
                    for b in range(G):
                        gb = g * G + b
                        m = act.activation(hN[:, b:b + 1, :], X[:, bass.ds(gb, 1), :], ACT.Relu,
                                           bias=shift[:, bass.ds(gb, 1)], scale=rstd[:, bass.ds(gb, 1)])
                    m.then_inc(s["ln_ready"], 1)

                def transposed(g):
                    if begun(g, 1):
                        act.wait_ge(s["proj"], g)
                    act.wait_ge(s["hT_psum"], g + 1)
                    act.activation(hT[:, :], psum[:, T_BANK, :], ACT.Copy).then_inc(s["hT_ready"], 1)

                def s2_copies(g, par):
                    if begun(g, 1):
                        act.wait_ge(s["d_ready"], g)
                    if begun(g, 2):
                        act.wait_ge(s["e_ready"], G * (g - 1))
                    act.wait_ge(s["proj"], g + 1)
                    act.wait_ge(s["s1_ready"], g + 1)
                    for into, scale in ((s2, 1.0), (ns2[par], -1.0)):
                        act.activation(into[:, :, :].rearrange("p (a b) h -> p a b h", a=2), score_columns(H), ACT.Copy, scale=scale).then_inc(s["s2_ready"], 1)

                def row_copy(g, par):
                    if begun(g, 2):
                        act.wait_ge(s["z_psum"], G * (g - 1))
                    act.wait_ge(s["rows_psum"], g + 1)
                    act.activation(rows[par][:, :], row_parts, ACT.Copy).then_inc(s["rows_ready"], 1)

                def factors(g, par):
                    if begun(g, 2):
                        act.wait_ge(s["y12_ready"], G * (g - 1))
                    act.wait_ge(s["d_ready"], g + 1)
                    act.activation(R[par][:, :, :, HD], d[:, :, :], ACT.Exp).then_inc(s["v_ready"], 1)
                    act.activation(R2[par][:, :, :, HD], d[:, :, :], ACT.Exp, scale=SLOPE).then_inc(s["v_ready"], 1)
                    act.wait_ge(s["tm_ready"], 2 * g + 2)
                    act.activation(U[par][:, :, :, 0], tm[:, :, :], ACT.Exp).then_inc(s["u_ready"], 1)
                    act.activation(U[par][:, :, :, 1], tm2[:, :, :], ACT.Exp).then_inc(s["u_ready"], 1)

                def negate(g, par):
                    act.wait_ge(s["vv_ready"], 2 * g + 2)
                    act.activation(R[par][:, :, :, HV:2 * HV], R2[par][:, :, :, :], ACT.Copy, scale=-1.0).then_inc(s["r_ready"], 1)

                def prepare(g, par):
                    transposed(g)
                    s2_copies(g, par)
                    row_copy(g, par)
                    factors(g, par)

                def before():
                    act.wait_ge(s["rs_ready"], 2)
                    normalise(0)
                    prepare(0, 0)
                    normalise(1)
                    negate(0, 0)

                def turn(g, par, first, left):
                    if left:
                        prepare(g + 1, 1 - par)
                        if left == 2:
                            normalise(g + 2)
                        negate(g + 1, 1 - par)

                act.activation(rstd[:, :], var[:, :], ACT.Sqrt, bias=env["epsc"][:, :]).then_inc(s["sd_ready"], 1)
                act.activation(env["scratch"][:, :], env["epsc"][:, :], ACT.Exp)
                each_group(act, before, turn)

            @block.vector
            def _(dve):
                def s1_sum(g):
                    if begun(g, 1):
                        dve.wait_ge(s["parts_ready"], g)
                        dve.wait_ge(s["t_step"], 4 * g)
                    dve.wait_ge(s["proj"], g + 1)
                    dve.tensor_tensor(s1[:, :, :].rearrange("p (a b) h -> p a b h", a=2), score_columns(0),
                                      bcast(bcast(w("emb"), 1, 2), 1, 2), ALU.add).then_inc(s["s1_ready"], 1)

                def values(g, par):
                    dve.wait_ge(s["v_ready"], 2 * g + 2)
                    for r in (R, R2):
                        for a in range(2):
                            V = psum[:, T_BANK + a, 0:2 * PROJ].rearrange("p (b k) -> p b k", b=2)[:, :, 0:P].rearrange("p b (h d) -> p b h d", h=H)
                            rr = r[par][:, 2 * a:2 * a + 2, :, :]
                            m = dve.tensor_tensor(rr[:, :, :, 0:HD], V, rr[:, :, :, HD:HD + 1].broadcast_to([P, 2, H, HD]), ALU.mult)
                        m.then_inc(s["vv_ready"], 1)

                def edges(g, par, k):
                    n = G * g + k
                    dve.wait_ge(s["z_psum"], n + 1)
                    dve.wait_ge(s["s2_ready"], 2 * g + 2)
                    if not (isinstance(g, int) and g == 0 and k < 2):
                        dve.wait_ge(s["pv"], n - 1)
                    dve.tensor_tensor(E[k % 2][:, :, :], slot(k), bcast(ns2[par][:, k, :], 2, P), ALU.is_gt).then_inc(s["e_ready"], 1)

                def weighted(g, par, k):
                    n = G * g + k
                    dve.wait_ge(s["pv"], n + 1)
                    dve.wait_ge(s["u_ready"], 2 * g + 2)
                    dve.tensor_tensor(y12[k % 2][:, :, :, :], sums(k)[:, :, 0:2 * HV].rearrange("p h (c d) -> p h c d", c=2),
                                      bcast(U[par][:, k, :, :], 3, HV), ALU.mult).then_inc(s["y12_ready"], 1)

                def summed(g, par, k):
                    dve.wait_ge(s["y12_ready"], G * g + k + 1)
                    dve.tensor_tensor(yy[k % 2][:, :, :], y12[k % 2][:, :, 0, :], y12[k % 2][:, :, 1, :], ALU.add).then_inc(s["yy_ready"], 1)

                def inverted(g, par, k):
                    dve.wait_ge(s["yy_ready"], G * g + k + 1)
                    dve.reciprocal(rden[k % 2][:, :], yy[k % 2][:, :, HD]).then_inc(s["rden_ready"], 1)

                def divided(g, par, k):
                    n = G * g + k
                    dve.wait_ge(s["rden_ready"], n + 1)
                    yg = Y[:, bass.ds(n, 1), :].rearrange("p b (h d) -> p (b h) d", h=H)
                    dve.tensor_tensor(yg, yy[k % 2][:, :, 0:HD], bcast(rden[k % 2][:, :], 2, HD), ALU.mult).then_inc(s["y_ready"], 1)

                def before():
                    dve.memset(selb[:, :, :, :], 0.0).then_inc(s["sel_clean"], 1)
                    for r in Rpad:
                        dve.memset(r[:, :, H * 2 * HV:], 0.0).then_inc(s["sel_clean"], 1)
                    dve.wait_ge(s["sd_ready"], 1)
                    dve.reciprocal(rstd[:, :], rstd[:, :]).then_inc(s["rs_ready"], 1)
                    dve.wait_ge(s["rs_ready"], 1)
                    dve.scalar_tensor_tensor(out=shift[:, :], in0=mean[:, :], scalar=-1.0, in1=rstd[:, :], op0=ALU.mult, op1=ALU.mult).then_inc(s["rs_ready"], 1)
                    dve.wait_ge(s["sel_clean"], 3)
                    for b in range(G):
                        at = b * ROWS
                        dve.tensor_copy(selb[at:at + PARTS * H, b, :, :], w("sel")[at:at + PARTS * H, :].rearrange("p (h n) -> p h n", h=H))
                    dve.tensor_copy(wproj[:, 0:P], w("w2")).then_inc(s["ws_ready"], 1)
                    dve.wait_ge(s["ws_psum"], 1)
                    dve.tensor_copy(wproj[:, P:PROJ], psum[:, 0, 0:2 * H]).then_inc(s["ws_ready"], 1)
                    s1_sum(0)
                    values(0, 0)

                def turn(g, par, first, left):
                    for k in range(G):
                        edges(g, par, k)
                        if left and k == 1:
                            s1_sum(g + 1)
                        if not first or k >= 2:
                            inverted(*unit_before(g, par, k, 2))
                        if not first or k >= 1:
                            weighted(*unit_before(g, par, k, 1))
                        if not first or k >= 2:
                            divided(*unit_before(g, par, k, 2))
                        if not first or k >= 1:
                            summed(*unit_before(g, par, k, 1))
                        if not first and k == 2:
                            output_statistics(g - 1)
                        if left and k == G - 1:
                            values(g + 1, 1 - par)
                    if not left:
                        inverted(g, par, G - 2)
                        weighted(g, par, G - 1)
                        divided(g, par, G - 2)
                        summed(g, par, G - 1)
                        inverted(g, par, G - 1)
                        divided(g, par, G - 1)
                        output_statistics(g)

                def output_statistics(g):
                    dve.wait_ge(s["y_ready"], G * (g + 1))
                    row_statistics(env, dve, Y, g, ymean, yvar, s["stat_step"])

                each_group(dve, before, turn)

        yn, pos, neg = sb("yn", [P, G, P]), sb("pos", [P, G, P]), sb("neg", [P, G, P])
        names2 = ("ysd", "yrs", "yn_ready", "gamma_done", "beta_done", "neg_ready", "pos_ready", "exp_ready", "elu_ready",
                  "x_ready", "stat_step")
        s2_ = {n: sem("second_" + n) for n in names2}
        NG2 = GRAPHS // (2 * G)
        with nc.Block() as block:
            @block.scalar
            def _(act):
                act.activation(rstd[:, :], yvar[:, :], ACT.Sqrt, bias=env["epsc"][:, :]).then_inc(s2_["ysd"], 1)
                act.activation(env["scratch"][:, :], env["epsc"][:, :], ACT.Exp)
                with act.Fori(0, NG2) as i:
                    for u in range(2):
                        act.wait_ge(s2_["neg_ready"], 2 * i + u + 1)
                        act.activation(neg[u][:, :, :], neg[u][:, :, :], ACT.Exp).then_inc(s2_["exp_ready"], 1)

            @block.gpsimd
            def _(pool):
                with pool.Fori(0, NG2) as i:
                    for u in range(2):
                        n = 2 * i + u
                        pool.wait_ge(s2_["yn_ready"], n + 1)
                        pool.tensor_tensor(yn[u][:, :, :], yn[u][:, :, :], bcast(w("gamma"), 1, G), ALU.mult).then_inc(s2_["gamma_done"], 1)
                        pool.wait_ge(s2_["gamma_done"], n + 1)
                        pool.tensor_tensor(yn[u][:, :, :], yn[u][:, :, :], bcast(w("beta"), 1, G), ALU.add).then_inc(s2_["beta_done"], 1)

            @block.vector
            def _(dve):
                prime(dve, s2_["x_ready"])
                dve.wait_ge(s2_["ysd"], 1)
                dve.reciprocal(rstd[:, :], rstd[:, :]).then_inc(s2_["yrs"], 1)
                dve.wait_ge(s2_["yrs"], 1)
                with dve.Fori(0, NG2) as i:
                    for u in range(2):
                        n = 2 * i + u
                        for b in range(G):
                            g = n * G + b
                            m = dve.tensor_scalar(yn[u][:, b, :], Y[:, bass.ds(g, 1), :], ymean[:, bass.ds(g, 1)], rstd[:, bass.ds(g, 1)],
                                                  ALU.subtract, ALU.mult)
                        m.then_inc(s2_["yn_ready"], 1)
                    for u in range(2):
                        n = 2 * i + u
                        dve.wait_ge(s2_["beta_done"], n + 1)
                        dve.tensor_scalar(neg[u][:, :, :], yn[u][:, :, :], 0.0, None, ALU.min).then_inc(s2_["neg_ready"], 1)
                        dve.tensor_scalar(pos[u][:, :, :], yn[u][:, :, :], 0.0, None, ALU.max).then_inc(s2_["pos_ready"], 1)
                    for u in range(2):
                        n = 2 * i + u
                        dve.wait_ge(s2_["exp_ready"], n + 1)
                        dve.wait_ge(s2_["pos_ready"], n + 1)
                        dve.scalar_tensor_tensor(out=pos[u][:, :, :], in0=neg[u][:, :, :], scalar=-1.0, in1=pos[u][:, :, :],
                                                 op0=ALU.add, op1=ALU.add).then_inc(s2_["elu_ready"], 1)
                        dve.wait_ge(s2_["elu_ready"], n + 1)
                        residual(env, dve, n * G, G, pos[u][:, :, :], n, s2_["x_ready"], s2_["stat_step"])


def gated_layer(env):
    nc, X, w, ident, psum = (env[k] for k in ("nc", "X", "w", "ident", "psum"))
    mean, var, rstd = (env[k] for k in ("mean", "var", "rstd"))
    F32R = mybir.dt.float32r
    NI = GRAPHS // (2 * G)
    HALVES = 2 * STEPS
    R_BANK, Z_BANK, HN_BANK, IN_BANK = range(4)
    with ExitStack() as ctx:
        def one(name, shape, dt=F32):
            return ctx.enter_context(nc.sbuf_tensor("g_" + name, shape, dt))

        def sb(name, shape, dt=F32):
            return [one(f"{name}{u}", shape, dt) for u in range(2)]

        wg = one("wg", [P, STEPS, 3 * P])
        wg_hi, wg_lo = one("wg_hi", [P, STEPS, 3 * P], F32R), one("wg_lo", [P, STEPS, 3 * P], F32R)
        whh_hi, whh_lo = one("whh_hi", [P, 3 * P], F32R), one("whh_lo", [P, 3 * P], F32R)
        brz, nbz = one("brz", [P, 2]), one("nbz", [P, 1])
        adj_i, A = sb("adj_i", [P, G, P], I32), sb("A", [P, G, P])
        h0, h0T = sb("h0", [P, G, P]), sb("h0T", [P, G * P])
        hN, hT = sb("hN", [P, G, P]), sb("hT", [P, G * P])
        h_hi, h_lo = sb("h_hi", [P, G * P], F32R), sb("h_lo", [P, G * P], F32R)
        a_hi, a_lo = sb("a_hi", [P, G * P], F32R), sb("a_lo", [P, G * P], F32R)
        r, z, omz, zh, nn, tt = (sb(n, [P, G * P]) for n in ("r", "z", "omz", "zh", "n", "t"))
        o = sb("o", [P, G, P])

        def sem(name):
            return ctx.enter_context(nc.semaphore("g_" + name))

        adj_in = [sem("adj_in0"), sem("adj_in1")]
        stored = [sem("stored0"), sem("stored1")]
        names = ("a_ready", "sd", "rs", "wg_psum", "wg_ready", "whi_ready", "wlo_ready", "ln_ready", "h0_ready",
                 "h0T_psum", "h0T_ready", "hi_ready", "lo_ready", "agg", "ahi_ready", "alo_ready", "r_psum", "z_psum", "n_psum",
                 "r_ready", "z_ready", "omz_ready", "rh_ready", "t_ready", "zh_ready", "n_ready", "nz_ready", "new_ready",
                 "hN_psum", "hN_ready", "out_ready")
        s = {n: sem(n) for n in names}
        w_in = env["w_in"]

        def bank(u, k):
            return psum[:, 4 * u + k, :]

        def graphs(u, k):
            return psum[:, 4 * u + k, :].rearrange("p (b n) -> p b n", b=G)

        def each_half(eng, half):
            def turn(i, last):
                order = [(i, k, u, HALVES * i + 2 * k + u) for k in range(STEPS) for u in range(2)]
                order.append(None if last else (i + 1, 0, 0, HALVES * (i + 1)))
                for at, nxt in zip(order, order[1:]):
                    half(*at, nxt)
            turn(0, False)
            with eng.Fori(1, NI - 1) as i:
                turn(i, False)
            turn(NI - 1, True)

        def begun(i):
            return not (isinstance(i, int) and i == 0)

        def follows(i):
            return not (isinstance(i, int) and i == NI - 1)

        with nc.Block() as block:
            @block.sync
            def _(sp):
                prime(sp, *stored)

                def load_adj(i, u):
                    sp.dma_start(adj_i[u][:, :, :], env["adj"][:, bass.ds((2 * i + u) * G, G), :]).then_inc(adj_in[u], 16)

                def turn(i, last):
                    if not last:
                        for u in range(2):
                            sp.wait_ge(s["a_ready"], primed(2 * i + u + 1))
                            load_adj(i + 1, u)
                    for u in range(2):
                        n = 2 * i + u
                        sp.wait_ge(s["out_ready"], n + 1)
                        sp.dma_start(env["out"][:, bass.ds(n * G, G), :], o[u][:, :, :]).then_inc(stored[u], 16)

                for u in range(2):
                    load_adj(0, u)
                with sp.Fori(0, NI - 1) as i:
                    turn(i, False)
                turn(NI - 1, True)
                for u in range(2):
                    sp.wait_ge(stored[u], primed(16 * NI))

            @block.gpsimd
            def _(pool):
                prime(pool, s["a_ready"])

                def adjacency(n, u, i):
                    if begun(i):
                        pool.wait_ge(s["agg"], HALVES * i - 2 + u + 1)
                    pool.wait_ge(adj_in[u], 16 * i + 16)
                    settle(pool, env["passed"])
                    pool.tensor_scalar(A[u][:, :, :], adj_i[u][:, :, :], 1.0, 0.0, ALU.min, ALU.max).then_inc(s["a_ready"], 1)

                def relu(n, u):
                    pool.wait_ge(s["ln_ready"], n + 1)
                    settle(pool, env["passed"])
                    pool.tensor_scalar(h0[u][:, :, :], h0[u][:, :, :], 0.0, None, ALU.max).then_inc(s["h0_ready"], 1)

                def low_part(q, u, state):
                    pool.wait_ge(s["hi_ready"], q + 1)
                    pool.tensor_tensor(h_lo[u][:, :], state[u][:, :], h_hi[u][:, :], ALU.subtract).then_inc(s["lo_ready"], 1)

                def half(i, k, u, q, nxt):
                    if nxt and nxt[1] == 0:
                        low_part(nxt[3], nxt[2], h0T)
                    pool.wait_ge(s["z_ready"], q + 1)
                    pool.tensor_tensor(zh[u][:, :], z[u][:, :], (hT if k else h0T)[u][:, :], ALU.mult).then_inc(s["zh_ready"], 1)
                    if k < STEPS - 1:
                        low_part(q + 2, u, hT)
                    if k == 1 and follows(i):
                        relu(2 * (i + 1) + u, u)
                    if k == STEPS - 1 and follows(i):
                        adjacency(2 * (i + 1) + u, u, i + 1)

                for u in range(2):
                    relu(u, u)
                for u in range(2):
                    adjacency(u, u, 0)
                low_part(0, 0, h0T)
                each_half(pool, half)

            @block.tensor
            def _(pe):
                prime(pe, s["hN_psum"])
                pe.wait_ge(w_in, 16)
                for k in range(STEPS):
                    pe.matmul(psum[:, k, 0:3 * P], w("gwT")[:, k * P:(k + 1) * P], w("wih"), start=True, stop=True).then_inc(s["wg_psum"], 1)

                def gate(u, bank_, hi, lo, x_hi, x_lo, start, stop):
                    pe.matmul(bank(u, bank_), hi, x_hi[u][:, :], start=start, stop=False)
                    pe.matmul(bank(u, bank_), hi, x_lo[u][:, :], start=False, stop=False)
                    return pe.matmul(bank(u, bank_), lo, x_hi[u][:, :], start=False, stop=stop)

                def state_gates(u, q):
                    pe.wait_ge(s["hi_ready"], q + 1)
                    pe.wait_ge(s["lo_ready"], q + 1)
                    for b, stop in ((R_BANK, False), (Z_BANK, False), (HN_BANK, True)):
                        gate(u, b, whh_hi[:, b * P:(b + 1) * P], whh_lo[:, b * P:(b + 1) * P], h_hi, h_lo, True, stop)

                def input_gate(k, u, which, start):
                    cols = slice(which * P, (which + 1) * P)
                    return gate(u, (R_BANK, Z_BANK, IN_BANK)[which], wg_hi[:, k, cols], wg_lo[:, k, cols], a_hi, a_lo, start, True)

                def transpose_first(n, u, q, i):
                    pe.wait_ge(s["h0_ready"], n + 1)
                    if begun(i):
                        pe.wait_ge(s["t_ready"], q - 2 + 1)
                    for b in range(G):
                        m = pe.transpose(graphs(u, IN_BANK)[:, b, :], h0[u][:, b, :], ident)
                    m.then_inc(s["h0T_psum"], 1)

                def transpose_state(u, q):
                    pe.wait_ge(s["new_ready"], q + 1)
                    for b in range(G):
                        m = pe.transpose(graphs(u, IN_BANK)[:, b, :], hT[u][:, b * P:(b + 1) * P], ident)
                    m.then_inc(s["hN_psum"], 1)

                def aggregate(i, k, u, q):
                    n = 2 * i + u
                    if k == 0:
                        pe.wait_ge(s["a_ready"], primed(n + 1))
                        pe.wait_ge(s["h0T_ready"], n + 1)
                        if begun(i):
                            pe.wait_ge(s["out_ready"], n - 1)
                    else:
                        pe.wait_ge(s["hN_ready"], 2 * (STEPS - 1) * i + 2 * (k - 1) + u + 1)
                    src = hN if k else h0
                    for b in range(G):
                        m = pe.matmul(graphs(u, IN_BANK)[:, b, :], src[u][:, b, :], A[u][:, b, :], start=True, stop=True)
                    m.then_inc(s["agg"], 1)

                def half(i, k, u, q, nxt):
                    state_gates(u, q)
                    if nxt and nxt[1] == 0:
                        transpose_first(2 * nxt[0] + nxt[2], nxt[2], nxt[3], nxt[0])
                    pe.wait_ge(s["ahi_ready"], q + 1)
                    pe.wait_ge(s["alo_ready"], q + 1)
                    input_gate(k, u, 0, False).then_inc(s["r_psum"], 1)
                    input_gate(k, u, 1, False).then_inc(s["z_psum"], 1)
                    if nxt is None:
                        transpose_state(1 - u, q - 1)
                    elif nxt[1] > 0 or begun(nxt[0]):
                        if nxt[1] == 0:
                            pe.wait_ge(s["h0T_ready"], 2 * nxt[0] + nxt[2] + 1)
                        transpose_state(nxt[2], nxt[3] - 2)
                    input_gate(k, u, 2, True).then_inc(s["n_psum"], 1)
                    if nxt:
                        aggregate(*nxt)
                    else:
                        transpose_state(u, q)

                transpose_first(0, 0, 0, 0)
                aggregate(0, 0, 0, 0)
                pe.wait_ge(s["wlo_ready"], 2)
                each_half(pe, half)

            @block.scalar
            def _(act):
                act.activation(rstd[:, :], var[:, :], ACT.Sqrt, bias=env["epsc"][:, :]).then_inc(s["sd"], 1)
                act.activation(env["scratch"][:, :], env["epsc"][:, :], ACT.Sigmoid)

                def first_state(n, u):
                    act.wait_ge(s["h0T_psum"], n + 1)
                    act.activation(h0T[u][:, :], bank(u, IN_BANK), ACT.Copy).then_inc(s["h0T_ready"], 1)

                def aggregate_high(u, q):
                    act.wait_ge(s["agg"], q + 1)
                    act.activation(a_hi[u][:, :], bank(u, IN_BANK), ACT.Copy).then_inc(s["ahi_ready"], 1)

                def half(i, k, u, q, nxt):
                    if nxt and nxt[1] == 0:
                        first_state(2 * nxt[0] + nxt[2], nxt[2])
                    act.wait_ge(s["r_psum"], q + 1)
                    act.activation(r[u][:, :], bank(u, R_BANK), ACT.Sigmoid, bias=brz[:, 0:1]).then_inc(s["r_ready"], 1)
                    if nxt and nxt[1] > 0:
                        act.wait_ge(s["hN_psum"], primed(nxt[3] - 2 + 1))
                        act.activation(hN[nxt[2]][:, :, :], graphs(nxt[2], IN_BANK), ACT.Copy).then_inc(s["hN_ready"], 1)
                    act.wait_ge(s["z_psum"], q + 1)
                    act.activation(z[u][:, :], bank(u, Z_BANK), ACT.Sigmoid, bias=brz[:, 1:2]).then_inc(s["z_ready"], 1)
                    act.activation(omz[u][:, :], bank(u, Z_BANK), ACT.Sigmoid, bias=nbz[:, :], scale=-1.0).then_inc(s["omz_ready"], 1)
                    if nxt:
                        aggregate_high(nxt[2], nxt[3])
                    act.wait_ge(s["t_ready"], q + 1)
                    act.activation(nn[u][:, :], tt[u][:, :], ACT.Tanh, bias=w("bih")[:, 2:3]).then_inc(s["n_ready"], 1)

                first_state(0, 0)
                aggregate_high(0, 0)
                act.wait_ge(s["rs"], 3)
                each_half(act, half)

            @block.vector
            def _(dve):
                dve.wait_ge(s["sd"], 1)
                dve.reciprocal(rstd[:, :], rstd[:, :]).then_inc(s["rs"], 1)
                dve.tensor_tensor(brz[:, :], w("bih")[:, 0:2], w("bhh")[:, 0:2], ALU.add).then_inc(s["rs"], 1)
                dve.wait_ge(s["rs"], 2)
                dve.tensor_scalar(nbz[:, :], brz[:, 1:2], -1.0, None, ALU.mult).then_inc(s["rs"], 1)

                def normalise(n, u):
                    for b in range(G):
                        g = n * G + b
                        m = dve.tensor_scalar(h0[u][:, b, :], X[:, bass.ds(g, 1), :], mean[:, bass.ds(g, 1)], rstd[:, bass.ds(g, 1)],
                                              ALU.subtract, ALU.mult)
                    m.then_inc(s["ln_ready"], 1)

                def aggregate_low(u, q):
                    dve.wait_ge(s["ahi_ready"], q + 1)
                    dve.tensor_tensor(a_lo[u][:, :], bank(u, IN_BANK), a_hi[u][:, :], ALU.subtract).then_inc(s["alo_ready"], 1)

                def result(n, u, i, src):
                    dve.wait_ge(s["hN_psum"], primed(src + 1))
                    dve.wait_ge(stored[u], primed(16 * i))
                    dve.tensor_tensor(o[u][:, :, :], graphs(u, IN_BANK), X[:, bass.ds(n * G, G), :], ALU.add).then_inc(s["out_ready"], 1)

                def half(i, k, u, q, nxt):
                    if nxt and nxt[1] == 0:
                        dve.wait_ge(s["h0T_ready"], 2 * nxt[0] + nxt[2] + 1)
                        dve.tensor_copy(h_hi[nxt[2]][:, :], h0T[nxt[2]][:, :]).then_inc(s["hi_ready"], 1)
                    dve.wait_ge(s["r_ready"], q + 1)
                    dve.scalar_tensor_tensor(out=tt[u][:, :], in0=bank(u, HN_BANK), scalar=w("bhh")[:, 2:3], in1=r[u][:, :],
                                             op0=ALU.add, op1=ALU.mult).then_inc(s["rh_ready"], 1)
                    dve.wait_ge(s["n_psum"], q + 1)
                    dve.wait_ge(s["rh_ready"], q + 1)
                    dve.tensor_tensor(tt[u][:, :], tt[u][:, :], bank(u, IN_BANK), ALU.add).then_inc(s["t_ready"], 1)
                    if nxt is None:
                        result(2 * i + 1 - u, 1 - u, i, q - 1)
                    elif nxt[1] == 0 and begun(nxt[0]):
                        result(2 * (nxt[0] - 1) + nxt[2], nxt[2], nxt[0] - 1, nxt[3] - 2)
                    if nxt:
                        aggregate_low(nxt[2], nxt[3])
                    dve.wait_ge(s["n_ready"], q + 1)
                    dve.wait_ge(s["omz_ready"], q + 1)
                    dve.tensor_tensor(nn[u][:, :], nn[u][:, :], omz[u][:, :], ALU.mult).then_inc(s["nz_ready"], 1)
                    dve.wait_ge(s["nz_ready"], q + 1)
                    dve.wait_ge(s["zh_ready"], q + 1)
                    dve.tensor_tensor(hT[u][:, :], nn[u][:, :], zh[u][:, :], ALU.add).then_inc(s["new_ready"], 1)
                    if k < STEPS - 1:
                        dve.wait_ge(s["new_ready"], q + 1)
                        dve.tensor_copy(h_hi[u][:, :], hT[u][:, :]).then_inc(s["hi_ready"], 1)
                    if k == 1 and follows(i):
                        normalise(2 * (i + 1) + u, u)
                    if nxt is None:
                        result(2 * i + u, u, i, q)

                for u in range(2):
                    normalise(u, u)
                for k in range(STEPS):
                    dve.wait_ge(s["wg_psum"], k + 1)
                    dve.tensor_copy(wg[:, k, :], psum[:, k, 0:3 * P]).then_inc(s["wg_ready"], 1)
                dve.wait_ge(s["h0T_ready"], 1)
                dve.tensor_copy(h_hi[0][:, :], h0T[0][:, :]).then_inc(s["hi_ready"], 1)
                dve.wait_ge(s["wg_ready"], STEPS)
                dve.tensor_copy(wg_hi[:, :, :], wg[:, :, :]).then_inc(s["whi_ready"], 1)
                dve.tensor_copy(whh_hi[:, :], w("whh")).then_inc(s["whi_ready"], 1)
                dve.wait_ge(s["whi_ready"], 2)
                dve.tensor_tensor(wg_lo[:, :, :], wg[:, :, :], wg_hi[:, :, :], ALU.subtract).then_inc(s["wlo_ready"], 1)
                dve.tensor_tensor(whh_lo[:, :], w("whh"), whh_hi[:, :], ALU.subtract).then_inc(s["wlo_ready"], 1)
                aggregate_low(0, 0)
                each_half(dve, half)


def _pack(a):
    import numpy as np
    f = np.float32

    def by_feature(m):
        return m.reshape((H, HD) + m.shape[1:]).swapaxes(0, 1).reshape(m.shape)

    def rows(v):
        return np.broadcast_to(v, (P, v.shape[-1]))

    a1, a2 = a["L1_gnn_a"][:P], a["L1_gnn_a"][P:]
    adiag = np.zeros((P, 2 * H), f)
    sel = np.zeros((P, H, P), f)
    for h in range(H):
        adiag[h * HD:(h + 1) * HD, h] = a["L2_gnn_a1"]
        adiag[h * HD:(h + 1) * HD, H + h] = a["L2_gnn_a2"]
        sel[h::H, h, :] = 1.0
    parts = {
        "wq": by_feature(a["L0_gnn_Wq"]).T, "wk": by_feature(a["L0_gnn_Wk"]).T,
        "wv": a["L0_gnn_Wv"].T, "wo": a["L0_gnn_Wo"].T,
        "w1": a["L1_gnn_W"], "a1rep": np.broadcast_to(a1, (P, P)), "a2col": a2, "han": a["L1_gnn_han_w"],
        "w2": a["L2_gnn_W"], "w2T": a["L2_gnn_W"].T, "adiag": adiag, "emb": rows(a["L2_gnn_edge_emb"][1]),
        "gwT": a["L3_gnn_weight"].transpose(2, 0, 1).reshape(P, STEPS * P),
        "wih": a["L3_gnn_w_ih"].T, "whh": a["L3_gnn_w_hh"].T,
        "bq": by_feature(a["L0_gnn_bq"])[:, None], "bk": by_feature(a["L0_gnn_bk"])[:, None],
        "bih": a["L3_gnn_b_ih"].reshape(3, P).T, "bhh": a["L3_gnn_b_hh"].reshape(3, P).T,
        "bv": rows(a["L0_gnn_bv"]), "bo": rows(a["L0_gnn_bo"]), "hanb": rows(a["L1_gnn_han_b"]),
        "gamma": rows(a["L2_gnn_ln_gamma"]), "beta": rows(a["L2_gnn_ln_beta"]),
        "ident": np.eye(P, dtype=f), "sel": sel.reshape(P, H * P),
    }
    return np.ascontiguousarray(np.concatenate([parts[n] for n, _ in WEIGHTS], axis=1))


def _arrays(inputs):
    import numpy as np
    a = {k: np.asarray(v) for k, v in inputs.items()}
    return {
        "x": np.ascontiguousarray(a["x"].transpose(1, 0, 2)),
        "adj": np.ascontiguousarray(a["adj"].transpose(1, 0, 2)),
        "adjT": np.ascontiguousarray(a["adj"].transpose(2, 0, 1)),
        "wpack": _pack(a),
    }


def kernel(**inputs):
    import concourse.bacc as bacc
    import numpy as np
    from concourse.bass_utils import run_bass_kernel_spmd

    nc = bacc.Bacc("TRN2", target_bir_lowering=False, num_devices=1)
    arrays = _arrays(inputs)
    args = [nc.dram_tensor(n, v.shape, mybir.dt.from_np(v.dtype), kind="ExternalInput").ap() for n, v in arrays.items()]
    out = nc.dram_tensor("out", (P, GRAPHS, P), F32, kind="ExternalOutput").ap()
    graph_layers(nc, *args, out)
    got = run_bass_kernel_spmd(nc, [arrays], core_ids=[0]).results[0]["out"]
    return np.ascontiguousarray(np.asarray(got).transpose(1, 0, 2))
```

```python
from contextlib import ExitStack

import concourse.bass as bass
from concourse import mybir

F32 = mybir.dt.float32
BF16 = mybir.dt.bfloat16
F32R = mybir.dt.float32r
I32 = mybir.dt.int32
ALU = mybir.AluOpType
ACT = mybir.ActivationFunctionType
AX = mybir.AxisListType
RMAX = bass.bass_isa.ReduceOp.max

P = 128
GRAPHS = 64
G = 4
H = 8
HD = 16
HV = HD + 1
BIG = 1e30
STEPS = 3
EPS = 1e-5
SLOPE = 0.2

WEIGHTS = [("ident", P), ("wq", P), ("wk", P), ("wv", P), ("wo", P), ("bq", 1), ("bk", 1), ("bv", P), ("bo", P),
           ("sel", H * P),
           ("w1", P), ("a1rep", P), ("a2rep", P), ("han", P),
           ("w2", P), ("w2T", P), ("adiag", 2 * H), ("emb", H),
           ("gwT", STEPS * P), ("wih", 3 * P), ("whh", 3 * P),
           ("bih", 3), ("bhh", 3), ("hanb", P), ("gamma", P), ("beta", P)]
OFFSET = {}
_at = 0
for _name, _n in WEIGHTS:
    OFFSET[_name] = (_at, _n)
    _at += _n
NW = _at
NW_FIRST = OFFSET["w1"][0]


def bcast(ap, axis, n):
    a = ap.unsqueeze(axis)
    shape = list(a.shape)
    shape[axis] = n
    return a.broadcast_to(shape)


def primed(n):
    return n + 1


def prime(eng, *sems):
    for s in sems:
        eng.sem_inc(s, 1)


def settle(eng, passed):
    eng.sem_inc(passed, 1)


def graph_layers(nc, x, adj, adjT, wpack, out):
    with ExitStack() as ctx:
        def sb(name, shape, dt=F32):
            return ctx.enter_context(nc.sbuf_tensor(name, shape, dt))

        def sem(name):
            return ctx.enter_context(nc.semaphore(name))

        X = sb("X", [P, GRAPHS, P])
        W = sb("W", [P, NW])
        stats = sb("stats", [P, G, 6])
        aggregates = sb("aggregates", [P, G, 2])
        meanvar = sb("meanvar", [P, GRAPHS, 2])
        rstd = sb("rstd", [P, GRAPHS])
        shift = sb("shift", [P, GRAPHS])
        epsc = sb("epsc", [P, 1])
        scratch = sb("scratch", [P, 1])
        identb = sb("identb", [P, P], BF16)
        wg = sb("wg", [P, STEPS, 3 * P])
        wg_hi, wg_lo = sb("wg_hi", [P, STEPS, 3 * P], F32R), sb("wg_lo", [P, STEPS, 3 * P], F32R)
        whh_hi, whh_lo = sb("whh_hi", [P, 3 * P], F32R), sb("whh_lo", [P, 3 * P], F32R)
        psum = ctx.enter_context(nc.psum_tensor("psum", [P, 8, 512], F32))

        def w(name):
            a, n = OFFSET[name]
            return W[:, a:a + n]

        ident = w("ident")

        env = dict(nc=nc, x=x, adj=adj, adjT=adjT, wpack=wpack, out=out, X=X, W=W, w=w, ident=ident,
                   identb=identb, stats=stats, aggregates=aggregates, meanvar=meanvar, rstd=rstd, shift=shift, epsc=epsc,
                   psum=psum, scratch=scratch,
                   wg=wg, wg_hi=wg_hi, wg_lo=wg_lo, whh_hi=whh_hi, whh_lo=whh_lo,
                   wg_psum=sem("wg_psum"), wg_step=sem("wg_step"), sb=sb, sem=sem)
        attention_layer(env)
        column_layer(env)
        edge_layer(env)
        gated_layer(env)


def load(env, fills, ahead):
    nc, x, X, W, sem = (env[k] for k in ("nc", "x", "X", "W", "sem"))
    meanvar = env["meanvar"]
    CHUNK = 16
    NL = GRAPHS // CHUNK
    x_in, w_in = [sem("x_in0"), sem("x_in1")], sem("w_in")
    x_stats, x_mv = sem("x_stats"), sem("x_mv")
    const, filled = sem("const"), sem("filled")
    env["rest_in"] = sem("rest_in")
    env["passed"] = sem("passed")
    with ExitStack() as ctx, nc.Block() as block:
        stats = ctx.enter_context(nc.sbuf_tensor("l_stats", [P, CHUNK, 6], F32))
        aggregates = ctx.enter_context(nc.sbuf_tensor("l_aggregates", [P, CHUNK, 2], F32))

        @block.sync
        def _(sp):
            prime(sp, *x_in)
            with sp.Fori(0, NL // 2) as i:
                for odd in range(2):
                    sp.wait_ge(x_in[odd], primed(16 * i))
                    settle(sp, env["passed"])
                    at = (2 * i + odd) * CHUNK
                    sp.dma_start(X[:, bass.ds(at, CHUNK), :], x[:, bass.ds(at, CHUNK), :]).then_inc(x_in[odd], 16)
            ahead(sp)
            sp.dma_start(W[:, NW_FIRST:], env["wpack"][:, NW_FIRST:]).then_inc(env["rest_in"], 16)

        @block.scalar
        def _(act):
            act.wait_ge(x_in[0], primed(16))
            act.dma_start(W[:, 0:NW_FIRST], env["wpack"][:, 0:NW_FIRST]).then_inc(w_in, 16)
            act.wait_ge(const, 1)
            sqrt_table(act, env)
            act.wait_ge(w_in, 16)

        @block.gpsimd
        def _(pool):
            for buffer, value in fills:
                pool.memset(buffer, value).then_inc(filled, 1)
            pool.wait_ge(filled, len(fills))

        @block.vector
        def _(dve):
            prime(dve, x_mv)
            dve.memset(env["epsc"][:, :], EPS).then_inc(const, 1)
            with dve.Fori(0, NL // 2) as i:
                for odd in range(2):
                    c = 2 * i + odd
                    dve.wait_ge(x_mv, primed(2 * c))
                    dve.wait_ge(x_in[odd], primed(16 * i + 16))
                    settle(dve, env["passed"])
                    for b in range(CHUNK):
                        m = dve.bn_stats(stats[:, b, :], X[:, bass.ds(c * CHUNK + b, 1), :])
                    m.then_inc(x_stats, 1)
                    dve.wait_ge(x_stats, c + 1)
                    settle(dve, env["passed"])
                    for b in range(CHUNK):
                        m = dve.bn_aggr(aggregates[:, b, :], stats[:, b, :])
                    m.then_inc(x_mv, 1)
                    dve.wait_ge(x_mv, primed(2 * c + 1))
                    dve.tensor_copy(meanvar[:, bass.ds(c * CHUNK, CHUNK), :], aggregates[:, :, :]).then_inc(x_mv, 1)
            dve.wait_ge(w_in, 16)
            dve.tensor_copy(env["identb"][:, :], env["ident"]).then_inc(const, 1)
            dve.wait_ge(const, 2)
            dve.wait_ge(x_mv, primed(2 * NL))


def attention_layer(env):
    nc, X, w, ident, identb, psum = (env[k] for k in ("nc", "X", "w", "ident", "identb", "psum"))
    meanvar, rstd = env["meanvar"], env["rstd"]
    NG = GRAPHS // G
    Q_PARTS = (0, 0, 1, 0, 2, 1)
    K_PARTS = (0, 1, 0, 2, 0, 1)
    TERMS = len(Q_PARTS)
    VS = 64
    VCOLS = (H - 1) * HV + VS
    with ExitStack() as ctx:
        def one(name, shape, dt=F32):
            return ctx.enter_context(nc.sbuf_tensor("a_" + name, shape, dt))

        def sb(name, shape, dt=F32):
            return [one(f"{name}{u}", shape, dt) for u in range(2)]

        adj_i, adjT_i = sb("adj_i", [P, G, P], I32), sb("adjT_i", [P, G, P], I32)
        maskN, maskT = sb("maskN", [P, G, P], BF16), sb("maskT", [P, G, P], BF16)
        selb = one("selb", [P, H, P], BF16)
        hN, hT = one("hN", [P, G, P]), one("hT", [P, G * P])
        qk = sb("qk", [P, G * P])
        rem = sb("rem", [P, G * P])
        parts = sb("parts", [P, 3, G * P], BF16)
        stack = [sb("stackq", [P, H, G * P], BF16), sb("stackk", [P, H, G * P], BF16)]
        V = sb("V", [P, G, VCOLS])
        negmax, mparts = sb("negmax", [P, H]), sb("mparts", [P, 2 * H], BF16)
        mT = sb("mT", [P, P], BF16)
        PT = sb("PT", [P, H, P])
        rden = sb("rden", [P, H])
        O, OT = sb("O", [P, P]), sb("OT", [P, P])

        names = ("sd", "rs", "sel_ready", "mask_ready", "ln_ready", "bias_added", "hT_psum", "hT_ready",
                 "q_psum", "k_psum", "v_psum", "qk_ready", "hi_ready", "rem_ready", "mid_ready", "lo_ready", "v_ready",
                 "scores", "max_ready", "mhi_ready", "mparts_ready", "mT_psum", "mT_ready", "scoresT", "exp_ready",
                 "pv", "rden_ready", "o_ready", "oT_psum", "oT_ready", "y_psum", "x_ready", "stat_step")
        s = {n: ctx.enter_context(nc.semaphore("a_" + n)) for n in names}
        adj_in = [ctx.enter_context(nc.semaphore(f"a_adj_in{u}")) for u in range(2)]
        stacked = [ctx.enter_context(nc.semaphore(f"a_stacked{u}")) for u in range(2)]

        def load_adj(sp, g, par):
            sp.dma_start(adj_i[par][:, :, :], env["adj"][:, bass.ds(g * G, G), :]).then_inc(adj_in[par], 16)
            sp.dma_start(adjT_i[par][:, :, :], env["adjT"][:, bass.ds(g * G, G), :]).then_inc(adj_in[par], 16)

        fills = [(stack[c][par][:, :, :], 0.0) for c in range(2) for par in range(2)]
        fills += [(V[par][:, :, :], 1.0) for par in range(2)] + [(mT[par][:, :], 0.0) for par in range(2)]
        load(env, fills, lambda sp: load_adj(sp, 0, 0))

        def each_group(eng, before, turn):
            before()
            turn(0, 0, True, 2)
            with eng.Fori(0, NG // 2 - 2) as i:
                turn(2 * i + 1, 1, False, 2)
                turn(2 * i + 2, 0, False, 2)
            turn(NG - 3, 1, False, 2)
            turn(NG - 2, 0, False, 1)
            turn(NG - 1, 1, False, 0)

        def slot(k):
            return psum[:, 2 * (k % 2):2 * (k % 2) + 2, :].rearrange("p a (h n) -> p (a h) n", h=H // 2)

        with nc.Block() as block:
            @block.sync
            def _(sp):
                def adj_again(g, par):
                    if not isinstance(g, int) or g >= 2:
                        sp.wait_ge(s["mask_ready"], primed(2 * (g - 1)))
                        settle(sp, env["passed"])
                    load_adj(sp, g, par)

                def stack_parts(g, par):
                    if not isinstance(g, int) or g >= 2:
                        sp.wait_ge(s["scoresT"], primed(G * (g - 1)))
                        settle(sp, env["passed"])
                    for part, ready in enumerate(("hi_ready", "mid_ready", "lo_ready")):
                        for c, order in ((0, Q_PARTS), (1, K_PARTS)):
                            sp.wait_ge(s[ready], primed(2 * g + c + 1))
                            settle(sp, env["passed"])
                            for t in range(TERMS):
                                if order[t] == part:
                                    sp.dma_start(stack[c][par][t * HD:(t + 1) * HD, :, :], parts[c][:, part, :]).then_inc(stacked[par], 16)

                def before():
                    prime(sp, *stacked)
                    stack_parts(0, 0)

                def turn(g, par, first, left):
                    if left:
                        adj_again(g + 1, 1 - par)
                        stack_parts(g + 1, 1 - par)

                each_group(sp, before, turn)
                sp.wait_ge(env["rest_in"], 16)

            @block.gpsimd
            def _(pool):
                def masks(g, par):
                    if not isinstance(g, int) or g >= 2:
                        pool.wait_ge(s["scoresT"], primed(G * (g - 1)))
                    for k, (m, a) in enumerate(((maskN, adj_i), (maskT, adjT_i))):
                        if k == 0:
                            pool.wait_ge(adj_in[par], 16 * (g - par + 2))
                            settle(pool, env["passed"])
                        pool.tensor_scalar(m[par][:, :, :], a[par][:, :, :], BIG, -BIG, ALU.mult, ALU.add).then_inc(s["mask_ready"], 1)

                def last_parts(g):
                    for c in range(2):
                        pool.wait_ge(s["mid_ready"], primed(2 * g + c + 1))
                        pool.tensor_tensor(parts[c][:, 2, :], rem[c][:, :], parts[c][:, 1, :], ALU.subtract).then_inc(s["lo_ready"], 1)

                def add_bias(g):
                    pool.wait_ge(s["ln_ready"], g + 1)
                    xg = X[:, bass.ds(g * G, G), :]
                    pool.tensor_tensor(xg, xg, bcast(w("bo"), 1, G), ALU.add).then_inc(s["bias_added"], 1)

                def before():
                    prime(pool, s["mask_ready"], s["lo_ready"])
                    masks(0, 0)
                    last_parts(0)
                    add_bias(0)

                def turn(g, par, first, left):
                    if left:
                        masks(g + 1, 1 - par)
                        add_bias(g + 1)
                        last_parts(g + 1)

                each_group(pool, before, turn)

            @block.tensor
            def _(pe):
                def project(g, par, item):
                    if item == 0:
                        pe.wait_ge(s["ln_ready"], g + 1)
                        if not isinstance(g, int) or g >= 1:
                            pe.wait_ge(s["qk_ready"], 2 * g)
                            pe.wait_ge(s["hi_ready"], primed(2 * g))
                        for b in range(G):
                            m = pe.transpose(psum[:, 4, b * P:(b + 1) * P], hN[:, b, :], ident)
                        m.then_inc(s["hT_psum"], 1)
                    elif item == 1:
                        pe.wait_ge(s["hT_ready"], g + 1)
                        if not isinstance(g, int) or g >= 1:
                            pe.wait_ge(s["v_ready"], g)
                        pe.matmul(psum[:, 5, :], w("wq"), hT[:, :], start=True, stop=True).then_inc(s["q_psum"], 1)
                    elif item == 2:
                        pe.matmul(psum[:, 4, :], w("wk"), hT[:, :], start=True, stop=True).then_inc(s["k_psum"], 1)
                    else:
                        pe.wait_ge(s["qk_ready"], 2 * g + 1)
                        pe.wait_ge(s["hi_ready"], primed(2 * g + 1))
                        for b in range(G):
                            m = pe.matmul(psum[:, 5, b * P:(b + 1) * P], hT[:, b * P:(b + 1) * P], w("wv"), start=True, stop=True)
                        m.then_inc(s["v_psum"], 1)

                def scores(g, par, k):
                    n = G * g + k
                    if k == 0:
                        pe.wait_ge(s["mask_ready"], primed(2 * g + 2))
                        pe.wait_ge(stacked[par], primed(16 * TERMS * (g - par + 2)))
                    if not (isinstance(g, int) and g == 0 and k < 2):
                        pe.wait_ge(s["o_ready"], n - 1)
                    for a in range(2):
                        for h in range(H // 2):
                            hh = a * (H // 2) + h
                            pe.matmul(slot(k)[:, hh, :], stack[0][par][:, hh, k * P:(k + 1) * P], stack[1][par][:, hh, k * P:(k + 1) * P],
                                      start=(h == 0), stop=False, skip_group_check=True)
                        m = pe.matmul(psum[:, 2 * (k % 2) + a, :], identb[:, :], bcast(maskN[par][:, k, :], 1, H // 2),
                                      start=False, stop=True, skip_group_check=True)
                    m.then_inc(s["scores"], 1)

                def shift_rows(g, par, k):
                    n = G * g + k
                    pe.wait_ge(s["mparts_ready"], n + 1)
                    pe.transpose(psum[:, 2 * (k % 2), :].bitcast(BF16)[0:2 * H, 0:P], mparts[k % 2][:, :], identb[:, :]).then_inc(s["mT_psum"], 1)

                def scores_transposed(g, par, k):
                    n = G * g + k
                    pe.wait_ge(s["mT_ready"], n + 1)
                    for a in range(2):
                        for h in range(H // 2):
                            hh = a * (H // 2) + h
                            pe.matmul(slot(k)[:, hh, :], stack[1][par][:, hh, k * P:(k + 1) * P], stack[0][par][:, hh, k * P:(k + 1) * P],
                                      start=(h == 0), stop=False, skip_group_check=True)
                            pe.matmul(slot(k)[:, hh, :], selb[:, hh, :], mT[k % 2][:, :], start=False, stop=False, skip_group_check=True)
                        m = pe.matmul(psum[:, 2 * (k % 2) + a, :], identb[:, :], bcast(maskT[par][:, k, :], 1, H // 2),
                                      start=False, stop=True, skip_group_check=True)
                    m.then_inc(s["scoresT"], 1)

                def weighted_values(g, par, k):
                    n = G * g + k
                    pe.wait_ge(s["exp_ready"], n + 1)
                    if k == 0:
                        pe.wait_ge(s["v_ready"], g + 1)
                    for h in range(H):
                        m = pe.matmul(psum[:, 2 * (k % 2), h * VS:(h + 1) * VS], PT[k % 2][:, h, :], V[par][:, k, h * HV:h * HV + VS], start=True, stop=True)
                    m.then_inc(s["pv"], 1)

                def transpose_output(g, par, k):
                    n = G * g + k
                    pe.wait_ge(s["o_ready"], n + 1)
                    pe.transpose(psum[:, 6, 0:P], O[k % 2][:, :], ident).then_inc(s["oT_psum"], 1)

                def output(g, par, k):
                    n = G * g + k
                    pe.wait_ge(s["oT_ready"], n + 1)
                    if not (isinstance(g, int) and g == 0 and k == 0):
                        pe.wait_ge(s["x_ready"], primed(n))
                    pe.matmul(psum[:, 7, 0:P], OT[k % 2][:, :], w("wo"), start=True, stop=True).then_inc(s["y_psum"], 1)

                def before():
                    prime(pe, s["scoresT"], s["pv"])
                    for item in range(4):
                        project(0, 0, item)
                    project(1, 1, 0)
                    pe.wait_ge(s["sel_ready"], 1)

                def unit_before(g, par, k, back):
                    return (g, par, k - back) if k >= back else (g - 1, 1 - par, k - back + G)

                def turn(g, par, first, left):
                    for k in range(G):
                        scores(g, par, k)
                        if not first or k >= 2:
                            output(*unit_before(g, par, k, 2))
                        if not first or k >= 1:
                            weighted_values(*unit_before(g, par, k, 1))
                        shift_rows(g, par, k)
                        if left:
                            for item in ((1, 2), (3,), (), ())[k]:
                                project(g + 1, 1 - par, item)
                        if left == 2 and k == 3:
                            project(g + 2, par, 0)
                        if not first or k >= 1:
                            transpose_output(*unit_before(g, par, k, 1))
                        scores_transposed(g, par, k)
                    if not left:
                        output(g, par, G - 2)
                        weighted_values(g, par, G - 1)
                        transpose_output(g, par, G - 1)
                        output(g, par, G - 1)

                each_group(pe, before, turn)

            @block.scalar
            def _(act):
                def relu(g):
                    if not isinstance(g, int) or g >= 1:
                        act.wait_ge(s["v_psum"], g)
                    act.wait_ge(s["hT_psum"], g + 1)
                    act.activation(hT[:, :], psum[:, 4, :], ACT.Relu).then_inc(s["hT_ready"], 1)

                def evacuate(g, par, c):
                    if not isinstance(g, int) or g >= 1:
                        act.wait_ge(s["rem_ready"], 2 * (g - 1) + c + 1)
                        act.wait_ge(stacked[1 - par], primed(16 * TERMS * (g + par)))
                    bank, bias, scale = ((5, w("bq"), 1.0 / 4), (4, w("bk"), 1.0))[c]
                    act.wait_ge(s[("q_psum", "k_psum")[c]], g + 1)
                    act.activation(parts[c][:, 0, :], psum[:, bank, :], ACT.Identity, bias=bias, scale=scale).then_inc(s["hi_ready"], 1)
                    act.activation(qk[c][:, :], psum[:, bank, :], ACT.Identity, bias=bias, scale=scale).then_inc(s["qk_ready"], 1)

                def shift_ready(g, k):
                    n = G * g + k
                    act.wait_ge(s["mT_psum"], n + 1)
                    act.activation(mT[k % 2][0:2 * H, :], psum[:, 2 * (k % 2), :].bitcast(BF16)[0:2 * H, 0:P], ACT.Copy).then_inc(s["mT_ready"], 1)

                def weights(g, k):
                    n = G * g + k
                    act.wait_ge(s["scoresT"], primed(n + 1))
                    act.activation(PT[k % 2][:, :, :], slot(k), ACT.Exp).then_inc(s["exp_ready"], 1)

                def output_ready(g, k):
                    n = G * g + k
                    act.wait_ge(s["oT_psum"], n + 1)
                    act.activation(OT[k % 2][:, :], psum[:, 6, 0:P], ACT.Copy).then_inc(s["oT_ready"], 1)

                def before():
                    prime(act, s["hi_ready"])
                    act.wait_ge(s["rs"], 3)
                    relu(0)
                    evacuate(0, 0, 0)
                    evacuate(0, 0, 1)
                    relu(1)

                def turn(g, par, first, left):
                    for k in range(G):
                        shift_ready(g, k)
                        if left and k == 0:
                            evacuate(g + 1, 1 - par, 0)
                        if not first or k >= 1:
                            output_ready(*((g, k - 1) if k else (g - 1, G - 1)))
                        weights(g, k)
                        if left and k == 0:
                            evacuate(g + 1, 1 - par, 1)
                        if left == 2 and k == 3:
                            relu(g + 2)
                    if not left:
                        output_ready(g, G - 1)

                deviations(act, env, s["sd"])
                each_group(act, before, turn)
                sqrt_table(act, env)

            @block.vector
            def _(dve):
                def normalise(g):
                    if not isinstance(g, int) or g >= 1:
                        dve.wait_ge(s["hT_psum"], g)
                    for b in range(G):
                        gb = g * G + b
                        m = dve.tensor_scalar(hN[:, b, :], X[:, bass.ds(gb, 1), :], meanvar[:, bass.ds(gb, 1), 0], rstd[:, bass.ds(gb, 1)],
                                              ALU.subtract, ALU.mult)
                    m.then_inc(s["ln_ready"], 1)

                def remainder(g, c):
                    if not isinstance(g, int) or g >= 1:
                        dve.wait_ge(s["lo_ready"], primed(2 * (g - 1) + c + 1))
                    dve.wait_ge(s["qk_ready"], 2 * g + c + 1)
                    dve.wait_ge(s["hi_ready"], primed(2 * g + c + 1))
                    dve.tensor_tensor(rem[c][:, :], qk[c][:, :], parts[c][:, 0, :], ALU.subtract).then_inc(s["rem_ready"], 1)
                    dve.wait_ge(s["rem_ready"], 2 * g + c + 1)
                    dve.tensor_copy(parts[c][:, 1, :], rem[c][:, :]).then_inc(s["mid_ready"], 1)

                def values(g, par):
                    dve.wait_ge(s["v_psum"], g + 1)
                    if not isinstance(g, int) or g >= 2:
                        dve.wait_ge(s["pv"], primed(G * (g - 1)))
                    dve.tensor_tensor(V[par][:, :, 0:H * HV].rearrange("p b (h d) -> p b h d", h=H)[:, :, :, 0:HD], psum[:, 5, :].rearrange("p (b h d) -> p b h d", b=G, h=H),
                                      bcast(w("bv").rearrange("p (h d) -> p h d", h=H), 1, G), ALU.add).then_inc(s["v_ready"], 1)

                def maxima(g, k):
                    n = G * g + k
                    dve.wait_ge(s["scores"], n + 1)
                    dve.tensor_reduce(negmax[k % 2][:, :], slot(k), AX.X, ALU.max, negate=True).then_inc(s["max_ready"], 1)
                    dve.wait_ge(s["max_ready"], n + 1)
                    dve.tensor_copy(mparts[k % 2][:, 0:H], negmax[k % 2][:, :]).then_inc(s["mhi_ready"], 1)
                    dve.wait_ge(s["mhi_ready"], n + 1)
                    dve.tensor_tensor(mparts[k % 2][:, H:2 * H], negmax[k % 2][:, :], mparts[k % 2][:, 0:H], ALU.subtract).then_inc(s["mparts_ready"], 1)

                def normalise_output(g, k):
                    n = G * g + k
                    dve.wait_ge(s["pv"], primed(n + 1))
                    y = psum[:, 2 * (k % 2), :].rearrange("p (h d) -> p h d", h=H)
                    dve.reciprocal(rden[k % 2][:, :], y[:, :, HD]).then_inc(s["rden_ready"], 1)
                    dve.wait_ge(s["rden_ready"], n + 1)
                    dve.tensor_tensor(O[k % 2][:, :].rearrange("p (h d) -> p h d", h=H), y[:, :, 0:HD],
                                      bcast(rden[k % 2][:, :], 2, HD), ALU.mult).then_inc(s["o_ready"], 1)

                def add_to_x(g, k):
                    n = G * g + k
                    dve.wait_ge(s["y_psum"], n + 1)
                    if k == 0:
                        dve.wait_ge(s["bias_added"], g + 1)
                    xu = X[:, bass.ds(n, 1), :]
                    dve.tensor_tensor(xu, psum[:, 7, 0:P].unsqueeze(1), xu, ALU.add).then_inc(s["x_ready"], 1)

                def before():
                    prime(dve, s["x_ready"], s["mid_ready"], s["stat_step"])
                    normalisers(dve, env, s["sd"], s["rs"])
                    dve.tensor_scalar(w("bq"), w("bq"), 1.0 / 4, None, ALU.mult).then_inc(s["rs"], 1)
                    dve.wait_ge(s["rs"], 2)
                    normalise(0)
                    dve.tensor_copy(selb[:, :, :], w("sel").rearrange("p (h n) -> p h n", h=H)).then_inc(s["sel_ready"], 1)
                    remainder(0, 0)
                    remainder(0, 1)
                    values(0, 0)
                    normalise(1)

                def turn(g, par, first, left):
                    for k in range(G):
                        maxima(g, k)
                        if not first or k >= 2:
                            add_to_x(*((g, k - 2) if k >= 2 else (g - 1, k + G - 2)))
                        if not first or k >= 1:
                            normalise_output(*((g, k - 1) if k else (g - 1, G - 1)))
                        if left and k == 1:
                            remainder(g + 1, 0)
                            remainder(g + 1, 1)
                        if left and k == 2:
                            values(g + 1, 1 - par)
                        if left == 2 and k == 2:
                            normalise(g + 2)
                        if not first and k == 3:
                            group_statistics(env, dve, g - 1, s["x_ready"], s["stat_step"])
                    if not left:
                        add_to_x(g, G - 2)
                        normalise_output(g, G - 1)
                        add_to_x(g, G - 1)
                        group_statistics(env, dve, g, s["x_ready"], s["stat_step"])
                        dve.wait_ge(s["stat_step"], primed(3 * NG))

                each_group(dve, before, turn)


def group_statistics(env, dve, g, x_ready, stat_step):
    dve.wait_ge(x_ready, primed(G * (g + 1)))
    row_statistics(env, dve, env["X"], g, env["meanvar"], stat_step)


def row_statistics(env, dve, source, g, meanvar, step):
    row_moments(env, dve, source, g, step)
    row_aggregates(env, dve, g, step)
    row_saved(env, dve, g, meanvar, step)


def row_moments(env, dve, source, g, step):
    dve.wait_ge(step, primed(3 * g))
    settle(dve, env["passed"])
    for b in range(G):
        m = dve.bn_stats(env["stats"][:, b, :], source[:, bass.ds(g * G + b, 1), :])
    m.then_inc(step, 1)


def row_aggregates(env, dve, g, step):
    dve.wait_ge(step, primed(3 * g + 1))
    settle(dve, env["passed"])
    for b in range(G):
        m = dve.bn_aggr(env["aggregates"][:, b, :], env["stats"][:, b, :])
    m.then_inc(step, 1)


def row_saved(env, dve, g, meanvar, step):
    dve.wait_ge(step, primed(3 * g + 2))
    dve.tensor_copy(meanvar[:, bass.ds(g * G, G), :], env["aggregates"][:, :, :]).then_inc(step, 1)


def in_pairs(eng, before, turn):
    NG = GRAPHS // G
    before()
    for g in range(4):
        turn(g, g % 2, 2)
    with eng.Fori(2, NG // 2 - 1) as i:
        turn(2 * i, 0, 2)
        turn(2 * i + 1, 1, 2)
    turn(NG - 2, 0, 1)
    turn(NG - 1, 1, 0)


def begun(g, n):
    return not isinstance(g, int) or g >= n


def column_layer(env):
    nc, X, w, ident, identb, psum = (env[k] for k in ("nc", "X", "w", "ident", "identb", "psum"))
    meanvar, rstd, shift = (env[k] for k in ("meanvar", "rstd", "shift"))
    TB, ZB, VB, AB = range(4)
    with ExitStack() as ctx:
        def one(name, shape, dt=F32):
            return ctx.enter_context(nc.sbuf_tensor("c_" + name, shape, dt))

        def sb(name, shape, dt=F32):
            return [one(f"{name}{u}", shape, dt) for u in range(2)]

        adjT_i, maskT = sb("adjT_i", [P, G, P], I32), sb("maskT", [P, G, P], BF16)
        hN, hT = one("hN", [P, G, P]), sb("hT", [P, G * P])
        E, PT = sb("E", [P, G, P]), sb("PT", [P, G, P])
        negmax, den, rden = sb("negmax", [P, G]), sb("den", [P, G]), sb("rden", [P, G])
        hs = sb("hs", [P, G, P])
        pos, exp, hid, hidT = (one(n, [P, G, P]) for n in ("pos", "exp", "hid", "hidT"))

        adj_in = [ctx.enter_context(nc.semaphore(f"c_adj_in{u}")) for u in range(2)]
        names = ("mask_ready", "sd_ready", "rs_ready", "ln_ready", "bias_added", "hT_psum", "hT_ready", "z_psum", "v_psum",
                 "sloped", "leaky_ready", "max_ready", "exp_ready", "rden_ready", "hs_ready", "att", "pos_ready", "yexp_ready",
                 "hid_ready", "hidT_psum", "hidT_ready", "y_psum", "x_ready", "stat_step")
        s = {n: ctx.enter_context(nc.semaphore("c_" + n)) for n in names}

        def bank(u, k):
            return psum[:, 4 * u + k, :]

        def graphs(u, k):
            return psum[:, 4 * u + k, :].rearrange("p (b n) -> p b n", b=G)

        with nc.Block() as block:
            @block.sync
            def _(sp):
                def load_adj(g, par):
                    if begun(g, 2):
                        sp.wait_ge(s["mask_ready"], g - 1)
                        settle(sp, env["passed"])
                    sp.dma_start(adjT_i[par][:, :, :], env["adjT"][:, bass.ds(g * G, G), :]).then_inc(adj_in[par], 16)

                def turn(g, par, left):
                    if left:
                        load_adj(g + 1, 1 - par)

                in_pairs(sp, lambda: load_adj(0, 0), turn)

            @block.gpsimd
            def _(pool):
                def mask(g, par):
                    if begun(g, 2):
                        pool.wait_ge(s["z_psum"], g - 1)
                    pool.wait_ge(adj_in[par], 8 * (g - par) + 16)
                    settle(pool, env["passed"])
                    pool.tensor_scalar(maskT[par][:, :, :], adjT_i[par][:, :, :], BIG, -BIG, ALU.mult, ALU.add).then_inc(s["mask_ready"], 1)

                def turn(g, par, left):
                    if left:
                        mask(g + 1, 1 - par)
                    pool.wait_ge(s["ln_ready"], g + 1)
                    xg = X[:, bass.ds(g * G, G), :]
                    pool.tensor_tensor(xg, xg, bcast(w("hanb"), 1, G), ALU.add).then_inc(s["bias_added"], 1)

                in_pairs(pool, lambda: mask(0, 0), turn)

            @block.tensor
            def _(pe):
                def transpose_input(g, par):
                    pe.wait_ge(s["ln_ready"], g + 1)
                    if begun(g, 4):
                        pe.wait_ge(s["hidT_ready"], primed(g - 3))
                    for b in range(G):
                        m = pe.transpose(graphs(par, TB)[:, b, :], hN[:, b, :], ident)
                    m.then_inc(s["hT_psum"], 1)

                def scores(g, par):
                    pe.wait_ge(s["hT_ready"], g + 1)
                    if begun(g, 2):
                        pe.wait_ge(s["leaky_ready"], g - 1)
                    pe.matmul(bank(par, ZB), w("a1rep"), hT[par][:, :], start=True, stop=False, skip_group_check=True)
                    for b in range(G):
                        pe.matmul(graphs(par, ZB)[:, b, :], hT[par][:, b * P:(b + 1) * P], w("a2rep"), start=False, stop=False, skip_group_check=True)
                    pe.wait_ge(s["mask_ready"], g + 1)
                    pe.matmul(bank(par, ZB), identb[:, :], maskT[par][:, :, :].rearrange("p b n -> p (b n)"),
                              start=False, stop=True, skip_group_check=True).then_inc(s["z_psum"], 1)

                def values(g, par):
                    if begun(g, 2):
                        pe.wait_ge(s["hs_ready"], g - 1)
                    for b in range(G):
                        m = pe.matmul(graphs(par, VB)[:, b, :], hT[par][:, b * P:(b + 1) * P], w("w1"), start=True, stop=True)
                    m.then_inc(s["v_psum"], 1)

                def attend(g, par):
                    pe.wait_ge(s["hs_ready"], g + 1)
                    if begun(g, 2):
                        pe.wait_ge(s["x_ready"], primed(g - 1))
                    for b in range(G):
                        m = pe.matmul(graphs(par, AB)[:, b, :], PT[par][:, b, :], hs[par][:, b, :], start=True, stop=True)
                    m.then_inc(s["att"], 1)

                def transpose_hidden(g, par):
                    pe.wait_ge(s["hid_ready"], g + 1)
                    for b in range(G):
                        m = pe.transpose(graphs(par, TB)[:, b, :], hid[:, b, :], ident)
                    m.then_inc(s["hidT_psum"], 1)

                def output(g, par):
                    pe.wait_ge(s["hidT_ready"], primed(g + 1))
                    for b in range(G):
                        m = pe.matmul(graphs(par, AB)[:, b, :], hidT[:, b, :], w("han"), start=True, stop=True)
                    m.then_inc(s["y_psum"], 1)

                def turn(g, par, left):
                    scores(g, par)
                    if begun(g, 2):
                        transpose_hidden(g - 2, par)
                    if left:
                        transpose_input(g + 1, 1 - par)
                    if begun(g, 1):
                        attend(g - 1, 1 - par)
                    if begun(g, 2):
                        output(g - 2, par)
                    values(g, par)
                    if not left:
                        transpose_hidden(g - 1, 1 - par)
                        attend(g, par)
                        output(g - 1, 1 - par)
                        transpose_hidden(g, par)
                        output(g, par)

                in_pairs(pe, lambda: transpose_input(0, 0), turn)

            @block.scalar
            def _(act):
                def normalise(g):
                    if begun(g, 1):
                        act.wait_ge(s["hT_psum"], g)
                    for b in range(G):
                        gb = g * G + b
                        m = act.activation(hN[:, b:b + 1, :], X[:, bass.ds(gb, 1), :], ACT.Relu,
                                           bias=shift[:, bass.ds(gb, 1)], scale=rstd[:, bass.ds(gb, 1)])
                    m.then_inc(s["ln_ready"], 1)

                def transposed(g, par):
                    if begun(g, 2):
                        act.wait_ge(s["v_psum"], g - 1)
                    act.wait_ge(s["hT_psum"], g + 1)
                    act.activation(hT[par][:, :], bank(par, TB), ACT.Copy).then_inc(s["hT_ready"], 1)

                def slope(g, par):
                    act.wait_ge(s["z_psum"], g + 1)
                    act.activation(E[par][:, :, :], graphs(par, ZB), ACT.Copy, scale=SLOPE).then_inc(s["sloped"], 1)

                def weights(g, par):
                    if begun(g, 2):
                        act.wait_ge(s["att"], g - 1)
                    act.wait_ge(s["max_ready"], g + 1)
                    for b in range(G):
                        m = act.activation(PT[par][:, b, :], E[par][:, b, :], ACT.Exp, bias=negmax[par][:, b:b + 1],
                                           accum_out=den[par][:, b:b + 1])
                    m.then_inc(s["exp_ready"], 1)

                def elu_exponential(g, par):
                    if begun(g, 1):
                        act.wait_ge(s["hid_ready"], g)
                    act.wait_ge(s["pos_ready"], g + 1)
                    act.activation(exp[:, :, :], graphs(par, AB), ACT.Exp).then_inc(s["yexp_ready"], 1)

                def hidden_copy(g, par):
                    if begun(g, 1):
                        act.wait_ge(s["y_psum"], g)
                    act.wait_ge(s["hidT_psum"], g + 1)
                    act.activation(hidT[:, :, :], graphs(par, TB), ACT.Copy).then_inc(s["hidT_ready"], 1)

                def before():
                    prime(act, s["hidT_ready"])
                    act.wait_ge(s["rs_ready"], 2)
                    normalise(0)
                    transposed(0, 0)
                    normalise(1)

                def turn(g, par, left):
                    slope(g, par)
                    if begun(g, 2):
                        hidden_copy(g - 2, par)
                    if left:
                        transposed(g + 1, 1 - par)
                    weights(g, par)
                    if begun(g, 1):
                        elu_exponential(g - 1, 1 - par)
                    if left == 2:
                        normalise(g + 2)
                    if not left:
                        hidden_copy(g - 1, 1 - par)
                        elu_exponential(g, par)
                        hidden_copy(g, par)

                deviations(act, env, s["sd_ready"])
                in_pairs(act, before, turn)
                sqrt_table(act, env)

            @block.vector
            def _(dve):
                def largest(g, par):
                    dve.wait_ge(s["sloped"], g + 1)
                    dve.tensor_tensor(E[par][:, :, :], graphs(par, ZB), E[par][:, :, :], ALU.max).then_inc(s["leaky_ready"], 1)
                    dve.wait_ge(s["leaky_ready"], g + 1)
                    dve.tensor_reduce(negmax[par][:, :], E[par][:, :, :], AX.X, ALU.max, negate=True).then_inc(s["max_ready"], 1)

                def inverses(g, par):
                    dve.wait_ge(s["exp_ready"], g + 1)
                    dve.reciprocal(rden[par][:, :], den[par][:, :]).then_inc(s["rden_ready"], 1)

                def scaled_values(g, par):
                    if begun(g, 2):
                        dve.wait_ge(s["att"], g - 1)
                    dve.wait_ge(s["v_psum"], g + 1)
                    dve.wait_ge(s["rden_ready"], g + 1)
                    dve.tensor_tensor(hs[par][:, :, :], graphs(par, VB), bcast(rden[par][:, :], 2, P), ALU.mult).then_inc(s["hs_ready"], 1)

                def positive(g, par):
                    if begun(g, 1):
                        dve.wait_ge(s["hid_ready"], g)
                    dve.wait_ge(s["att"], g + 1)
                    dve.tensor_scalar(pos[:, :, :], graphs(par, AB), 0.0, -1.0, ALU.max, ALU.add).then_inc(s["pos_ready"], 1)

                def hidden(g, par):
                    if begun(g, 1):
                        dve.wait_ge(s["hidT_psum"], g)
                    dve.wait_ge(s["yexp_ready"], g + 1)
                    dve.scalar_tensor_tensor(out=hid[:, :, :], in0=exp[:, :, :], scalar=1.0, in1=pos[:, :, :],
                                             op0=ALU.min, op1=ALU.add).then_inc(s["hid_ready"], 1)

                def add_to_x(g, par):
                    dve.wait_ge(s["y_psum"], g + 1)
                    dve.wait_ge(s["bias_added"], g + 1)
                    xg = X[:, bass.ds(g * G, G), :]
                    dve.tensor_tensor(xg, graphs(par, AB), xg, ALU.add).then_inc(s["x_ready"], 1)

                def statistics(g):
                    dve.wait_ge(s["x_ready"], primed(g + 1))
                    row_statistics(env, dve, X, g, meanvar, s["stat_step"])

                def before():
                    prime(dve, s["x_ready"], s["stat_step"])
                    normalisers(dve, env, s["sd_ready"], s["rs_ready"])

                def turn(g, par, left):
                    largest(g, par)
                    if begun(g, 1):
                        positive(g - 1, 1 - par)
                    if begun(g, 3):
                        dve.wait_ge(s["x_ready"], primed(g - 2))
                        row_moments(env, dve, X, g - 3, s["stat_step"])
                    inverses(g, par)
                    if begun(g, 3):
                        row_aggregates(env, dve, g - 3, s["stat_step"])
                    scaled_values(g, par)
                    if begun(g, 3):
                        row_saved(env, dve, g - 3, meanvar, s["stat_step"])
                    if begun(g, 1):
                        hidden(g - 1, 1 - par)
                    if begun(g, 2):
                        add_to_x(g - 2, par)
                    if not left:
                        positive(g, par)
                        statistics(g - 2)
                        add_to_x(g - 1, 1 - par)
                        hidden(g, par)
                        statistics(g - 1)
                        add_to_x(g, par)
                        statistics(g)
                        dve.wait_ge(s["stat_step"], primed(3 * (g + 1)))

                in_pairs(dve, before, turn)


def sqrt_table(act, env):
    act.activation(env["scratch"][:, :], env["epsc"][:, :], ACT.Sqrt)


def deviations(act, env, sd_ready, source="meanvar", table=ACT.Exp):
    act.activation(env["rstd"][:, :], env[source][:, :, 1], ACT.Sqrt, bias=env["epsc"][:, :]).then_inc(sd_ready, 1)
    act.activation(env["scratch"][:, :], env["epsc"][:, :], table)


def normalisers(dve, env, sd_ready, rs_ready, source="meanvar"):
    rstd, shift = env["rstd"], env["shift"]
    dve.wait_ge(sd_ready, 1)
    dve.reciprocal(rstd[:, :], rstd[:, :]).then_inc(rs_ready, 1)
    dve.wait_ge(rs_ready, 1)
    dve.scalar_tensor_tensor(out=shift[:, :], in0=env[source][:, :, 0], scalar=-1.0, in1=rstd[:, :], op0=ALU.mult, op1=ALU.mult).then_inc(rs_ready, 1)


def edge_layer(env):
    nc, X, w, ident, identb, psum = (env[k] for k in ("nc", "X", "w", "ident", "identb", "psum"))
    meanvar, rstd, shift = (env[k] for k in ("meanvar", "rstd", "shift"))
    NG = GRAPHS // G
    PARTS = 3
    ROWS = P // G
    PROJ = P + 2 * H
    T_BANK, ROW_BANK = 6, 7
    RS = 64
    RCOLS = (H - 1) * 2 * HV + RS
    with ExitStack() as ctx:
        def one(name, shape, dt=F32):
            return ctx.enter_context(nc.sbuf_tensor("e_" + name, shape, dt))

        def sb(name, shape, dt=F32):
            return [one(f"{name}{u}", shape, dt) for u in range(2)]

        def sem(name):
            return ctx.enter_context(nc.semaphore("e_" + name))

        Y = one("Y", [P, GRAPHS, P])
        ymeanvar = one("ymeanvar", [P, GRAPHS, 2])
        wproj = one("wproj", [P, PROJ])
        selb = one("selb", [P, G, H, P], BF16)
        adjT_i, maskT, MT = sb("adjT_i", [P, G, P], I32), sb("maskT", [P, G, P], BF16), sb("MT", [P, G, P])
        hN, hT = one("hN", [P, G, P]), one("hT", [P, G * P])
        s1, s2, c, d, t, m8, m02, tm, t02, tm2 = (one(n, [P, G, H]) for n in ("s1", "s2", "c", "d", "t", "m8", "m", "tm", "t02", "tm2"))
        rem1, parts, rows = one("rem1", [P, G, H]), one("parts", [P, G, ROWS], BF16), sb("rows", [P, P], BF16)
        ns2, U = sb("ns2", [P, G, H]), sb("U", [P, G, H, 2])
        Rpad, R2 = sb("R", [P, G, RCOLS]), sb("R2", [P, G, H, HV])
        R = [a[:, :, 0:H * 2 * HV].rearrange("p b (h d) -> p b h d", h=H) for a in Rpad]
        V, E = sb("V", [P, G, P]), sb("E", [P, H, P])
        y12, yy, rden = sb("y12", [P, H, 2, HV]), sb("yy", [P, H, HV]), sb("rden", [P, H])

        adj_in = [sem("adj_in0"), sem("adj_in1")]
        names = ("mask_ready", "sd_ready", "rs_ready", "ln_ready", "ws_psum", "ws_ready", "parts_clean", "sel_clean", "hT_psum", "hT_ready", "proj",
                 "s1_ready", "s2_ready", "c_ready", "d_ready", "t_step", "tm_ready", "v_ready", "u_ready", "split_step",
                 "parts_ready", "rows_psum", "rows_ready", "v_copied", "vv_ready", "r_ready",
                 "z_psum", "e_ready", "pv", "y12_ready", "yy_ready", "rden_ready", "y_ready", "stat_step")
        s = {n: sem(n) for n in names}

        def each_group(eng, before, turn):
            before()
            turn(0, 0, True, 2)
            with eng.Fori(0, NG // 2 - 2) as i:
                turn(2 * i + 1, 1, False, 2)
                turn(2 * i + 2, 0, False, 2)
            turn(NG - 3, 1, False, 2)
            turn(NG - 2, 0, False, 1)
            turn(NG - 1, 1, False, 0)

        def unit_before(g, par, k, back):
            return (g, par, k - back) if k >= back else (g - 1, 1 - par, k - back + G)

        def slot(k):
            return psum[:, 2 * (k % 2):2 * (k % 2) + 2, :].rearrange("p a (h n) -> p (a h) n", h=H // 2)

        def sums(k):
            return psum[:, 4 + k % 2, :].rearrange("p (h d) -> p h d", h=H)

        def projections(b):
            at = PROJ * (b % 2)
            return psum[:, T_BANK + b // 2, at:at + PROJ]

        def score_columns(first):
            return psum[:, T_BANK:T_BANK + 2, 0:2 * PROJ].rearrange("p a (b k) -> p a b k", b=2)[:, :, :, P + first:P + first + H]

        row_parts = psum[:, ROW_BANK, 2 * PROJ:2 * PROJ + P // 2].bitcast(BF16)

        with nc.Block() as block:
            @block.sync
            def _(sp):
                def load_adj(g, par):
                    if begun(g, 2):
                        sp.wait_ge(s["mask_ready"], 2 * (g - 1))
                        settle(sp, env["passed"])
                    sp.dma_start(adjT_i[par][:, :, :], env["adjT"][:, bass.ds(g * G, G), :]).then_inc(adj_in[par], 16)

                def turn(g, par, first, left):
                    if left:
                        load_adj(g + 1, 1 - par)

                each_group(sp, lambda: load_adj(0, 0), turn)

            @block.gpsimd
            def _(pool):
                def masks(g, par):
                    if begun(g, 2):
                        pool.wait_ge(s["pv"], G * (g - 1))
                    pool.wait_ge(adj_in[par], 8 * (g - par) + 16)
                    settle(pool, env["passed"])
                    pool.tensor_scalar(maskT[par][:, :, :], adjT_i[par][:, :, :], BIG, -BIG, ALU.mult, ALU.add).then_inc(s["mask_ready"], 1)
                    pool.tensor_scalar(MT[par][:, :, :], adjT_i[par][:, :, :], 1.0, 0.0, ALU.mult, ALU.add).then_inc(s["mask_ready"], 1)

                def split(g):
                    if begun(g, 1):
                        pool.wait_ge(s["rows_psum"], g)
                    pool.wait_ge(s["s1_ready"], g + 1)
                    settle(pool, env["passed"])
                    pool.tensor_copy(parts[:, :, 0:H], s1[:, :, :]).then_inc(s["split_step"], 1)
                    pool.wait_ge(s["split_step"], 3 * g + 1)
                    pool.tensor_tensor(rem1[:, :, :], s1[:, :, :], parts[:, :, 0:H], ALU.subtract).then_inc(s["split_step"], 1)
                    pool.wait_ge(s["split_step"], 3 * g + 2)
                    settle(pool, env["passed"])
                    pool.tensor_copy(parts[:, :, H:2 * H], rem1[:, :, :]).then_inc(s["split_step"], 1)
                    pool.wait_ge(s["split_step"], 3 * g + 3)
                    pool.tensor_tensor(parts[:, :, 2 * H:3 * H], rem1[:, :, :], parts[:, :, H:2 * H], ALU.subtract).then_inc(s["parts_ready"], 1)

                def exponents(g):
                    if begun(g, 1):
                        pool.wait_ge(s["v_ready"], 2 * g)
                        pool.wait_ge(s["u_ready"], 2 * g)
                    pool.wait_ge(s["s2_ready"], 2 * g + 2)
                    settle(pool, env["passed"])
                    pool.partition_all_reduce(c[:, :, :].rearrange("p b h -> p (b h)"), s2[:, :, :].rearrange("p b h -> p (b h)"),
                                              P, RMAX).then_inc(s["c_ready"], 1)
                    pool.wait_ge(s["c_ready"], g + 1)
                    pool.tensor_tensor(d[:, :, :], s2[:, :, :], c[:, :, :], ALU.subtract).then_inc(s["d_ready"], 1)
                    pool.tensor_tensor(t[:, :, :], s1[:, :, :], c[:, :, :], ALU.add).then_inc(s["t_step"], 1)
                    pool.wait_ge(s["t_step"], 4 * g + 1)
                    settle(pool, env["passed"])
                    pool.tensor_scalar(m8[:, :, :], t[:, :, :], 0.0, 1.0 - SLOPE, ALU.max, ALU.mult).then_inc(s["t_step"], 1)
                    pool.tensor_scalar(t02[:, :, :], t[:, :, :], SLOPE, None, ALU.mult).then_inc(s["t_step"], 1)
                    pool.wait_ge(s["t_step"], 4 * g + 3)
                    pool.tensor_tensor(m02[:, :, :], m8[:, :, :], t02[:, :, :], ALU.add).then_inc(s["t_step"], 1)
                    pool.wait_ge(s["t_step"], 4 * g + 4)
                    pool.tensor_tensor(tm[:, :, :], t[:, :, :], m02[:, :, :], ALU.subtract).then_inc(s["tm_ready"], 1)
                    pool.tensor_tensor(tm2[:, :, :], t02[:, :, :], m02[:, :, :], ALU.subtract).then_inc(s["tm_ready"], 1)

                def values(g, par):
                    pool.wait_ge(s["v_copied"], 2 * g + 2)
                    pool.wait_ge(s["v_ready"], 2 * g + 2)
                    for r in (R, R2):
                        rr = r[par][:, :, :, :]
                        pool.tensor_tensor(rr[:, :, :, 0:HD], V[par][:, :, :].rearrange("p b (h d) -> p b h d", h=H),
                                           rr[:, :, :, HD:HD + 1].broadcast_to([P, G, H, HD]), ALU.mult).then_inc(s["vv_ready"], 1)

                def prepare(g, par):
                    masks(g, par)
                    split(g)
                    exponents(g)
                    values(g, par)

                def turn(g, par, first, left):
                    if left:
                        prepare(g + 1, 1 - par)

                pool.memset(parts[:, :, :], 0.0).then_inc(s["parts_clean"], 1)
                pool.wait_ge(s["parts_clean"], 1)
                each_group(pool, lambda: prepare(0, 0), turn)

            @block.tensor
            def _(pe):
                def project(g, par, item):
                    if item == 0:
                        pe.wait_ge(s["ln_ready"], g + 1)
                        if begun(g, 1):
                            pe.wait_ge(s["v_copied"], 2 * g)
                            pe.wait_ge(s["rows_ready"], g)
                        for b in range(G):
                            m = pe.transpose(psum[:, T_BANK, b * P:(b + 1) * P], hN[:, b, :], ident)
                        m.then_inc(s["hT_psum"], 1)
                    if item == 1:
                        pe.wait_ge(s["hT_ready"], g + 1)
                        for b in range(G):
                            m = pe.matmul(projections(b), hT[:, b * P:(b + 1) * P], wproj[:, :], start=True, stop=True)
                        m.then_inc(s["proj"], 1)
                    if item == 2:
                        pe.wait_ge(s["v_copied"], 2 * g + 2)
                        pe.wait_ge(s["parts_ready"], g + 1)
                        pe.transpose(row_parts, parts[:, :, :].rearrange("p b r -> p (b r)"), identb[:, :]).then_inc(s["rows_psum"], 1)

                def scores(g, par, k):
                    n = G * g + k
                    if k == 0:
                        pe.wait_ge(s["rows_ready"], g + 1)
                        pe.wait_ge(s["mask_ready"], 2 * g + 2)
                    if not (isinstance(g, int) and g == 0 and k < 2):
                        pe.wait_ge(s["e_ready"], n - 1)
                    for a in range(2):
                        for h in range(H // 2):
                            hh = a * (H // 2) + h
                            pe.matmul(slot(k)[:, hh, :], selb[:, k, hh, :], rows[par][:, :], start=(h == 0), stop=False, skip_group_check=True)
                        m = pe.matmul(psum[:, 2 * (k % 2) + a, :], identb[:, :], bcast(maskT[par][:, k, :], 1, H // 2),
                                      start=False, stop=True, skip_group_check=True)
                    m.then_inc(s["z_psum"], 1)

                def products(g, par, k):
                    n = G * g + k
                    if k == 0:
                        pe.wait_ge(s["r_ready"], g + 1)
                    if not (isinstance(g, int) and g == 0 and k < 2):
                        pe.wait_ge(s["y12_ready"], n - 1)
                    pe.matmul(sums(k)[:, :, HV:2 * HV], MT[par][:, k, :], R2[par][:, k, :, :], start=True, stop=False, skip_group_check=True)
                    pe.wait_ge(s["e_ready"], n + 1)
                    for h in range(H):
                        m = pe.matmul(sums(k)[:, h, :], E[k % 2][:, h, :], Rpad[par][:, k, 2 * HV * h:2 * HV * h + RS], start=False, stop=(h == H - 1), skip_group_check=True)
                    m.then_inc(s["pv"], 1)

                def before():
                    pe.matmul(psum[:, 0, 0:2 * H], w("w2T"), w("adiag"), start=True, stop=True).then_inc(s["ws_psum"], 1)
                    project(0, 0, 0)
                    pe.wait_ge(s["ws_ready"], 2)
                    project(0, 0, 1)
                    project(0, 0, 2)
                    pe.wait_ge(s["ws_ready"], 3)

                def turn(g, par, first, left):
                    for k in range(G):
                        scores(g, par, k)
                        if left and k in (1, 2):
                            project(g + 1, 1 - par, k)
                        if not first or k >= 1:
                            products(*unit_before(g, par, k, 1))
                        if left and k == 0:
                            project(g + 1, 1 - par, k)
                    if not left:
                        products(g, par, G - 1)

                each_group(pe, before, turn)

            @block.scalar
            def _(act):
                def normalise(g):
                    if begun(g, 1):
                        act.wait_ge(s["hT_psum"], g)
                    for b in range(G):
                        gb = g * G + b
                        m = act.activation(hN[:, b:b + 1, :], X[:, bass.ds(gb, 1), :], ACT.Relu,
                                           bias=shift[:, bass.ds(gb, 1)], scale=rstd[:, bass.ds(gb, 1)])
                    m.then_inc(s["ln_ready"], 1)

                def transposed(g):
                    if begun(g, 1):
                        act.wait_ge(s["proj"], g)
                    act.wait_ge(s["hT_psum"], g + 1)
                    act.activation(hT[:, :], psum[:, T_BANK, :], ACT.Copy).then_inc(s["hT_ready"], 1)

                def s2_copies(g, par):
                    if begun(g, 1):
                        act.wait_ge(s["d_ready"], g)
                    if begun(g, 2):
                        act.wait_ge(s["e_ready"], G * (g - 1))
                    act.wait_ge(s["proj"], g + 1)
                    act.wait_ge(s["s1_ready"], g + 1)
                    for into, scale in ((s2, 1.0), (ns2[par], -1.0)):
                        act.activation(into[:, :, :].rearrange("p (a b) h -> p a b h", a=2), score_columns(H), ACT.Copy, scale=scale).then_inc(s["s2_ready"], 1)

                def values_copy(g, par):
                    if begun(g, 2):
                        act.wait_ge(s["vv_ready"], 2 * (g - 1))
                    for a in range(2):
                        act.activation(V[par][:, 2 * a:2 * a + 2, :], psum[:, T_BANK + a, 0:2 * PROJ].rearrange("p (b k) -> p b k", b=2)[:, :, 0:P],
                                       ACT.Copy).then_inc(s["v_copied"], 1)

                def row_copy(g, par):
                    if begun(g, 2):
                        act.wait_ge(s["z_psum"], G * (g - 1))
                    act.wait_ge(s["rows_psum"], g + 1)
                    act.activation(rows[par][:, :], row_parts, ACT.Copy).then_inc(s["rows_ready"], 1)

                def factors(g, par):
                    if begun(g, 2):
                        act.wait_ge(s["y12_ready"], G * (g - 1))
                    act.wait_ge(s["d_ready"], g + 1)
                    act.activation(R[par][:, :, :, HD], d[:, :, :], ACT.Exp).then_inc(s["v_ready"], 1)
                    act.activation(R2[par][:, :, :, HD], d[:, :, :], ACT.Exp, scale=SLOPE).then_inc(s["v_ready"], 1)
                    act.wait_ge(s["tm_ready"], 2 * g + 2)
                    act.activation(U[par][:, :, :, 0], tm[:, :, :], ACT.Exp).then_inc(s["u_ready"], 1)
                    act.activation(U[par][:, :, :, 1], tm2[:, :, :], ACT.Exp).then_inc(s["u_ready"], 1)

                def negate(g, par):
                    act.wait_ge(s["vv_ready"], 2 * g + 2)
                    act.activation(R[par][:, :, :, HV:2 * HV], R2[par][:, :, :, :], ACT.Copy, scale=-1.0).then_inc(s["r_ready"], 1)

                def prepare(g, par):
                    transposed(g)
                    s2_copies(g, par)
                    values_copy(g, par)
                    row_copy(g, par)
                    factors(g, par)

                def before():
                    act.wait_ge(s["rs_ready"], 2)
                    normalise(0)
                    prepare(0, 0)
                    normalise(1)
                    negate(0, 0)

                def turn(g, par, first, left):
                    if left:
                        prepare(g + 1, 1 - par)
                        if left == 2:
                            normalise(g + 2)
                        negate(g + 1, 1 - par)

                deviations(act, env, s["sd_ready"])
                each_group(act, before, turn)
                sqrt_table(act, env)

            @block.vector
            def _(dve):
                def s1_sum(g):
                    if begun(g, 1):
                        dve.wait_ge(s["parts_ready"], g)
                        dve.wait_ge(s["t_step"], 4 * g)
                    dve.wait_ge(s["proj"], g + 1)
                    dve.tensor_tensor(s1[:, :, :].rearrange("p (a b) h -> p a b h", a=2), score_columns(0),
                                      bcast(bcast(w("emb"), 1, 2), 1, 2), ALU.add).then_inc(s["s1_ready"], 1)

                def edges(g, par, k):
                    n = G * g + k
                    dve.wait_ge(s["z_psum"], n + 1)
                    dve.wait_ge(s["s2_ready"], 2 * g + 2)
                    if not (isinstance(g, int) and g == 0 and k < 2):
                        dve.wait_ge(s["pv"], n - 1)
                    dve.tensor_tensor(E[k % 2][:, :, :], slot(k), bcast(ns2[par][:, k, :], 2, P), ALU.is_gt).then_inc(s["e_ready"], 1)

                def weighted(g, par, k):
                    n = G * g + k
                    dve.wait_ge(s["pv"], n + 1)
                    dve.wait_ge(s["u_ready"], 2 * g + 2)
                    dve.tensor_tensor(y12[k % 2][:, :, :, :], sums(k)[:, :, 0:2 * HV].rearrange("p h (c d) -> p h c d", c=2),
                                      bcast(U[par][:, k, :, :], 3, HV), ALU.mult).then_inc(s["y12_ready"], 1)

                def summed(g, par, k):
                    dve.wait_ge(s["y12_ready"], G * g + k + 1)
                    dve.tensor_tensor(yy[k % 2][:, :, :], y12[k % 2][:, :, 0, :], y12[k % 2][:, :, 1, :], ALU.add).then_inc(s["yy_ready"], 1)

                def inverted(g, par, k):
                    dve.wait_ge(s["yy_ready"], G * g + k + 1)
                    dve.reciprocal(rden[k % 2][:, :], yy[k % 2][:, :, HD]).then_inc(s["rden_ready"], 1)

                def divided(g, par, k):
                    n = G * g + k
                    dve.wait_ge(s["rden_ready"], n + 1)
                    yg = Y[:, bass.ds(n, 1), :].rearrange("p b (h d) -> p (b h) d", h=H)
                    dve.tensor_tensor(yg, yy[k % 2][:, :, 0:HD], bcast(rden[k % 2][:, :], 2, HD), ALU.mult).then_inc(s["y_ready"], 1)

                def before():
                    prime(dve, s["stat_step"])
                    normalisers(dve, env, s["sd_ready"], s["rs_ready"])
                    dve.tensor_copy(wproj[:, 0:P], w("w2")).then_inc(s["ws_ready"], 1)
                    dve.wait_ge(s["ws_psum"], 1)
                    dve.tensor_copy(wproj[:, P:PROJ], psum[:, 0, 0:2 * H]).then_inc(s["ws_ready"], 1)
                    dve.memset(selb[:, :, :, :], 0.0).then_inc(s["sel_clean"], 1)
                    for r in Rpad:
                        dve.memset(r[:, :, H * 2 * HV:], 0.0).then_inc(s["sel_clean"], 1)
                    dve.wait_ge(s["sel_clean"], 3)
                    for b in range(G):
                        at = b * ROWS
                        m = dve.tensor_copy(selb[at:at + PARTS * H, b, :, :], w("sel")[at:at + PARTS * H, :].rearrange("p (h n) -> p h n", h=H))
                    m.then_inc(s["ws_ready"], 1)
                    s1_sum(0)

                def turn(g, par, first, left):
                    for k in range(G):
                        edges(g, par, k)
                        if left and k == 1:
                            s1_sum(g + 1)
                        if not first or k >= 2:
                            inverted(*unit_before(g, par, k, 2))
                        if not first and k == 2:
                            output_statistics(g - 1)
                        if not first or k >= 1:
                            weighted(*unit_before(g, par, k, 1))
                        if not first or k >= 2:
                            divided(*unit_before(g, par, k, 2))
                        if not first or k >= 1:
                            summed(*unit_before(g, par, k, 1))
                    if not left:
                        inverted(g, par, G - 2)
                        weighted(g, par, G - 1)
                        divided(g, par, G - 2)
                        summed(g, par, G - 1)
                        inverted(g, par, G - 1)
                        divided(g, par, G - 1)
                        output_statistics(g)
                        dve.wait_ge(s["stat_step"], primed(3 * NG))

                def output_statistics(g):
                    dve.wait_ge(s["y_ready"], G * (g + 1))
                    row_statistics(env, dve, Y, g, ymeanvar, s["stat_step"])

                each_group(dve, before, turn)

        yn, pos, exp = sb("yn", [P, G, P]), sb("pos", [P, G, P]), sb("exp", [P, G, P])
        elu = one("elu", [P, G, P])
        names2 = ("sd_ready", "rs_ready", "yn_ready", "gamma_done", "beta_done", "exp_ready",
                  "elu_ready", "x_ready", "stat_step")
        s2_ = {n: sem("second_" + n) for n in names2}
        env["ymeanvar"] = ymeanvar
        with nc.Block() as block:
            @block.tensor
            def _(pe):
                gate_products(pe, env)

            @block.scalar
            def _(act):
                def normalise(g, par):
                    if begun(g, 2):
                        act.wait_ge(s2_["exp_ready"], g - 1)
                    for b in range(G):
                        gb = g * G + b
                        m = act.activation(yn[par][:, b:b + 1, :], Y[:, bass.ds(gb, 1), :], ACT.Identity,
                                           bias=shift[:, bass.ds(gb, 1)], scale=rstd[:, bass.ds(gb, 1)])
                    m.then_inc(s2_["yn_ready"], 1)

                def turn(g, par, left):
                    if left:
                        normalise(g + 1, 1 - par)
                    if begun(g, 2):
                        act.wait_ge(s2_["elu_ready"], g - 1)
                    act.wait_ge(s2_["beta_done"], g + 1)
                    act.activation(pos[par][:, :, :], yn[par][:, :, :], ACT.Relu)
                    act.activation(exp[par][:, :, :], yn[par][:, :, :], ACT.Exp).then_inc(s2_["exp_ready"], 1)

                def before():
                    act.wait_ge(s2_["rs_ready"], 2)
                    normalise(0, 0)

                deviations(act, env, s2_["sd_ready"], "ymeanvar")
                in_pairs(act, before, turn)
                sqrt_table(act, env)

            @block.gpsimd
            def _(pool):
                def turn(g, par, left):
                    pool.wait_ge(s2_["yn_ready"], g + 1)
                    pool.tensor_tensor(yn[par][:, :, :], yn[par][:, :, :], bcast(w("gamma"), 1, G), ALU.mult).then_inc(s2_["gamma_done"], 1)
                    pool.wait_ge(s2_["gamma_done"], g + 1)
                    pool.tensor_tensor(yn[par][:, :, :], yn[par][:, :, :], bcast(w("beta"), 1, G), ALU.add).then_inc(s2_["beta_done"], 1)

                in_pairs(pool, lambda: None, turn)

            @block.vector
            def _(dve):
                def elu_plus_one(g, par):
                    dve.wait_ge(s2_["exp_ready"], g + 1)
                    if begun(g, 1):
                        dve.wait_ge(s2_["x_ready"], g)
                    dve.scalar_tensor_tensor(out=elu[:, :, :], in0=exp[par][:, :, :], scalar=1.0, in1=pos[par][:, :, :],
                                             op0=ALU.min, op1=ALU.add).then_inc(s2_["elu_ready"], 1)

                def add_to_x(g):
                    dve.wait_ge(s2_["elu_ready"], g + 1)
                    xg = X[:, bass.ds(g * G, G), :]
                    dve.scalar_tensor_tensor(out=xg, in0=elu[:, :, :], scalar=-1.0, in1=xg, op0=ALU.add, op1=ALU.add).then_inc(s2_["x_ready"], 1)

                def turn(g, par, left):
                    if begun(g, 2):
                        row_saved(env, dve, g - 2, meanvar, s2_["stat_step"])
                    elu_plus_one(g, par)
                    if begun(g, 1):
                        dve.wait_ge(s2_["x_ready"], g)
                        row_moments(env, dve, X, g - 1, s2_["stat_step"])
                    add_to_x(g)
                    if begun(g, 1):
                        row_aggregates(env, dve, g - 1, s2_["stat_step"])
                    if not left:
                        row_saved(env, dve, g - 1, meanvar, s2_["stat_step"])
                        dve.wait_ge(s2_["x_ready"], g + 1)
                        row_statistics(env, dve, X, g, meanvar, s2_["stat_step"])
                        dve.wait_ge(s2_["stat_step"], primed(3 * (g + 1)))

                def before():
                    prime(dve, s2_["stat_step"])
                    normalisers(dve, env, s2_["sd_ready"], s2_["rs_ready"], "ymeanvar")
                    gate_parts(dve, env)

                in_pairs(dve, before, turn)


def gate_products(pe, env):
    for k in range(STEPS):
        pe.matmul(env["psum"][:, k, 0:3 * P], env["w"]("gwT")[:, k * P:(k + 1) * P], env["w"]("wih"),
                  start=True, stop=True).then_inc(env["wg_psum"], 1)


def gate_parts(dve, env):
    wg, whh = env["wg"], env["w"]("whh")
    for k in range(STEPS):
        dve.wait_ge(env["wg_psum"], k + 1)
        dve.tensor_copy(wg[:, k, :], env["psum"][:, k, 0:3 * P]).then_inc(env["wg_step"], 1)
    dve.wait_ge(env["wg_step"], STEPS)
    dve.tensor_copy(env["wg_hi"][:, :, :], wg[:, :, :])
    dve.tensor_copy(env["whh_hi"][:, :], whh).then_inc(env["wg_step"], 1)
    dve.wait_ge(env["wg_step"], STEPS + 1)
    dve.tensor_tensor(env["wg_lo"][:, :, :], wg[:, :, :], env["wg_hi"][:, :, :], ALU.subtract)
    dve.tensor_tensor(env["whh_lo"][:, :], whh, env["whh_hi"][:, :], ALU.subtract).then_inc(env["wg_step"], 1)


def gated_layer(env):
    nc, X, w, ident, psum = (env[k] for k in ("nc", "X", "w", "ident", "psum"))
    meanvar, rstd = env["meanvar"], env["rstd"]
    NI = GRAPHS // (2 * G)
    HALVES = 2 * STEPS
    R_BANK, Z_BANK, HN_BANK, IN_BANK = range(4)
    with ExitStack() as ctx:
        def one(name, shape, dt=F32):
            return ctx.enter_context(nc.sbuf_tensor("g_" + name, shape, dt))

        def sb(name, shape, dt=F32):
            return [one(f"{name}{u}", shape, dt) for u in range(2)]

        wg_hi, wg_lo, whh_hi, whh_lo = (env[k] for k in ("wg_hi", "wg_lo", "whh_hi", "whh_lo"))
        brz, nbz = one("brz", [P, 2]), one("nbz", [P, 1])
        adj_i, A = sb("adj_i", [P, G, P], I32), sb("A", [P, G, P])
        h0, h0T = sb("h0", [P, G, P]), sb("h0T", [P, G * P])
        hN, hT = sb("hN", [P, G, P]), sb("hT", [P, G * P])
        h_hi, h_lo = sb("h_hi", [P, G * P], F32R), sb("h_lo", [P, G * P], F32R)
        a_hi, a_lo = sb("a_hi", [P, G * P], F32R), sb("a_lo", [P, G * P], F32R)
        r, z, omz, zh, nn, tt = (sb(n, [P, G * P]) for n in ("r", "z", "omz", "zh", "n", "t"))
        o = sb("o", [P, G, P])

        def sem(name):
            return ctx.enter_context(nc.semaphore("g_" + name))

        adj_in = [sem("adj_in0"), sem("adj_in1")]
        stored = [sem("stored0"), sem("stored1")]
        names = ("sd", "a_ready", "rs", "ln_ready", "h0_ready",
                 "h0T_psum", "h0T_ready", "hi_ready", "lo_ready", "agg", "ahi_ready", "alo_ready", "r_psum", "z_psum", "n_psum",
                 "r_ready", "z_ready", "omz_ready", "rh_ready", "t_ready", "zh_ready", "n_ready", "nz_ready", "new_ready",
                 "hN_psum", "hN_ready", "out_ready")
        s = {n: sem(n) for n in names}

        def bank(u, k):
            return psum[:, 4 * u + k, :]

        def graphs(u, k):
            return psum[:, 4 * u + k, :].rearrange("p (b n) -> p b n", b=G)

        def each_half(eng, half):
            def turn(i, last):
                order = [(i, k, u, HALVES * i + 2 * k + u) for k in range(STEPS) for u in range(2)]
                order.append(None if last else (i + 1, 0, 0, HALVES * (i + 1)))
                for at, nxt in zip(order, order[1:]):
                    half(*at, nxt)
            turn(0, False)
            with eng.Fori(1, NI - 1) as i:
                turn(i, False)
            turn(NI - 1, True)

        def begun(i):
            return not (isinstance(i, int) and i == 0)

        def follows(i):
            return not (isinstance(i, int) and i == NI - 1)

        with nc.Block() as block:
            @block.sync
            def _(sp):
                prime(sp, *stored)

                def load_adj(i, u):
                    sp.dma_start(adj_i[u][:, :, :], env["adj"][:, bass.ds((2 * i + u) * G, G), :]).then_inc(adj_in[u], 16)

                def turn(i, last):
                    if not last:
                        for u in range(2):
                            sp.wait_ge(s["a_ready"], primed(2 * i + u + 1))
                            load_adj(i + 1, u)
                    for u in range(2):
                        n = 2 * i + u
                        sp.wait_ge(s["out_ready"], n + 1)
                        sp.dma_start(env["out"][:, bass.ds(n * G, G), :], o[u][:, :, :]).then_inc(stored[u], 16)

                for u in range(2):
                    load_adj(0, u)
                with sp.Fori(0, NI - 1) as i:
                    turn(i, False)
                turn(NI - 1, True)
                for u in range(2):
                    sp.wait_ge(stored[u], primed(16 * NI))

            @block.gpsimd
            def _(pool):
                prime(pool, s["a_ready"])

                def adjacency(n, u, i):
                    if begun(i):
                        pool.wait_ge(s["agg"], HALVES * i - 2 + u + 1)
                    pool.wait_ge(adj_in[u], 16 * i + 16)
                    settle(pool, env["passed"])
                    pool.tensor_scalar(A[u][:, :, :], adj_i[u][:, :, :], 1.0, 0.0, ALU.mult, ALU.add).then_inc(s["a_ready"], 1)

                def relu(n, u):
                    pool.wait_ge(s["ln_ready"], n + 1)
                    settle(pool, env["passed"])
                    pool.tensor_scalar(h0[u][:, :, :], h0[u][:, :, :], 0.0, None, ALU.max).then_inc(s["h0_ready"], 1)

                def low_part(q, u, state):
                    pool.wait_ge(s["hi_ready"], q + 1)
                    pool.tensor_tensor(h_lo[u][:, :], state[u][:, :], h_hi[u][:, :], ALU.subtract).then_inc(s["lo_ready"], 1)

                def half(i, k, u, q, nxt):
                    if nxt and nxt[1] == 0:
                        low_part(nxt[3], nxt[2], h0T)
                    pool.wait_ge(s["z_ready"], q + 1)
                    pool.tensor_tensor(zh[u][:, :], z[u][:, :], (hT if k else h0T)[u][:, :], ALU.mult).then_inc(s["zh_ready"], 1)
                    if k < STEPS - 1:
                        low_part(q + 2, u, hT)
                    if k == 1 and follows(i):
                        relu(2 * (i + 1) + u, u)
                    if k == STEPS - 1 and follows(i):
                        adjacency(2 * (i + 1) + u, u, i + 1)

                adjacency(0, 0, 0)
                for u in range(2):
                    relu(u, u)
                low_part(0, 0, h0T)
                adjacency(1, 1, 0)
                each_half(pool, half)

            @block.tensor
            def _(pe):
                prime(pe, s["hN_psum"])

                def gate(u, bank_, hi, lo, x_hi, x_lo, start, stop, passes=(0, 1, 2)):
                    pairs = ((hi, x_hi), (hi, x_lo), (lo, x_hi))
                    for p in passes:
                        m = pe.matmul(bank(u, bank_), pairs[p][0], pairs[p][1][u][:, :], start=start and p == 0, stop=stop and p == 2)
                    return m

                def state_gates(u, q):
                    pe.wait_ge(s["hi_ready"], q + 1)
                    pe.wait_ge(s["lo_ready"], q + 1)
                    for b, stop in ((R_BANK, False), (Z_BANK, False), (HN_BANK, True)):
                        gate(u, b, whh_hi[:, b * P:(b + 1) * P], whh_lo[:, b * P:(b + 1) * P], h_hi, h_lo, True, stop)

                def input_gate(k, u, which, start, passes=(0, 1, 2)):
                    cols = slice(which * P, (which + 1) * P)
                    return gate(u, (R_BANK, Z_BANK, IN_BANK)[which], wg_hi[:, k, cols], wg_lo[:, k, cols], a_hi, a_lo, start, True, passes)

                def transpose_first(n, u, q, i):
                    pe.wait_ge(s["h0_ready"], n + 1)
                    if begun(i):
                        pe.wait_ge(s["t_ready"], q - 2 + 1)
                    for b in range(G):
                        m = pe.transpose(graphs(u, IN_BANK)[:, b, :], h0[u][:, b, :], ident)
                    m.then_inc(s["h0T_psum"], 1)

                def transpose_state(u, q):
                    pe.wait_ge(s["new_ready"], q + 1)
                    for b in range(G):
                        m = pe.transpose(graphs(u, IN_BANK)[:, b, :], hT[u][:, b * P:(b + 1) * P], ident)
                    m.then_inc(s["hN_psum"], 1)

                def aggregate(i, k, u, q):
                    n = 2 * i + u
                    if k == 0:
                        pe.wait_ge(s["a_ready"], primed(n + 1))
                        pe.wait_ge(s["h0T_ready"], n + 1)
                        if begun(i):
                            pe.wait_ge(s["out_ready"], n - 1)
                    else:
                        pe.wait_ge(s["hN_ready"], 2 * (STEPS - 1) * i + 2 * (k - 1) + u + 1)
                    src = hN if k else h0
                    for b in range(G):
                        m = pe.matmul(graphs(u, IN_BANK)[:, b, :], src[u][:, b, :], A[u][:, b, :], start=True, stop=True)
                    m.then_inc(s["agg"], 1)

                def half(i, k, u, q, nxt):
                    state_gates(u, q)
                    if nxt and nxt[1] == 0:
                        transpose_first(2 * nxt[0] + nxt[2], nxt[2], nxt[3], nxt[0])
                    pe.wait_ge(s["ahi_ready"], q + 1)
                    pe.wait_ge(s["alo_ready"], q + 1)
                    input_gate(k, u, 0, False).then_inc(s["r_psum"], 1)
                    input_gate(k, u, 1, False, (0, 1))
                    if nxt is None:
                        transpose_state(1 - u, q - 1)
                    elif nxt[1] > 0 or begun(nxt[0]):
                        if nxt[1] == 0:
                            pe.wait_ge(s["h0T_ready"], 2 * nxt[0] + nxt[2] + 1)
                        transpose_state(nxt[2], nxt[3] - 2)
                    input_gate(k, u, 1, False, (2,)).then_inc(s["z_psum"], 1)
                    input_gate(k, u, 2, True).then_inc(s["n_psum"], 1)
                    if nxt:
                        aggregate(*nxt)
                    else:
                        transpose_state(u, q)

                transpose_first(0, 0, 0, 0)
                aggregate(0, 0, 0, 0)
                each_half(pe, half)

            @block.scalar
            def _(act):
                deviations(act, env, s["sd"], table=ACT.Sigmoid)

                def first_state(n, u):
                    act.wait_ge(s["h0T_psum"], n + 1)
                    act.activation(h0T[u][:, :], bank(u, IN_BANK), ACT.Copy).then_inc(s["h0T_ready"], 1)

                def aggregate_high(u, q):
                    act.wait_ge(s["agg"], q + 1)
                    act.activation(a_hi[u][:, :], bank(u, IN_BANK), ACT.Copy).then_inc(s["ahi_ready"], 1)

                def half(i, k, u, q, nxt):
                    if nxt and nxt[1] == 0:
                        first_state(2 * nxt[0] + nxt[2], nxt[2])
                    act.wait_ge(s["r_psum"], q + 1)
                    act.activation(r[u][:, :], bank(u, R_BANK), ACT.Sigmoid, bias=brz[:, 0:1]).then_inc(s["r_ready"], 1)
                    if nxt and nxt[1] > 0:
                        act.wait_ge(s["hN_psum"], primed(nxt[3] - 2 + 1))
                        act.activation(hN[nxt[2]][:, :, :], graphs(nxt[2], IN_BANK), ACT.Copy).then_inc(s["hN_ready"], 1)
                    act.wait_ge(s["z_psum"], q + 1)
                    act.activation(z[u][:, :], bank(u, Z_BANK), ACT.Sigmoid, bias=brz[:, 1:2]).then_inc(s["z_ready"], 1)
                    act.activation(omz[u][:, :], bank(u, Z_BANK), ACT.Sigmoid, bias=nbz[:, :], scale=-1.0).then_inc(s["omz_ready"], 1)
                    if nxt:
                        aggregate_high(nxt[2], nxt[3])
                    act.wait_ge(s["t_ready"], q + 1)
                    act.activation(nn[u][:, :], tt[u][:, :], ACT.Tanh, bias=w("bih")[:, 2:3]).then_inc(s["n_ready"], 1)

                first_state(0, 0)
                aggregate_high(0, 0)
                act.wait_ge(s["rs"], 4)
                each_half(act, half)

            @block.vector
            def _(dve):
                normalisers(dve, env, s["sd"], s["rs"])
                dve.tensor_tensor(brz[:, :], w("bih")[:, 0:2], w("bhh")[:, 0:2], ALU.add).then_inc(s["rs"], 1)
                dve.wait_ge(s["rs"], 3)
                dve.tensor_scalar(nbz[:, :], brz[:, 1:2], -1.0, None, ALU.mult).then_inc(s["rs"], 1)

                def normalise(n, u):
                    for b in range(G):
                        g = n * G + b
                        m = dve.tensor_scalar(h0[u][:, b, :], X[:, bass.ds(g, 1), :], meanvar[:, bass.ds(g, 1), 0], rstd[:, bass.ds(g, 1)],
                                              ALU.subtract, ALU.mult)
                    m.then_inc(s["ln_ready"], 1)

                def aggregate_low(u, q):
                    dve.wait_ge(s["ahi_ready"], q + 1)
                    dve.tensor_tensor(a_lo[u][:, :], bank(u, IN_BANK), a_hi[u][:, :], ALU.subtract).then_inc(s["alo_ready"], 1)

                def result(n, u, i, src):
                    dve.wait_ge(s["hN_psum"], primed(src + 1))
                    dve.wait_ge(stored[u], primed(16 * i))
                    dve.tensor_tensor(o[u][:, :, :], graphs(u, IN_BANK), X[:, bass.ds(n * G, G), :], ALU.add).then_inc(s["out_ready"], 1)

                def half(i, k, u, q, nxt):
                    if nxt and nxt[1] == 0:
                        dve.wait_ge(s["h0T_ready"], 2 * nxt[0] + nxt[2] + 1)
                        dve.tensor_copy(h_hi[nxt[2]][:, :], h0T[nxt[2]][:, :]).then_inc(s["hi_ready"], 1)
                    dve.wait_ge(s["r_ready"], q + 1)
                    dve.scalar_tensor_tensor(out=tt[u][:, :], in0=bank(u, HN_BANK), scalar=w("bhh")[:, 2:3], in1=r[u][:, :],
                                             op0=ALU.add, op1=ALU.mult).then_inc(s["rh_ready"], 1)
                    if nxt is None:
                        result(2 * i + 1 - u, 1 - u, i, q - 1)
                    elif nxt[1] == 0 and begun(nxt[0]):
                        result(2 * (nxt[0] - 1) + nxt[2], nxt[2], nxt[0] - 1, nxt[3] - 2)
                    dve.wait_ge(s["n_psum"], q + 1)
                    dve.wait_ge(s["rh_ready"], q + 1)
                    dve.tensor_tensor(tt[u][:, :], tt[u][:, :], bank(u, IN_BANK), ALU.add).then_inc(s["t_ready"], 1)
                    if nxt:
                        aggregate_low(nxt[2], nxt[3])
                    dve.wait_ge(s["n_ready"], q + 1)
                    dve.wait_ge(s["omz_ready"], q + 1)
                    dve.tensor_tensor(nn[u][:, :], nn[u][:, :], omz[u][:, :], ALU.mult).then_inc(s["nz_ready"], 1)
                    dve.wait_ge(s["nz_ready"], q + 1)
                    dve.wait_ge(s["zh_ready"], q + 1)
                    dve.tensor_tensor(hT[u][:, :], nn[u][:, :], zh[u][:, :], ALU.add).then_inc(s["new_ready"], 1)
                    if k < STEPS - 1:
                        dve.wait_ge(s["new_ready"], q + 1)
                        dve.tensor_copy(h_hi[u][:, :], hT[u][:, :]).then_inc(s["hi_ready"], 1)
                    if k == 1 and follows(i):
                        normalise(2 * (i + 1) + u, u)
                    if nxt is None:
                        result(2 * i + u, u, i, q)

                for u in range(2):
                    normalise(u, u)
                dve.wait_ge(s["h0T_ready"], 1)
                dve.tensor_copy(h_hi[0][:, :], h0T[0][:, :]).then_inc(s["hi_ready"], 1)
                aggregate_low(0, 0)
                each_half(dve, half)


def _pack(a):
    import numpy as np
    f = np.float32

    def by_feature(m):
        return m.reshape((H, HD) + m.shape[1:]).swapaxes(0, 1).reshape(m.shape)

    def rows(v):
        return np.broadcast_to(v, (P, v.shape[-1]))

    a1, a2 = a["L1_gnn_a"][:P], a["L1_gnn_a"][P:]
    adiag = np.zeros((P, 2 * H), f)
    sel = np.zeros((P, H, P), f)
    for h in range(H):
        adiag[h * HD:(h + 1) * HD, h] = a["L2_gnn_a1"]
        adiag[h * HD:(h + 1) * HD, H + h] = a["L2_gnn_a2"]
        sel[h::H, h, :] = 1.0
    parts = {
        "wq": by_feature(a["L0_gnn_Wq"]).T, "wk": by_feature(a["L0_gnn_Wk"]).T,
        "wv": a["L0_gnn_Wv"].T, "wo": a["L0_gnn_Wo"].T,
        "w1": a["L1_gnn_W"], "a1rep": np.broadcast_to(a1, (P, P)), "a2rep": np.broadcast_to(a2, (P, P)), "han": a["L1_gnn_han_w"],
        "w2": a["L2_gnn_W"], "w2T": a["L2_gnn_W"].T, "adiag": adiag, "emb": rows(a["L2_gnn_edge_emb"][1]),
        "gwT": a["L3_gnn_weight"].transpose(2, 0, 1).reshape(P, STEPS * P),
        "wih": a["L3_gnn_w_ih"].T, "whh": a["L3_gnn_w_hh"].T,
        "bq": by_feature(a["L0_gnn_bq"])[:, None], "bk": by_feature(a["L0_gnn_bk"])[:, None],
        "bih": a["L3_gnn_b_ih"].reshape(3, P).T, "bhh": a["L3_gnn_b_hh"].reshape(3, P).T,
        "bv": rows(a["L0_gnn_bv"]), "bo": rows(a["L0_gnn_bo"]), "hanb": rows(a["L1_gnn_han_b"]),
        "gamma": rows(a["L2_gnn_ln_gamma"]), "beta": rows(a["L2_gnn_ln_beta"]),
        "ident": np.eye(P, dtype=f), "sel": sel.reshape(P, H * P),
    }
    return np.ascontiguousarray(np.concatenate([parts[n] for n, _ in WEIGHTS], axis=1))


def _arrays(inputs):
    import numpy as np
    a = {k: np.asarray(v) for k, v in inputs.items()}
    return {
        "x": np.ascontiguousarray(a["x"].transpose(1, 0, 2)),
        "adj": np.ascontiguousarray(a["adj"].transpose(1, 0, 2)),
        "adjT": np.ascontiguousarray(a["adj"].transpose(2, 0, 1)),
        "wpack": _pack(a),
    }


def kernel(**inputs):
    import concourse.bacc as bacc
    import numpy as np
    from concourse.bass_utils import run_bass_kernel_spmd

    nc = bacc.Bacc("TRN2", target_bir_lowering=False, num_devices=1)
    arrays = _arrays(inputs)
    args = [nc.dram_tensor(n, v.shape, mybir.dt.from_np(v.dtype), kind="ExternalInput").ap() for n, v in arrays.items()]
    out = nc.dram_tensor("out", (P, GRAPHS, P), F32, kind="ExternalOutput").ap()
    graph_layers(nc, *args, out)
    got = run_bass_kernel_spmd(nc, [arrays], core_ids=[0]).results[0]["out"]
    return np.ascontiguousarray(np.asarray(got).transpose(1, 0, 2))
```
